# Optimizing a Trainium2 kernel written in Bass

```python
import numpy as np
import jax
import jax.numpy as jnp

def _softmax(x, axis=-1):
    return jax.nn.softmax(x, axis=axis)

def _gelu(x):
    return jax.nn.gelu(x, approximate=True)

def _silu(x):
    return jax.nn.silu(x)

def _sigmoid(x):
    return jax.nn.sigmoid(x)

def _layernorm(x, axis=-1, eps=1e-05):
    m = jnp.mean(x, axis=axis, keepdims=True)
    v = jnp.var(x, axis=axis, keepdims=True)
    return (x - m) / jnp.sqrt(v + eps)

def _scatter_add(tgt, idx, src, axis=0):
    return tgt.at[idx].add(src)

def _segment_sum(src, seg, n):
    return jax.ops.segment_sum(src, seg, n)
kernel_name = 'mk_gps_d2_gnn_r16_f355c3'

def setup_inputs(seed: int=0):
    np.random.seed(seed)
    _w = jnp.asarray

    def _rec_inputs():
        import jax
        import jax.numpy as jnp
        _gk = jax.random.key(seed)
        x = -0.0001126 + 1 * jax.random.normal(jax.random.fold_in(_gk, 1), (625, 768), jnp.float32)
        src = jax.random.randint(jax.random.fold_in(_gk, 2), (10000,), 0, 625, jnp.int32)
        dst = jnp.minimum((625 * jax.random.uniform(jax.random.fold_in(_gk, 3), (10000,)) ** 2.0).astype(jnp.int32), 9999)
        _o = jnp.argsort(dst, stable=True)
        src = src[_o]
        dst = dst[_o]
        edge_type_3 = jax.random.randint(jax.random.fold_in(_gk, 12), (10000,), 0, 3, jnp.int32)
        node_type_3 = jax.random.randint(jax.random.fold_in(_gk, 13), (625,), 0, 3, jnp.int32)
        return (x, src, dst, edge_type_3, node_type_3)
    x, src, dst, edge_type_3, node_type_3 = _rec_inputs()

    def _L0_gnn_setup():
        import jax, jax.numpy as jnp
        import numpy as np
        NUM_NODES = 625
        NUM_EDGES = 10000
        IN_CH = 768
        TYPE_DIM = 128
        HID = 768
        OUT = 768
        NUM_REL = 3
        NUM_NODE_TYPE = 3

        def _glorot(key, shape):
            fan_in, fan_out = (shape[-2], shape[-1])
            lim = (6.0 / (fan_in + fan_out)) ** 0.5
            return jax.random.uniform(key, shape, jnp.float32, -lim, lim)

        def rgcn_conv(h, src, dst, edge_type, w_rel, w_root, bias):
            num_nodes = h.shape[0]
            xw = jnp.einsum('nd,rde->rne', h, w_rel)
            msg = xw[edge_type, src]
            onehot = jax.nn.one_hot(edge_type, NUM_REL, dtype=h.dtype)
            count = jax.ops.segment_sum(onehot, dst, num_segments=num_nodes)
            inv = jnp.where(count > 0, 1.0 / jnp.maximum(count, 1.0), 0.0)
            msg = msg * inv[dst, edge_type][:, None]
            agg = jax.ops.segment_sum(msg, dst, num_segments=num_nodes)
            return agg + h @ w_root + bias
        key = jax.random.key(seed)
        ks = jax.random.split(key, 16)
        d1 = IN_CH + TYPE_DIM
        inp = {'x': jax.random.normal(ks[0], (NUM_NODES, IN_CH), jnp.float32), 'node_type': jax.random.randint(ks[1], (NUM_NODES,), 0, NUM_NODE_TYPE, jnp.int32), 'edge_index': jax.random.randint(ks[2], (2, NUM_EDGES), 0, NUM_NODES, jnp.int32), 'edge_type': jax.random.randint(ks[3], (NUM_EDGES,), 0, NUM_REL, jnp.int32), 'node_emb': jax.random.normal(ks[4], (NUM_NODE_TYPE, TYPE_DIM), jnp.float32), 'w_rel1': _glorot(ks[5], (NUM_REL, d1, d1)), 'w_root1': _glorot(ks[6], (d1, d1)), 'b1': jnp.zeros((d1,), jnp.float32), 'w_rel2': _glorot(ks[7], (NUM_REL, d1, HID)), 'w_root2': _glorot(ks[8], (d1, HID)), 'b2': jnp.zeros((HID,), jnp.float32), 'w_rel3': _glorot(ks[9], (NUM_REL, HID, OUT)), 'w_root3': _glorot(ks[10], (HID, OUT)), 'b3': jnp.zeros((OUT,), jnp.float32)}
        return inp
    _L0_gnn_all = _L0_gnn_setup()
    _L0_gnn_in = {k: v for k, v in _L0_gnn_all.items() if k in ('node_emb', 'w_rel1', 'w_root1', 'b1', 'w_rel2', 'w_root2', 'b2', 'w_rel3', 'w_root3', 'b3')}
    del _L0_gnn_all

    def _L0_mix_setup():
        import jax, jax.numpy as jnp
        import numpy as np
        B, N, C = (16, 256, 768)
        H, D, M = (12, 64, 256)
        key = jax.random.key(seed)
        ks = jax.random.split(key, 6)
        rf = jax.random.normal(ks[5], (M, D), jnp.float32)
        rf = rf / jnp.linalg.norm(rf, axis=1, keepdims=True)
        return {'x': jax.random.normal(ks[0], (B, N, C), jnp.float32), 'W_qkv': jax.random.normal(ks[1], (C, 3 * C), jnp.float32) * C ** (-0.5), 'b_qkv': jax.random.normal(ks[2], (3 * C,), jnp.float32) * 0.02, 'W_proj': jax.random.normal(ks[3], (C, C), jnp.float32) * C ** (-0.5), 'b_proj': jax.random.normal(ks[4], (C,), jnp.float32) * 0.02, 'random_features': rf}
    _L0_mix_all = _L0_mix_setup()
    _L0_mix_in = {k: v for k, v in _L0_mix_all.items() if k in ('W_qkv', 'b_qkv', 'W_proj', 'b_proj', 'random_features')}
    del _L0_mix_all

    def _L0_ffn_setup():
        import math
        import jax, jax.numpy as jnp
        import numpy as np
        EMBED_CHOICES = [384, 576, 768]
        RATIO_CHOICES = [2, 3, 4]
        E_MAX = 768
        H_MAX = 192

        def new_gelu(x):
            c = math.sqrt(2.0 / math.pi)
            return 0.5 * x * (1.0 + jnp.tanh(c * (x + 0.044715 * x * x * x)))

        def _mixed_coeffs(alpha_e, alpha_r):
            h_idx = jnp.arange(H_MAX)
            d_idx = jnp.arange(E_MAX)
            C0 = jnp.zeros((H_MAX, E_MAX), jnp.float32)
            c0b = jnp.zeros((H_MAX,), jnp.float32)
            C1 = jnp.zeros((E_MAX, H_MAX), jnp.float32)
            c1b = jnp.zeros((E_MAX,), jnp.float32)
            for i, e in enumerate(EMBED_CHOICES):
                m_in = (d_idx < e).astype(jnp.float32)
                for j, r in enumerate(RATIO_CHOICES):
                    a = alpha_e[i] * alpha_r[j]
                    m_out = (h_idx < r * e).astype(jnp.float32)
                    C0 = C0 + a * (m_out[:, None] * m_in[None, :])
                    c0b = c0b + a * m_out
                    C1 = C1 + a * (m_in[:, None] * m_out[None, :])
                    c1b = c1b + a * m_in
            return (C0, c0b, C1, c1b)
        key = jax.random.key(seed)
        ks = jax.random.split(key, 6)
        x = jax.random.normal(ks[0], (8, 128, E_MAX), jnp.float32)
        w_fc = jax.random.normal(ks[1], (H_MAX, E_MAX), jnp.float32) * 0.02
        b_fc = jnp.zeros((H_MAX,), jnp.float32)
        w_proj = jax.random.normal(ks[2], (E_MAX, H_MAX), jnp.float32) * 0.02
        b_proj = jnp.zeros((E_MAX,), jnp.float32)
        alpha_e = jax.nn.softmax(jax.random.normal(ks[3], (3,), jnp.float32))
        alpha_r = jax.nn.softmax(jax.random.normal(ks[4], (3,), jnp.float32))
        return {'x': x, 'w_fc': w_fc, 'b_fc': b_fc, 'w_proj': w_proj, 'b_proj': b_proj, 'alpha_e': alpha_e, 'alpha_r': alpha_r}
    _L0_ffn_all = _L0_ffn_setup()
    _L0_ffn_in = {k: v for k, v in _L0_ffn_all.items() if k in ('w_fc', 'b_fc', 'w_proj', 'b_proj', 'alpha_e', 'alpha_r')}
    del _L0_ffn_all

    def _L1_gnn_setup():
        import jax, jax.numpy as jnp
        import numpy as np
        N_NODES = 625
        N_EDGES = 6250
        DIM = 768
        key = jax.random.key(seed)
        k1, k2, k3, k4 = jax.random.split(key, 4)
        x = jax.random.normal(k1, (N_NODES, DIM), dtype=jnp.float32)
        edge_index = jax.random.randint(k2, (2, N_EDGES), 0, N_NODES, dtype=jnp.int32)
        W = jax.random.normal(k3, (DIM, DIM), dtype=jnp.float32) / np.sqrt(DIM)
        b = jnp.zeros((DIM,), dtype=jnp.float32)
        return {'x': x, 'edge_index': edge_index, 'W': W, 'b': b}
    _L1_gnn_all = _L1_gnn_setup()
    _L1_gnn_in = {k: v for k, v in _L1_gnn_all.items() if k in ('W', 'b')}
    del _L1_gnn_all

    def _L1_mix_setup():
        import jax, jax.numpy as jnp
        import numpy as np
        import math
        B, N, C = (8, 256, 768)
        H = 12
        DH = C // H
        M = 256
        LN_EPS = 1e-05

        def _phi(t, random_features):
            norm_sq = 0.5 * jnp.sum(t * t, axis=-1, keepdims=True)
            proj = jnp.einsum('bhnd,md->bhnm', t, random_features)
            return jnp.exp(proj - norm_sq) * (1.0 / math.sqrt(M))
        key = jax.random.key(seed)
        ks = jax.random.split(key, 7)
        x = jax.random.normal(ks[0], (B, N, C), dtype=jnp.float32)
        W_qkv = jax.random.normal(ks[1], (C, 3 * C), dtype=jnp.float32) * (1.0 / math.sqrt(C))
        W_proj = jax.random.normal(ks[2], (C, C), dtype=jnp.float32) * (1.0 / math.sqrt(C))
        b_proj = jnp.zeros((C,), dtype=jnp.float32)
        gamma = jnp.ones((C,), dtype=jnp.float32)
        beta = jnp.zeros((C,), dtype=jnp.float32)
        random_features = jax.random.normal(ks[3], (M, DH), dtype=jnp.float32) / math.sqrt(DH)
        return {'x': x, 'W_qkv': W_qkv, 'W_proj': W_proj, 'b_proj': b_proj, 'gamma': gamma, 'beta': beta, 'random_features': random_features}
    _L1_mix_all = _L1_mix_setup()
    _L1_mix_in = {k: v for k, v in _L1_mix_all.items() if k in ('W_qkv', 'W_proj', 'b_proj', 'gamma', 'beta', 'random_features')}
    del _L1_mix_all

    def _L1_ffn_setup():
        import jax, jax.numpy as jnp
        import numpy as np
        K_ACTIVE = 2
        key = jax.random.key(seed)
        ks = jax.random.split(key, 9)
        B, S, D, F, E, NS = (2, 128, 768, 1536, 8, 1)
        sd = 1.0 / np.sqrt(D)
        sf = 1.0 / np.sqrt(F)
        return {'x': jax.random.normal(ks[0], (B, S, D), jnp.float32), 'Wg_s': jax.random.normal(ks[1], (NS, D, F), jnp.float32) * sd, 'Wu_s': jax.random.normal(ks[2], (NS, D, F), jnp.float32) * sd, 'Wd_s': jax.random.normal(ks[3], (NS, F, D), jnp.float32) * sf, 'Wg_r': jax.random.normal(ks[4], (E, D, F), jnp.float32) * sd, 'Wu_r': jax.random.normal(ks[5], (E, D, F), jnp.float32) * sd, 'Wd_r': jax.random.normal(ks[6], (E, F, D), jnp.float32) * sf, 'W_router': jax.random.normal(ks[7], (D, E), jnp.float32) * sd, 'expert_bias': jnp.zeros((E,), jnp.float32)}
    _L1_ffn_all = _L1_ffn_setup()
    _L1_ffn_in = {k: v for k, v in _L1_ffn_all.items() if k in ('Wg_s', 'Wu_s', 'Wd_s', 'Wg_r', 'Wu_r', 'Wd_r', 'W_router', 'expert_bias')}
    del _L1_ffn_all
    return {'x': x, 'src': src, 'dst': dst, 'edge_type_3': edge_type_3, 'node_type_3': node_type_3, 'L0_gnn_node_emb': _L0_gnn_in['node_emb'], 'L0_gnn_w_rel1': _L0_gnn_in['w_rel1'], 'L0_gnn_w_root1': _L0_gnn_in['w_root1'], 'L0_gnn_b1': _L0_gnn_in['b1'], 'L0_gnn_w_rel2': _L0_gnn_in['w_rel2'], 'L0_gnn_w_root2': _L0_gnn_in['w_root2'], 'L0_gnn_b2': _L0_gnn_in['b2'], 'L0_gnn_w_rel3': _L0_gnn_in['w_rel3'], 'L0_gnn_w_root3': _L0_gnn_in['w_root3'], 'L0_gnn_b3': _L0_gnn_in['b3'], 'L0_mix_W_qkv': _L0_mix_in['W_qkv'], 'L0_mix_b_qkv': _L0_mix_in['b_qkv'], 'L0_mix_W_proj': _L0_mix_in['W_proj'], 'L0_mix_b_proj': _L0_mix_in['b_proj'], 'L0_mix_random_features': _L0_mix_in['random_features'], 'L0_ffn_w_fc': _L0_ffn_in['w_fc'], 'L0_ffn_b_fc': _L0_ffn_in['b_fc'], 'L0_ffn_w_proj': _L0_ffn_in['w_proj'], 'L0_ffn_b_proj': _L0_ffn_in['b_proj'], 'L0_ffn_alpha_e': _L0_ffn_in['alpha_e'], 'L0_ffn_alpha_r': _L0_ffn_in['alpha_r'], 'L1_gnn_W': _L1_gnn_in['W'], 'L1_gnn_b': _L1_gnn_in['b'], 'L1_mix_W_qkv': _L1_mix_in['W_qkv'], 'L1_mix_W_proj': _L1_mix_in['W_proj'], 'L1_mix_b_proj': _L1_mix_in['b_proj'], 'L1_mix_gamma': _L1_mix_in['gamma'], 'L1_mix_beta': _L1_mix_in['beta'], 'L1_mix_random_features': _L1_mix_in['random_features'], 'L1_ffn_Wg_s': _L1_ffn_in['Wg_s'], 'L1_ffn_Wu_s': _L1_ffn_in['Wu_s'], 'L1_ffn_Wd_s': _L1_ffn_in['Wd_s'], 'L1_ffn_Wg_r': _L1_ffn_in['Wg_r'], 'L1_ffn_Wu_r': _L1_ffn_in['Wu_r'], 'L1_ffn_Wd_r': _L1_ffn_in['Wd_r'], 'L1_ffn_W_router': _L1_ffn_in['W_router'], 'L1_ffn_expert_bias': _L1_ffn_in['expert_bias']}

def reference(x, src, dst, edge_type_3, node_type_3, L0_gnn_node_emb, L0_gnn_w_rel1, L0_gnn_w_root1, L0_gnn_b1, L0_gnn_w_rel2, L0_gnn_w_root2, L0_gnn_b2, L0_gnn_w_rel3, L0_gnn_w_root3, L0_gnn_b3, L0_mix_W_qkv, L0_mix_b_qkv, L0_mix_W_proj, L0_mix_b_proj, L0_mix_random_features, L0_ffn_w_fc, L0_ffn_b_fc, L0_ffn_w_proj, L0_ffn_b_proj, L0_ffn_alpha_e, L0_ffn_alpha_r, L1_gnn_W, L1_gnn_b, L1_mix_W_qkv, L1_mix_W_proj, L1_mix_b_proj, L1_mix_gamma, L1_mix_beta, L1_mix_random_features, L1_ffn_Wg_s, L1_ffn_Wu_s, L1_ffn_Wd_s, L1_ffn_Wg_r, L1_ffn_Wu_r, L1_ffn_Wd_r, L1_ffn_W_router, L1_ffn_expert_bias):
    import jax
    import jax.numpy as jnp

    def _L0_gnn_ref(x, node_type, edge_index, edge_type, node_emb, w_rel1, w_root1, b1, w_rel2, w_root2, b2, w_rel3, w_root3, b3):
        import jax, jax.numpy as jnp
        import numpy as np
        NUM_NODES = 625
        NUM_EDGES = 10000
        IN_CH = 768
        TYPE_DIM = 128
        HID = 768
        OUT = 768
        NUM_REL = 3
        NUM_NODE_TYPE = 3

        def _glorot(key, shape):
            fan_in, fan_out = (shape[-2], shape[-1])
            lim = (6.0 / (fan_in + fan_out)) ** 0.5
            return jax.random.uniform(key, shape, jnp.float32, -lim, lim)

        def rgcn_conv(h, src, dst, edge_type, w_rel, w_root, bias):
            num_nodes = h.shape[0]
            xw = jnp.einsum('nd,rde->rne', h, w_rel)
            msg = xw[edge_type, src]
            onehot = jax.nn.one_hot(edge_type, NUM_REL, dtype=h.dtype)
            count = jax.ops.segment_sum(onehot, dst, num_segments=num_nodes)
            inv = jnp.where(count > 0, 1.0 / jnp.maximum(count, 1.0), 0.0)
            msg = msg * inv[dst, edge_type][:, None]
            agg = jax.ops.segment_sum(msg, dst, num_segments=num_nodes)
            return agg + h @ w_root + bias
        src, dst = (edge_index[0], edge_index[1])
        h = jnp.concatenate([x, node_emb[node_type]], axis=-1)
        h = jax.nn.relu(rgcn_conv(h, src, dst, edge_type, w_rel1, w_root1, b1))
        h = jax.nn.relu(rgcn_conv(h, src, dst, edge_type, w_rel2, w_root2, b2))
        h = jax.nn.relu(rgcn_conv(h, src, dst, edge_type, w_rel3, w_root3, b3))
        return h

    def _L0_mix_ref(x, W_qkv, b_qkv, W_proj, b_proj, random_features):
        import jax, jax.numpy as jnp
        import numpy as np
        B, N, C = (16, 256, 768)
        H, D, M = (12, 64, 256)
        b, n, c = x.shape
        qkv = (x @ W_qkv + b_qkv).reshape(b, n, 3, H, D)
        qkv = jnp.transpose(qkv, (2, 0, 3, 1, 4))
        q, k, v = (qkv[0], qkv[1], qkv[2])
        scale = D ** (-0.5)
        q = q * scale
        k = k * scale
        phi_q = jax.nn.relu(jnp.einsum('bhnd,md->bhnm', q, random_features))
        phi_k = jax.nn.relu(jnp.einsum('bhnd,md->bhnm', k, random_features))
        kv = jnp.einsum('bhnm,bhnd->bhmd', phi_k, v)
        attn = jnp.einsum('bhnm,bhmd->bhnd', phi_q, kv) / M
        out = jnp.transpose(attn, (0, 2, 1, 3)).reshape(b, n, c)
        return out @ W_proj + b_proj

    def _L0_ffn_ref(x, w_fc, b_fc, w_proj, b_proj, alpha_e, alpha_r):
        import math
        import jax, jax.numpy as jnp
        import numpy as np
        EMBED_CHOICES = [384, 576, 768]
        RATIO_CHOICES = [2, 3, 4]
        E_MAX = 768
        H_MAX = 192

        def new_gelu(x):
            c = math.sqrt(2.0 / math.pi)
            return 0.5 * x * (1.0 + jnp.tanh(c * (x + 0.044715 * x * x * x)))

        def _mixed_coeffs(alpha_e, alpha_r):
            h_idx = jnp.arange(H_MAX)
            d_idx = jnp.arange(E_MAX)
            C0 = jnp.zeros((H_MAX, E_MAX), jnp.float32)
            c0b = jnp.zeros((H_MAX,), jnp.float32)
            C1 = jnp.zeros((E_MAX, H_MAX), jnp.float32)
            c1b = jnp.zeros((E_MAX,), jnp.float32)
            for i, e in enumerate(EMBED_CHOICES):
                m_in = (d_idx < e).astype(jnp.float32)
                for j, r in enumerate(RATIO_CHOICES):
                    a = alpha_e[i] * alpha_r[j]
                    m_out = (h_idx < r * e).astype(jnp.float32)
                    C0 = C0 + a * (m_out[:, None] * m_in[None, :])
                    c0b = c0b + a * m_out
                    C1 = C1 + a * (m_in[:, None] * m_out[None, :])
                    c1b = c1b + a * m_in
            return (C0, c0b, C1, c1b)
        C0, c0b, C1, c1b = _mixed_coeffs(alpha_e, alpha_r)
        W0 = w_fc * C0
        b0 = b_fc * c0b
        h = jnp.einsum('bte,he->bth', x, W0) + b0
        h = new_gelu(h)
        W1 = w_proj * C1
        b1 = b_proj * c1b
        out = jnp.einsum('bth,eh->bte', h, W1) + b1
        return out

    def _L1_gnn_ref(x, edge_index, W, b):
        import jax, jax.numpy as jnp
        import numpy as np
        N_NODES = 625
        N_EDGES = 6250
        DIM = 768
        n = x.shape[0]
        loop = jnp.arange(n, dtype=edge_index.dtype)
        src = jnp.concatenate([edge_index[0], loop])
        dst = jnp.concatenate([edge_index[1], loop])
        deg = jax.ops.segment_sum(jnp.ones_like(dst, dtype=x.dtype), dst, num_segments=n)
        deg_inv_sqrt = jnp.where(deg > 0, jax.lax.rsqrt(deg), 0.0)
        norm = deg_inv_sqrt[src] * deg_inv_sqrt[dst]
        h = x @ W
        msg = h[src] * norm[:, None]
        out = jax.ops.segment_sum(msg, dst, num_segments=n)
        return out + b

    def _L1_mix_ref(x, W_qkv, W_proj, b_proj, gamma, beta, random_features):
        import jax, jax.numpy as jnp
        import numpy as np
        import math
        B, N, C = (8, 256, 768)
        H = 12
        DH = C // H
        M = 256
        LN_EPS = 1e-05

        def _phi(t, random_features):
            norm_sq = 0.5 * jnp.sum(t * t, axis=-1, keepdims=True)
            proj = jnp.einsum('bhnd,md->bhnm', t, random_features)
            return jnp.exp(proj - norm_sq) * (1.0 / math.sqrt(M))
        b, n, c = x.shape
        qkv = (x @ W_qkv).reshape(b, n, 3, H, DH)
        qkv = jnp.transpose(qkv, (2, 0, 3, 1, 4))
        q, k, v = (qkv[0], qkv[1], qkv[2])
        q_p = _phi(q, random_features)
        k_p = _phi(k, random_features)
        kv = jnp.einsum('bhnm,bhnd->bhmd', k_p, v)
        out = jnp.einsum('bhnm,bhmd->bhnd', q_p, kv)
        k_sum = jnp.sum(k_p, axis=2)
        normalizer = jnp.einsum('bhnm,bhm->bhn', q_p, k_sum)[..., None]
        out = out / (normalizer + 1e-06)
        x_attn = jnp.transpose(out, (0, 2, 1, 3)).reshape(b, n, c)
        x_attn = x_attn @ W_proj + b_proj
        y = x + x_attn
        mu = jnp.mean(y, axis=-1, keepdims=True)
        var = jnp.mean(jnp.square(y - mu), axis=-1, keepdims=True)
        return (y - mu) * jax.lax.rsqrt(var + LN_EPS) * gamma + beta

    def _L1_ffn_ref(x, Wg_s, Wu_s, Wd_s, Wg_r, Wu_r, Wd_r, W_router, expert_bias):
        import jax, jax.numpy as jnp
        import numpy as np
        K_ACTIVE = 2
        B, S, D = x.shape
        E = Wg_r.shape[0]
        xf = x.reshape(-1, D)
        T = xf.shape[0]
        g_s = jax.nn.silu(jnp.einsum('td,edf->etf', xf, Wg_s))
        u_s = jnp.einsum('td,edf->etf', xf, Wu_s)
        shared_out = jnp.einsum('etf,efd->td', g_s * u_s, Wd_s)
        logits = xf @ W_router + expert_bias
        top_vals, top_idx = jax.lax.top_k(logits, K_ACTIVE)
        rw = jax.nn.softmax(top_vals, axis=-1)
        combine = jnp.zeros((T, E), xf.dtype).at[jnp.arange(T)[:, None], top_idx].set(rw)
        g_r = jax.nn.silu(jnp.einsum('td,edf->etf', xf, Wg_r))
        u_r = jnp.einsum('td,edf->etf', xf, Wu_r)
        out_e = jnp.einsum('etf,efd->etd', g_r * u_r, Wd_r)
        routed_out = jnp.einsum('etd,te->td', out_e, combine)
        return (shared_out + routed_out).reshape(B, S, D)
    edge_index = jnp.stack([src, dst])
    xn = _layernorm(x, axis=-1)
    x = x + _L0_gnn_ref(xn, node_type_3, edge_index, edge_type_3, L0_gnn_node_emb, L0_gnn_w_rel1, L0_gnn_w_root1, L0_gnn_b1, L0_gnn_w_rel2, L0_gnn_w_root2, L0_gnn_b2, L0_gnn_w_rel3, L0_gnn_w_root3, L0_gnn_b3) + _L0_mix_ref(xn[None], L0_mix_W_qkv, L0_mix_b_qkv, L0_mix_W_proj, L0_mix_b_proj, L0_mix_random_features)[0]
    x = x + _L0_ffn_ref(_layernorm(x, axis=-1)[None], L0_ffn_w_fc, L0_ffn_b_fc, L0_ffn_w_proj, L0_ffn_b_proj, L0_ffn_alpha_e, L0_ffn_alpha_r)[0]
    xn = _layernorm(x, axis=-1)
    x = x + _L1_gnn_ref(xn, edge_index, L1_gnn_W, L1_gnn_b) + _L1_mix_ref(xn[None], L1_mix_W_qkv, L1_mix_W_proj, L1_mix_b_proj, L1_mix_gamma, L1_mix_beta, L1_mix_random_features)[0]
    x = x + _L1_ffn_ref(_layernorm(x, axis=-1)[None], L1_ffn_Wg_s, L1_ffn_Wu_s, L1_ffn_Wd_s, L1_ffn_Wg_r, L1_ffn_Wu_r, L1_ffn_Wd_r, L1_ffn_W_router, L1_ffn_expert_bias)[0]
    return x

_drawn_inputs = setup_inputs


def setup_inputs(seed=0):
    import zlib

    import numpy as np

    out = dict(_drawn_inputs(seed))
    spreads = {'L0_gnn_b1': (0.0, 0.1),
     'L0_gnn_b2': (0.0, 0.1),
     'L0_gnn_b3': (0.0, 0.1),
     'L0_ffn_b_fc': (0.0, 0.1),
     'L0_ffn_b_proj': (0.0, 0.1),
     'L1_gnn_b': (0.0, 0.1),
     'L1_mix_b_proj': (0.0, 0.1),
     'L1_mix_gamma': (1.0, 0.2),
     'L1_mix_beta': (0.0, 0.1),
     'L1_ffn_expert_bias': (0.0, 0.1)}
    factors = {}
    for name, (base, spread) in spreads.items():
        noise = np.random.default_rng([zlib.crc32(name.encode()), seed]).standard_normal(out[name].shape)
        drawn = base * np.exp(spread * noise) if base else spread * noise
        out[name] = jnp.asarray(drawn.astype(out[name].dtype))
    for name, factor in factors.items():
        out[name] = (out[name] * factor).astype(out[name].dtype)
    return out
```

```python
from contextlib import ExitStack

import numpy as np
import concourse.bass as bass
from concourse import mybir

F32 = mybir.dt.float32
F32R = mybir.dt.float32r
BF16 = mybir.dt.bfloat16
F16 = mybir.dt.float16
I32 = mybir.dt.int32
U32 = mybir.dt.uint32
ALU = mybir.AluOpType
ACT = mybir.ActivationFunctionType
AX = mybir.AxisListType

P = 128
NODES = 625
TT = (NODES + P - 1) // P
TS = [min(P, NODES - P * t) for t in range(TT)]
HN = 314
NT = 2 * HN
D = 768
KD = D // P
EMB = 128
D1 = D + EMB
K1 = D1 // P
EDGES = 10000
EP = 125
ET = EDGES // EP
RELS = 3
HEADS = 12
PAIRS = HEADS // 2
DH = 64
VW = DH + 2
MF = 256
H_FF = 192
HP = 96
EXPERTS = 8
F_MOE = 1536
EPS = 1e-5
WE_MIX, WE_GNN, WE_MOE = KD * 256, K1 * 256, KD * 384


def weight_view(w):
    return w.rearrange("(k p) n -> p k n", p=P)


class Stream:

    def __init__(self, k, name, chunks, elems, raws, splits):
        self.chunks, self.raws, self.splits, self.one = chunks, raws, splits, k.one[:]
        self.raw = k.sb(f"{name}_raw", [P, raws, elems], F32)
        self.hi = k.sb(f"{name}_hi", [P, splits, elems], F32R)
        self.lo = k.sb(f"{name}_lo", [P, splits, elems], F32R)
        self.loaded = [k.sem(f"{name}_loaded{i}") for i in range(raws)]
        self.hi_done = k.sem(f"{name}_hi_done")
        self.lo_done = k.sem(f"{name}_lo_done")
        self.freed = {}

    def landed(self, n):
        return 16 * sum(len(c[2]) for i, c in enumerate(self.chunks[:n + 1]) if i % self.raws == n % self.raws)

    def views(self, n):
        kt, cols, _ = self.chunks[n]
        s = n % self.splits
        return [b[:, s, 0:kt * cols].rearrange("p (k c) -> p k c", c=cols) for b in (self.hi, self.lo)]


def stream_loads(sp, st):
    for n, (kt, cols, parts) in enumerate(st.chunks):
        if n >= st.raws:
            sp.wait_ge(st.lo_done, n - st.raws + 1)
        dst = st.raw[:, n % st.raws, 0:kt * cols].rearrange("p (k c) -> p k c", c=cols)
        for c0, c1, src in parts:
            sp.dma_start(dst[:, :, c0:c1], src).then_inc(st.loaded[n % st.raws], 16)


def stream_splits(pool, st):
    for n, (kt, cols, _) in enumerate(st.chunks):
        size = kt * cols
        raw = st.raw[:, n % st.raws, 0:size]
        hi, lo = st.hi[:, n % st.splits, 0:size], st.lo[:, n % st.splits, 0:size]
        pool.wait_ge(st.loaded[n % st.raws], st.landed(n))
        if n >= st.splits:
            pool.wait_ge(*st.freed[n - st.splits])
        pool.tensor_tensor(hi, raw, st.one.broadcast_to([P, size]), ALU.mult).then_inc(st.hi_done, 1)
        pool.wait_ge(st.hi_done, n + 1)
        pool.tensor_tensor(lo, raw, hi.bitcast(F32), ALU.subtract).then_inc(st.lo_done, 1)


def one_chunk(w, cols, c0):
    v = weight_view(w)
    return (v.shape[1], cols, [(0, cols, v[:, :, c0:c0 + cols])])


def split_product(pe, out, lhs, rhs, first, last):
    for i, (a, b) in enumerate(((0, 0), (0, 1), (1, 0))):
        mm = pe.matmul(out, lhs[a], rhs[b], start=(first and i == 0), stop=(last and i == 2))
    return mm


def split_product_wide(pe, bank_pair, lhs, rhs, first, last):
    for i, (a, b) in enumerate(((0, 0), (0, 1), (1, 0))):
        for h in range(2):
            mm = pe.matmul(bank_pair[:, h, 0:HN], lhs[a], rhs(b, h),
                           start=(first and i == 0), stop=(last and i == 2))
    return mm


def halves(t):
    return t.rearrange("p (h n) -> p h n", h=2)


def signals(k, phase, names):
    return {name: k.sem(f"{phase}_{name}") for name in names}


class Link:

    def __init__(self, eng, sem):
        self.eng, self.sem, self.n = eng, sem, 0

    def __call__(self, ins):
        self.n += 1
        ins.then_inc(self.sem, 1)
        self.eng.wait_ge(self.sem, self.n)



def turn_tile(pe, k, src, t):
    ts = TS[t]
    for j in range(KD):
        bank = k.banks[2 * (t % 2) + j // 4]
        mm = pe.transpose(bank[:, (j % 4) * P:(j % 4) * P + ts], src[0:ts, j * P:(j + 1) * P], k.ident[0:ts, 0:ts])
    return mm


def to_feature_major_act(act, k, dst, t, turned, hi_done):
    act.wait_ge(turned, t + 1)
    for b, (j0, j1) in enumerate(((0, 4), (4, KD))):
        src = k.banks[2 * (t % 2) + b][:, 0:(j1 - j0) * P].rearrange("p (j n) -> p j n", n=P)[:, :, 0:TS[t]]
        act.activation(dst[:, j0:j1, 0, t * P:t * P + TS[t]], src, ACT.Copy).then_inc(hi_done, 1)


def to_feature_major_dve(dve, k, dst, t, hi_done, lo_done):
    dve.wait_ge(hi_done, 2 * t + 2)
    for b, (j0, j1) in enumerate(((0, 4), (4, KD))):
        src = k.banks[2 * (t % 2) + b][:, 0:(j1 - j0) * P].rearrange("p (j n) -> p j n", n=P)[:, :, 0:TS[t]]
        ins = dve.tensor_tensor(dst[:, j0:j1, 1, t * P:t * P + TS[t]], src,
                                dst[:, j0:j1, 0, t * P:t * P + TS[t]].bitcast(F32), ALU.subtract)
    ins.then_inc(lo_done, 1)


def norm_stats(dve, link, k, src, mean_var):
    for t in range(TT):
        ts = TS[t]
        for h in range(2):
            ins = dve.bn_stats(k.bn[0:ts, t, h, :], src[0:ts, t, h * 384:(h + 1) * 384])
        link(ins)
        dve.bn_aggr(mean_var[0:ts, t, :], k.bn[0:ts, t, :, :].rearrange("p h s -> p (h s)"))


def phase_norm(k, name, load_x=False):
    with ExitStack() as ctx:
        k.begin(ctx)
        xn = k.sb(f"{name}_xn", [P, 2, D], F32)
        s = signals(k, name, (
            "x_loaded", "consts", "chain", "var_ready", "root_ready", "xn_ready", "turned", "hi_done", "lo_done"))
        block = ctx.enter_context(k.nc.Block())

        @block.sync
        def _(sp):
            if load_x:
                for t in range(TT):
                    sp.dma_start(k.x[0:TS[t], t, :], k.x_in[t * P:t * P + TS[t], :]).then_inc(s["x_loaded"], 16)

        @block.gpsimd
        def _(pool):
            k.clear_last(pool)
            if load_x:
                pool.memset(k.one[:], 1.0)
                pool.memset(k.ident[:], 0.0).then_inc(s["consts"], 1)
                pool.wait_ge(s["consts"], 1)
                pool.affine_select(out=k.ident[:], in_=k.ident[:], compare_op=ALU.not_equal, fill=1.0, base=0,
                                   pattern=[[-1, P]], channel_multiplier=1).then_inc(s["consts"], 1)

        @block.vector
        def _(dve):
            link = Link(dve, s["chain"])
            if load_x:
                dve.memset(k.xt[:, :, :, NODES:NT].bitcast(F32), 0.0)
            if load_x:
                dve.memset(k.mv[:], 1.0)
                link(dve.memset(k.bn[:], 0.0))
                dve.wait_ge(s["x_loaded"], 16 * TT)
            norm_stats(dve, link, k, k.x, k.mv)
            rsqrt_of_var(dve, link, k, s)
            for t in range(TT):
                ts = TS[t]
                if t >= 2:
                    dve.wait_ge(s["turned"], t - 1)
                dve.tensor_scalar(xn[0:ts, t % 2, :], k.x[0:ts, t, :], k.mv[0:ts, t, 0:1], k.rstd[0:ts, t:t + 1],
                                  ALU.subtract, ALU.mult).then_inc(s["xn_ready"], 1)
                if t >= 1:
                    to_feature_major_dve(dve, k, k.xt, t - 1, s["hi_done"], s["lo_done"])
            to_feature_major_dve(dve, k, k.xt, TT - 1, s["hi_done"], s["lo_done"])

        @block.scalar
        def _(act):
            act.wait_ge(s["var_ready"], 1)
            act.activation(k.root[:], k.ve[:], ACT.Sqrt).then_inc(s["root_ready"], 1)
            for t in range(TT):
                to_feature_major_act(act, k, k.xt, t, s["turned"], s["hi_done"])

        @block.tensor
        def _(pe):
            if load_x:
                pe.wait_ge(s["consts"], 2)
            for t in range(TT):
                pe.wait_ge(s["xn_ready"], t + 1)
                if t >= 2:
                    pe.wait_ge(s["lo_done"], t - 1)
                turn_tile(pe, k, xn[:, t % 2, :], t).then_inc(s["turned"], 1)


def rsqrt_of_var(dve, link, k, s):
    link(dve.tensor_copy(k.ve[:, 0:1], k.mv[:, 0, 1:2]))
    link(dve.tensor_scalar(k.ve[:], k.mv[:, :, 1], EPS, None, ALU.add))
    rsqrt_of_ve(dve, link, k, s)


def rsqrt_of_ve(dve, link, k, s):
    dve.tensor_copy(k.tmp5[:], k.ve[:]).then_inc(s["var_ready"], 1)
    dve.wait_ge(s["root_ready"], 1)
    link(dve.reciprocal(k.rstd[:], k.root[:]))
    link(dve.tensor_tensor(k.tmp5[:], k.rstd[:], k.rstd[:], ALU.mult))
    link(dve.tensor_tensor(k.tmp5[:], k.tmp5[:], k.ve[:], ALU.mult))
    link(dve.tensor_scalar(k.tmp5[:], k.tmp5[:], -0.5, 1.5, ALU.mult, ALU.add))
    link(dve.tensor_tensor(k.rstd[:], k.rstd[:], k.tmp5[:], ALU.mult))



def phase_attend(k, name, second, w_qkv, b_qkv, rf):
    pw = weight_view(w_qkv)
    chunks = [(KD, 256, [(0, 256, pw[:, :, 2 * D + c * 256:2 * D + (c + 1) * 256])]) for c in range(3)]
    chunks += [(KD, 256, [(0, P, pw[:, :, p * P:(p + 1) * P]), (P, 2 * P, pw[:, :, D + p * P:D + (p + 1) * P])])
               for p in range(PAIRS)]
    FUNC = ACT.Exp if second else ACT.Relu
    KV_SCALE = 1.0 / MF if second else 1.0 / (DH * MF)
    with ExitStack() as ctx:
        k.begin(ctx)
        st = Stream(k, f"{name}_w", chunks, WE_MIX, 2, 2)
        vt = k.sb(f"{name}_v", [P, TT, 2, HEADS, VW], F32R)
        vf = k.sb(f"{name}_vf", [P, 2, 256], F32)
        qk = k.sb(f"{name}_qk", [P, 2, 2, NT], F32R)
        phik = k.sb(f"{name}_phik", [P, TT, 2, 512], F32R)
        phiq = k.sb(f"{name}_phiq", [P, 4, 2, NT], F32R)
        scratch = k.x[:].rearrange("p t d -> p (t d)")
        qkf = scratch[:, 0:2 * NT].rearrange("p (a n) -> p a n", a=2)
        pf = scratch[:, 2 * NT:4 * NT].rearrange("p (a n) -> p a n", a=2)
        sqf = scratch[:, 4 * NT:5 * NT]
        a_sb = k.a
        kv = k.sb(f"{name}_kv", [P, 2, 4, VW], F32R)
        kvf = k.sb(f"{name}_kvf", [P, 4, VW], F32)
        rfin = k.sb(f"{name}_rfin", [P, 2, DH], F32)
        rff = k.sb(f"{name}_rff", [P, 512], F32)
        rfbd = k.sb(f"{name}_rfbd", [P, 2, 512], F32R)
        if second:
            sq = k.sb(f"{name}_sq", [P, 2, 2, NT], F32R)
            nh = k.sb(f"{name}_nh", [P, 512], F32R)
            den = k.sb(f"{name}_den", [P, 2, 2], F32)
        else:
            bv = k.sb(f"{name}_bv", [P, D], F32)
            bq = k.sb(f"{name}_bq", [P, 2 * PAIRS], F32)
        s = signals(k, name, (
            "small", "consts", "chain", "rf_turned", "rf_bd", "rf_hi", "rf_ready", "v_mm", "v_f", "v_hi", "v_lo",
            "qk_mm", "qk_f", "qk_hi", "qk_lo", "sq_f", "sq_hi", "pk_mm", "pk_f", "pk_hi", "pk_lo",
            "pq_mm", "pq_f", "pq_hi", "pq_lo", "kv_mm", "kv_f", "kv_hi", "kv_lo", "at_mm", "at_out",
            ))
        smalls = 1 if second else 3
        st.freed.update({c: (s["v_mm"], TT * (c + 1)) for c in range(3)})
        st.freed.update({3 + p: (s["qk_mm"], 2 * (p + 1)) for p in range(PAIRS)})
        block = ctx.enter_context(k.nc.Block())
        kvb = k.banks[2]

        @block.sync
        def _(sp):
            sp.dma_start(rfin[:], rf.rearrange("(a p) d -> p a d", p=P)).then_inc(s["small"], 16)
            if not second:
                sp.dma_start(bv[:], b_qkv[2 * D:3 * D].partition_broadcast(P)).then_inc(s["small"], 16)
                sp.dma_start(bq[:], b_qkv[0:2 * D].rearrange("(j p) -> p j", p=P),
                             allow_slow_non_contiguous=True).then_inc(s["small"], 16)
            stream_loads(sp, st)

        @block.gpsimd
        def _(pool):
            k.clear_last(pool)
            stream_splits(pool, st)

        @block.tensor
        def _(pe):
            pe.wait_ge(s["small"], 16 * smalls)
            for a in range(2):
                mm = pe.transpose(k.banks[7][0:DH, a * P:(a + 1) * P], rfin[:, a, :], k.ident[:])
            mm.then_inc(s["rf_turned"], 1)
            for c in range(3):
                pe.wait_ge(st.lo_done, c + 1)
                wh = st.views(c)
                for t in range(TT):
                    i = c * TT + t
                    if i >= 2:
                        pe.wait_ge(s["v_f"], i - 1)
                    for j in range(KD):
                        mm = split_product(pe, k.banks[i % 2][0:TS[t], 0:256],
                                           [k.xt[:, j, a, t * P:t * P + TS[t]] for a in range(2)],
                                           [w[:, j, :] for w in wh], j == 0, j == KD - 1)
                    mm.then_inc(s["v_mm"], 1)

            def project_qk(p):
                n = 3 + p
                pe.wait_ge(st.lo_done, n + 1)
                wh = st.views(n)
                for a in range(2):
                    i = 2 * p + a
                    if i >= 2:
                        pe.wait_ge(s["qk_f"], i - 1)
                    if a == 1 and p >= 1:
                        pe.wait_ge(s["kv_f"], p)
                    for j in range(KD):
                        mm = split_product_wide(pe, k.pair[2 - a], [w[:, j, a * P:(a + 1) * P] for w in wh],
                                                lambda b, h: k.xt[:, j, b, h * HN:(h + 1) * HN], j == 0, j == KD - 1)
                    mm.then_inc(s["qk_mm"], 1)

            def features_k(p):
                pe.wait_ge(s["qk_lo"], 2 * p + 2)
                for t in range(TT):
                    i = p * TT + t
                    if i >= 2:
                        pe.wait_ge(s["pk_f"], i - 1)
                    if t < 2 and p >= 1:
                        pe.wait_ge(s["pq_f"], 4 * p)
                    out = k.banks[6 + t % 2][0:TS[t], 0:512]
                    mm = split_product(pe, out, [qk[:, 1, a, t * P:t * P + TS[t]] for a in range(2)],
                                       [rfbd[:, a, :] for a in range(2)], True, not second)
                    if second:
                        for a in range(2):
                            mm = pe.matmul(out, sq[:, 1, a, t * P:t * P + TS[t]], nh[:], start=False, stop=(a == 1))
                    mm.then_inc(s["pk_mm"], 1)

            def features_q(p):
                for m in range(4):
                    i = p * 4 + m
                    if i >= 2:
                        pe.wait_ge(s["pq_f"], i - 1)
                    if m == 0:
                        pe.wait_ge(s["at_out"], TT * p)
                    if m == 1:
                        pe.wait_ge(s["pk_f"], TT * (p + 1))
                    pair = k.pair[0] if m % 2 == 0 else k.pair[3]
                    mm = split_product_wide(pe, pair, [rfbd[:, a, m * P:(m + 1) * P] for a in range(2)],
                                            lambda b, h: qk[:, 0, b, h * HN:(h + 1) * HN], True, not second)
                    if second:
                        for a in range(2):
                            for h in range(2):
                                mm = pe.matmul(pair[:, h, 0:HN], nh[:, m * P:(m + 1) * P],
                                               sq[:, 0, a, h * HN:(h + 1) * HN], start=False, stop=(a == 1))
                    mm.then_inc(s["pq_mm"], 1)

            def keys_values(p):
                pe.wait_ge(s["pk_lo"], TT * (p + 1))
                pe.wait_ge(s["qk_f"], 2 * p + 2)
                for m in range(4):
                    for t in range(TT):
                        mm = split_product(pe, kvb[:, m * VW:(m + 1) * VW],
                                           [phik[0:TS[t], t, a, m * P:(m + 1) * P] for a in range(2)],
                                           [vt[0:TS[t], t, a, 2 * p + m // 2, :] for a in range(2)], t == 0, t == TT - 1)
                mm.then_inc(s["kv_mm"], 1)

            def attend(p):
                pe.wait_ge(s["kv_lo"], p + 1)
                pe.wait_ge(s["pq_lo"], 4 * (p + 1))
                for t in range(TT):
                    i = p * TT + t
                    if t >= 2:
                        pe.wait_ge(s["at_out"], i - 1)
                    for hd in range(2):
                        for m in range(2):
                            mm = split_product(pe, k.banks[t % 2][0:TS[t], hd * VW:(hd + 1) * VW],
                                               [phiq[:, 2 * hd + m, a, t * P:t * P + TS[t]] for a in range(2)],
                                               [kv[:, a, 2 * hd + m, :] for a in range(2)], m == 0, m == 1)
                    mm.then_inc(s["at_mm"], 1)

            pe.wait_ge(s["rf_ready"], 1)
            pe.wait_ge(s["v_lo"], 3 * TT)
            project_qk(0)
            for p in range(PAIRS):
                features_k(p)
                features_q(p)
                keys_values(p)
                if p + 1 < PAIRS:
                    project_qk(p + 1)
                attend(p)

        @block.scalar
        def _(act):
            def high(dst, src, after, at_least, done):
                act.wait_ge(after, at_least)
                act.activation(dst, src, ACT.Copy).then_inc(done, 1)

            high(rfbd[:, 0, :], rff[:], s["rf_bd"], 1, s["rf_hi"])
            for i in range(3 * TT):
                c, t = i // TT, i % TT
                high(vt[0:TS[t], t, 0, 4 * c:4 * c + 4, 0:DH],
                     vf[0:TS[t], i % 2, :].rearrange("p (h d) -> p h d", d=DH), s["v_f"], i + 1, s["v_hi"])

            def qk_high(p):
                for a in range(2):
                    i = 2 * p + a
                    if p >= 1 and a == 0:
                        act.wait_ge(s["pk_mm"], TT * p)
                        act.wait_ge(s["pq_mm"], 4 * p)
                    high(qk[:, a, 0, :], qkf[:, a, :], s["qk_f"], i + 1, s["qk_hi"])
                    if second:
                        high(sq[:, a, 0, :], sqf[:], s["sq_f"], i + 1, s["sq_hi"])

            qk_high(0)
            for p in range(PAIRS):
                for t in range(TT):
                    i = p * TT + t
                    if p >= 1 and t == 0:
                        act.wait_ge(s["kv_mm"], p)
                    act.wait_ge(s["pk_mm"], i + 1)
                    if t >= 2:
                        act.wait_ge(s["pk_lo"], i - 1)
                    elif p >= 1:
                        act.wait_ge(s["pq_lo"], 4 * p)
                    f = pf[0:TS[t], t % 2, 0:512]
                    act.activation(f, k.banks[6 + t % 2][0:TS[t], 0:512], FUNC).then_inc(s["pk_f"], 1)
                    high(phik[0:TS[t], t, 0, :], f, s["pk_f"], i + 1, s["pk_hi"])
                for m in range(4):
                    i = p * 4 + m
                    if p >= 1 and m == 0:
                        act.wait_ge(s["at_mm"], TT * p)
                    act.wait_ge(s["pq_mm"], i + 1)
                    if m >= 2:
                        act.wait_ge(s["pq_lo"], i - 1)
                    else:
                        act.wait_ge(s["pk_lo"], TT * (p + 1))
                    pair = k.pair[0] if m % 2 == 0 else k.pair[3]
                    f = pf[:, m % 2, :]
                    act.activation(halves(f), pair[:, :, 0:HN], FUNC).then_inc(s["pq_f"], 1)
                    high(phiq[:, m, 0, :], f, s["pq_f"], i + 1, s["pq_hi"])
                if p >= 1:
                    act.wait_ge(s["at_mm"], TT * p)
                act.wait_ge(s["kv_mm"], p + 1)
                if p >= 1:
                    act.wait_ge(s["kv_lo"], p)
                act.activation(kvf[:], kvb[:, 0:4 * VW].rearrange("p (m v) -> p m v", v=VW), ACT.Copy,
                               scale=KV_SCALE).then_inc(s["kv_f"], 1)
                high(kv[:, 0, :, :], kvf[:], s["kv_f"], p + 1, s["kv_hi"])
                if p + 1 < PAIRS:
                    qk_high(p + 1)
                if not second:
                    for t in range(TT):
                        act.wait_ge(s["at_mm"], p * TT + t + 1)
                        act.activation(a_sb[0:TS[t], t, p * P:(p + 1) * P].rearrange("p (h d) -> p h d", d=DH),
                                       k.banks[t % 2][0:TS[t], 0:2 * VW].rearrange("p (h d) -> p h d", d=VW)[:, :, 0:DH],
                                       ACT.Copy).then_inc(s["at_out"], 1)

        @block.vector
        def _(dve):
            link = Link(dve, s["chain"])
            dve.memset(vt[:, :, :, :, DH:VW].bitcast(F32), 0.0)
            link(dve.memset(rff[:], 0.0))
            link(dve.memset(vt[:, :, 0, :, DH:DH + 1].bitcast(F32), 1.0))
            if second:
                link(dve.memset(nh[:].bitcast(F32), 0.0))
                for hd in range(2):
                    link(dve.memset(nh[hd * DH:(hd + 1) * DH, hd * MF:(hd + 1) * MF].bitcast(F32), -0.5))
            dve.wait_ge(s["rf_turned"], 1)
            for hd in range(2):
                ins = dve.tensor_copy(rff[hd * DH:(hd + 1) * DH, hd * MF:(hd + 1) * MF], k.banks[7][0:DH, 0:MF])
                if hd == 0:
                    link(ins)
            ins.then_inc(s["rf_bd"], 1)
            dve.wait_ge(s["rf_hi"], 1)
            dve.tensor_tensor(rfbd[:, 1, :], rff[:], rfbd[:, 0, :].bitcast(F32), ALU.subtract).then_inc(s["rf_ready"], 1)
            dve.wait_ge(s["small"], 16 * smalls)

            def v_low(i):
                c, t = i // TT, i % TT
                dve.wait_ge(s["v_hi"], i + 1)
                dve.tensor_tensor(vt[0:TS[t], t, 1, 4 * c:4 * c + 4, 0:DH],
                                  vf[0:TS[t], i % 2, :].rearrange("p (h d) -> p h d", d=DH),
                                  vt[0:TS[t], t, 0, 4 * c:4 * c + 4, 0:DH].bitcast(F32), ALU.subtract).then_inc(s["v_lo"], 1)

            for i in range(3 * TT):
                c, t = i // TT, i % TT
                dve.wait_ge(s["v_mm"], i + 1)
                if i >= 2:
                    dve.wait_ge(s["v_lo"], i - 1)
                src, dst = k.banks[i % 2][0:TS[t], 0:256], vf[0:TS[t], i % 2, :]
                if second:
                    dve.tensor_copy(dst, src).then_inc(s["v_f"], 1)
                else:
                    dve.tensor_tensor(dst, src, bv[0:TS[t], c * 256:(c + 1) * 256], ALU.add).then_inc(s["v_f"], 1)
                if i >= 1:
                    v_low(i - 1)
            v_low(3 * TT - 1)

            def qk_parts(p):
                for a in range(2):
                    i = 2 * p + a
                    dve.wait_ge(s["qk_mm"], i + 1)
                    if p >= 1:
                        dve.wait_ge(s["qk_lo"], 2 * p)
                    src = k.pair[2 - a][:, :, 0:HN]
                    if second:
                        dve.tensor_copy(halves(qkf[:, a, :]), src).then_inc(s["qk_f"], 1)
                        dve.wait_ge(s["qk_f"], i + 1)
                        if i >= 1:
                            dve.wait_ge(s["sq_hi"], i)
                        dve.tensor_tensor(sqf[:], qkf[:, a, :], qkf[:, a, :], ALU.mult).then_inc(s["sq_f"], 1)
                        dve.wait_ge(s["sq_hi"], i + 1)
                        link(dve.tensor_tensor(sq[:, a, 1, :], sqf[:], sq[:, a, 0, :].bitcast(F32), ALU.subtract))
                    else:
                        dve.tensor_scalar(halves(qkf[:, a, :]), src, bq[:, a * PAIRS + p:a * PAIRS + p + 1], None,
                                          ALU.add).then_inc(s["qk_f"], 1)
                    dve.wait_ge(s["qk_hi"], i + 1)
                    dve.tensor_tensor(qk[:, a, 1, :], qkf[:, a, :], qk[:, a, 0, :].bitcast(F32),
                                      ALU.subtract).then_inc(s["qk_lo"], 1)

            qk_parts(0)
            for p in range(PAIRS):
                for t in range(TT):
                    dve.wait_ge(s["pk_hi"], p * TT + t + 1)
                    dve.tensor_tensor(phik[0:TS[t], t, 1, :], pf[0:TS[t], t % 2, 0:512],
                                      phik[0:TS[t], t, 0, :].bitcast(F32), ALU.subtract).then_inc(s["pk_lo"], 1)
                for m in range(4):
                    dve.wait_ge(s["pq_hi"], p * 4 + m + 1)
                    dve.tensor_tensor(phiq[:, m, 1, :], pf[:, m % 2, :], phiq[:, m, 0, :].bitcast(F32),
                                      ALU.subtract).then_inc(s["pq_lo"], 1)
                dve.wait_ge(s["kv_hi"], p + 1)
                dve.tensor_tensor(kv[:, 1, :, :], kvf[:], kv[:, 0, :, :].bitcast(F32), ALU.subtract).then_inc(s["kv_lo"], 1)
                if p + 1 < PAIRS:
                    qk_parts(p + 1)
                if second:
                    for t in range(TT):
                        ts = TS[t]
                        dve.wait_ge(s["at_mm"], p * TT + t + 1)
                        o = k.banks[t % 2][0:ts, 0:2 * VW].rearrange("p (h d) -> p h d", d=VW)
                        link(dve.tensor_scalar(den[0:ts, 0, :], o[:, :, DH], 1e-6, None, ALU.add))
                        link(dve.reciprocal(den[0:ts, 1, :], den[0:ts, 0, :]))
                        for hd in range(2):
                            ins = dve.tensor_scalar(a_sb[0:ts, t, (2 * p + hd) * DH:(2 * p + hd + 1) * DH],
                                                    o[:, hd, 0:DH], den[0:ts, 1, hd:hd + 1], None, ALU.mult)
                        ins.then_inc(s["at_out"], 1)
                        dve.wait_ge(s["at_out"], p * TT + t + 1)


def phase_project(k, name, second, w_proj, b_proj, x_src, gamma=None, beta=None):
    chunks = [one_chunk(w_proj, 256, c * 256) for c in range(3)]
    with ExitStack() as ctx:
        k.begin(ctx)
        st = Stream(k, f"{name}_w", chunks, WE_MIX, 2, 3)
        at = k.sb(f"{name}_at", [P, KD, 2, NT], F32R)
        bp = k.sb(f"{name}_bp", [P, D], F32)
        a_sb = k.a
        if second:
            gb = k.sb(f"{name}_gb", [P, 2, D], F32)
            y_sb = k.sb(f"{name}_y", [P, TT, D], F32)
        s = signals(k, name, (
            "small", "x_loaded", "chain", "turned", "t_hi", "t_lo", "proj_mm", "proj_out", "var_ready", "root_ready"))
        st.freed.update({c: (s["proj_mm"], TT * (c + 1)) for c in range(3)})
        smalls = 3 if second else 1
        block = ctx.enter_context(k.nc.Block())

        @block.sync
        def _(sp):
            stream_loads(sp, st)

        @block.gpsimd
        def _(pool):
            k.clear_last(pool)
            stream_splits(pool, st)

        @block.tensor
        def _(pe):
            for t in range(TT):
                if t >= 2:
                    pe.wait_ge(s["t_lo"], t - 1)
                turn_tile(pe, k, a_sb[:, t, :], t).then_inc(s["turned"], 1)
            pe.wait_ge(s["t_lo"], TT)
            for c in range(3):
                pe.wait_ge(st.lo_done, c + 1)
                wh = st.views(c)
                for t in range(TT):
                    i = c * TT + t
                    if i >= 2:
                        pe.wait_ge(s["proj_out"], i - 1)
                    for j in range(KD):
                        mm = split_product(pe, k.banks[4 + i % 2][0:TS[t], 0:256],
                                           [at[:, j, a, t * P:t * P + TS[t]] for a in range(2)],
                                           [w[:, j, :] for w in wh], j == 0, j == KD - 1)
                    mm.then_inc(s["proj_mm"], 1)

        @block.scalar
        def _(act):
            act.dma_start(bp[:], b_proj.partition_broadcast(P)).then_inc(s["small"], 16)
            if second:
                act.dma_start(gb[:, 0, :], gamma.partition_broadcast(P)).then_inc(s["small"], 16)
                act.dma_start(gb[:, 1, :], beta.partition_broadcast(P)).then_inc(s["small"], 16)
            for t in range(TT):
                act.dma_start(k.x[0:TS[t], t, :], x_src[t * P:t * P + TS[t], :]).then_inc(s["x_loaded"], 16)
            for t in range(TT):
                to_feature_major_act(act, k, at, t, s["turned"], s["t_hi"])
            if second:
                act.wait_ge(s["var_ready"], 1)
                act.activation(k.root[:], k.ve[:], ACT.Sqrt).then_inc(s["root_ready"], 1)

        @block.vector
        def _(dve):
            link = Link(dve, s["chain"])
            for t in range(TT):
                to_feature_major_dve(dve, k, at, t, s["t_hi"], s["t_lo"])
            dve.wait_ge(s["small"], 16 * smalls)
            dve.wait_ge(s["x_loaded"], 16 * TT)
            y_all = y_sb if second else k.x
            if second:
                for t in range(TT):
                    ins = dve.tensor_scalar(y_sb[0:TS[t], t, :], k.x[0:TS[t], t, :], k.mv[0:TS[t], t, 0:1],
                                            k.rstd[0:TS[t], t:t + 1], ALU.subtract, ALU.mult)
                link(ins)
            for t in range(TT):
                ins = dve.tensor_tensor(y_all[0:TS[t], t, :], y_all[0:TS[t], t, :], bp[0:TS[t], :], ALU.add)
            link(ins)
            for i in range(3 * TT):
                c, t = i // TT, i % TT
                y = y_all[0:TS[t], t, c * 256:(c + 1) * 256]
                dve.wait_ge(s["proj_mm"], i + 1)
                dve.tensor_tensor(y, k.banks[4 + i % 2][0:TS[t], 0:256], y, ALU.add).then_inc(s["proj_out"], 1)
            if second:
                dve.wait_ge(s["proj_out"], 3 * TT)
                norm_stats(dve, link, k, y_sb, k.mv)
                rsqrt_of_var(dve, link, k, s)
                for op in range(4):
                    for t in range(TT):
                        ts = TS[t]
                        y = y_sb[0:ts, t, :]
                        if op == 0:
                            ins = dve.tensor_scalar(y, y, k.mv[0:ts, t, 0:1], k.rstd[0:ts, t:t + 1], ALU.subtract, ALU.mult)
                        elif op == 3:
                            ins = dve.tensor_tensor(k.x[0:ts, t, :], k.x[0:ts, t, :], y, ALU.add)
                        else:
                            ins = dve.tensor_tensor(y, y, gb[0:ts, op - 1, :], ALU.mult if op == 1 else ALU.add)
                    link(ins)



UNROLL = 4
SW = TT * P


def count_pieces():
    pieces, seen = [], set()
    for s in range(TT):
        c0 = s * NT
        while c0 < (s + 1) * NT:
            c1 = min((s + 1) * NT, (c0 // 512 + 1) * 512)
            pieces.append((s, c0, c1, c0 // 512 not in seen))
            seen.add(c0 // 512)
            c0 = c1
    return pieces


def phase_counts(k, src, dst, edge_type, node_emb, node_type):
    flat = k.psum[:].rearrange("p b n -> p (b n)")
    with ExitStack() as ctx:
        k.begin(ctx)
        edges_i = k.sb("edges_i", [EP, 3, ET], I32)
        edges_f = k.sb("edges_f", [EP, 3, ET], F32)
        of_rel = k.sb("of_rel", [EP, RELS, ET], F32)
        iota_i = k.sb("iota_i", [P, SW], I32)
        iota = k.sb("iota", [P, SW], F16)
        src_hot = k.sb("src_hot", [EP, UNROLL, SW], BF16)
        dst_hot = k.sb("dst_hot", [EP, UNROLL, NT], BF16)
        total = k.sb("count_total", [P, TT, NT], F32)
        ones_f = k.sb("ones_f", [P, P], F32)
        ones = k.sb("ones_r", [P, P], F32R)
        pos = k.sb("count_pos", [P, NT], F32)
        cnt = k.sb("count_rel", [P, NT], F32)
        emb_sb = k.sb("node_emb", [RELS, EMB], F32)
        type_i = k.sb("type_i", [RELS, NODES], I32)
        type_f = k.sb("type_f", [RELS, NODES], F32)
        own = k.sb("own_type", [RELS, 1], F32)
        onehot = k.sb("type_onehot", [RELS, NT], F32)
        s = signals(k, "c", (
            "loaded", "iota_made", "chain", "hot", "tile_mm", "copied", "ones_made", "sum_mm", "sum_read",
            "total_made", "saved", "emb_loaded", "own_made", "emb_made", "emb_ready", "emb_hi"))
        block = ctx.enter_context(k.nc.Block())
        pieces = count_pieces()

        @block.sync
        def _(sp):
            for i, e in enumerate((src, dst, edge_type)):
                sp.dma_start(edges_i[:, i, :], e.rearrange("(p j) -> p j", p=EP)).then_inc(s["loaded"], 16)
            sp.dma_start(emb_sb[:], node_emb).then_inc(s["emb_loaded"], 16)
            for r in range(RELS):
                sp.dma_start(type_i[r:r + 1, :], node_type.rearrange("(a n) -> a n", a=1)).then_inc(s["emb_loaded"], 16)
            sp.wait_ge(s["total_made"], 2)
            sp.dma_start(k.total_dram, total[:].rearrange("p t n -> p (t n)")).then_inc(s["saved"], 16)
            sp.wait_ge(s["saved"], 16)

        @block.gpsimd
        def _(pool):
            k.clear_last(pool)
            pool.iota(iota_i[:], [[1, SW]], base=0, channel_multiplier=0).then_inc(s["iota_made"], 1)
            pool.iota(own[:], [[0, 1]], base=0, channel_multiplier=1,
                      allow_small_or_imprecise_dtypes=True).then_inc(s["own_made"], 1)

        @block.vector
        def _(dve):
            link = Link(dve, s["chain"])
            dve.memset(ones_f[:], 1.0).then_inc(s["ones_made"], 1)
            link(dve.memset(onehot[:], 0.0))
            dve.wait_ge(s["iota_made"], 1)
            dve.tensor_copy(iota[:], iota_i[:])
            dve.wait_ge(s["loaded"], 48)
            link(dve.tensor_copy(edges_f[:], edges_i[:]))
            for r in range(RELS):
                link(dve.tensor_scalar(of_rel[:, r, :], edges_f[:, 2, :], float(r), None, ALU.is_equal))

            by_slot = edges_f[:].rearrange("e f (g u) -> e f u g", u=UNROLL)
            rel_by_slot = of_rel[:].rearrange("e r (g u) -> e r u g", u=UNROLL)

            def one_hots(r, g, u, seq, wait):
                if wait:
                    dve.wait_ge(s["tile_mm"], seq - UNROLL + 1)
                dve.tensor_scalar(src_hot[:, u, :], iota[0:EP, :], by_slot[:, 0, u, bass.ds(g, 1)], None, ALU.is_equal)
                dve.tensor_scalar(dst_hot[:, u, :], iota[0:EP, 0:NT], by_slot[:, 1, u, bass.ds(g, 1)],
                                  rel_by_slot[:, r, u, bass.ds(g, 1)], ALU.is_equal, ALU.mult).then_inc(s["hot"], 1)

            for r in range(RELS):
                for u in range(UNROLL):
                    one_hots(r, 0, u, r * ET + u, r > 0)
                with dve.Fori(1, ET // UNROLL) as g:
                    for u in range(UNROLL):
                        one_hots(r, g, u, g * UNROLL + (r * ET + u), True)
            for r in range(RELS):
                dve.wait_ge(s["sum_mm"], r + 1)
                sums = k.pair[r][:, :, 0:HN]
                link(dve.tensor_scalar(halves(pos[:]), sums, 0.0, None, ALU.is_gt))
                link(dve.tensor_scalar(halves(cnt[:]), sums, 1.0, None, ALU.max))
                link(dve.reciprocal(cnt[:], cnt[:]))
                link(dve.tensor_tensor(k.inv[:, r, :], cnt[:], pos[:], ALU.mult))
            dve.tensor_tensor(total[:], k.C[:, 0, :, :].bitcast(F32), k.C[:, 1, :, :].bitcast(F32), ALU.add).then_inc(s["total_made"], 1)
            dve.wait_ge(s["total_made"], 1)
            dve.tensor_tensor(total[:], total[:], k.C[:, 2, :, :].bitcast(F32), ALU.add).then_inc(s["total_made"], 1)
            dve.wait_ge(s["emb_loaded"], 64)
            link(dve.tensor_copy(type_f[:], type_i[:]))
            dve.wait_ge(s["own_made"], 1)
            dve.tensor_scalar(onehot[:, 0:NODES], type_f[:], own[:, 0:1], None, ALU.is_equal).then_inc(s["emb_made"], 1)
            dve.wait_ge(s["emb_hi"], 1)
            dve.tensor_tensor(halves(k.et[:, 0, 1, :]), k.pair[3][:, :, 0:HN], halves(k.et[:, 0, 0, :].bitcast(F32)),
                              ALU.subtract)

        @block.scalar
        def _(act):
            act.wait_ge(s["ones_made"], 1)
            act.activation(ones[:], ones_f[:], ACT.Copy).then_inc(s["ones_made"], 1)
            for r in range(RELS):
                act.wait_ge(s["tile_mm"], ET * (r + 1))
                for t in range(TT):
                    act.activation(k.C[:, r, t, :], flat[:, t * NT:(t + 1) * NT], ACT.Copy).then_inc(s["copied"], 1)
            act.wait_ge(s["emb_ready"], 1)
            act.activation(halves(k.et[:, 0, 0, :]), k.pair[3][:, :, 0:HN], ACT.Copy).then_inc(s["emb_hi"], 1)

        @block.tensor
        def _(pe):
            def count(u, seq, first, last):
                pe.wait_ge(s["hot"], seq + 1)
                for t, c0, c1, opens in pieces:
                    mm = pe.matmul(flat[:, c0:c1], src_hot[:, u, t * P:(t + 1) * P],
                                   dst_hot[:, u, c0 - t * NT:c1 - t * NT], start=(first and opens), stop=last,
                                   skip_group_check=True)
                return mm

            for r in range(RELS):
                if r > 0:
                    pe.wait_ge(s["copied"], TT * r)
                for u in range(UNROLL):
                    count(u, r * ET + u, u == 0, False).then_inc(s["tile_mm"], 1)
                with pe.Fori(1, ET // UNROLL - 1) as g:
                    for u in range(UNROLL):
                        count(u, g * UNROLL + (r * ET + u), False, False).then_inc(s["tile_mm"], 1)
                for u in range(UNROLL):
                    count(u, r * ET + ET - UNROLL + u, False, u == UNROLL - 1).then_inc(s["tile_mm"], 1)
            pe.wait_ge(s["copied"], TT * RELS)
            pe.wait_ge(s["ones_made"], 2)
            for r in range(RELS):
                for t in range(TT):
                    for h in range(2):
                        mm = pe.matmul(k.pair[r][:, h, 0:HN], ones[:], k.C[:, r, t, h * HN:(h + 1) * HN],
                                       start=(t == 0), stop=(t == TT - 1))
                mm.then_inc(s["sum_mm"], 1)
            pe.wait_ge(s["emb_made"], 1)
            for h in range(2):
                mm = pe.matmul(k.pair[3][:, h, 0:HN], emb_sb[:], onehot[:, h * HN:(h + 1) * HN], start=True, stop=True)
            mm.then_inc(s["emb_ready"], 1)



def phase_rgcn(k, name, h_in, h_out, w_rel, w_root, bias):
    d_in, d_out = w_root.shape
    kt, mt = d_in // P, d_out // P
    cuts = [(c, min(256, d_out - c)) for c in range(0, d_out, 256)]
    chunks = [(kt, w, [(0, w, weight_view(m)[:, :, c:c + w])])
              for c, w in cuts for m in (w_rel[0], w_rel[1], w_rel[2], w_root)]
    with ExitStack() as ctx:
        k.begin(ctx)
        st = Stream(k, f"{name}_w", chunks, kt * 256, 2, 2)
        y = k.sb(f"{name}_y", [P, 2, TT, 2, 256], F32R)
        room = k.a[:].rearrange("p t d -> p (t d)")
        acc = room[:, RELS * NT:(RELS + 2) * NT].rearrange("p (m n) -> p m n", m=2)
        part = room[:, (RELS + 2) * NT:(RELS + 3) * NT]
        b = k.sb(f"{name}_b", [P, mt], F32)
        s = signals(k, name, (
            "small", "chain", "y_mm", "y_hi", "y_lo", "g_mm", "g_read", "h_f", "h_hi", "h_lo"))
        jobs = [(kind, c, r) for c in range(len(cuts))
                for kind, r in (("Y", 0), ("Y", 1), ("G", 0), ("Y", 2), ("G", 1), ("R", 3), ("G", 2))]
        y_at = {(c, r): RELS * c + r for c in range(len(cuts)) for r in range(RELS)}
        g_at, g_count = {}, 0
        for kind, c, r in jobs:
            if kind != "Y":
                g_at[c, r] = g_count
                g_count += cuts[c][1] // P
        for c in range(len(cuts)):
            for r in range(RELS):
                st.freed[4 * c + r] = (s["y_mm"], TT * (y_at[c, r] + 1))
            st.freed[4 * c + 3] = (s["g_mm"], g_at[c, 3] + cuts[c][1] // P)
        block = ctx.enter_context(k.nc.Block())

        @block.sync
        def _(sp):
            sp.dma_start(b[:], bias.rearrange("(m p) -> p m", p=P), allow_slow_non_contiguous=True).then_inc(s["small"], 16)
            stream_loads(sp, st)

        @block.gpsimd
        def _(pool):
            k.clear_last(pool)
            stream_splits(pool, st)

        @block.tensor
        def _(pe):
            for kind, c, r in jobs:
                w = cuts[c][1]
                if kind == "Y":
                    pe.wait_ge(st.lo_done, 4 * c + r + 1)
                    wh = st.views(4 * c + r)
                    for t in range(TT):
                        i = TT * y_at[c, r] + t
                        if i >= 3:
                            pe.wait_ge(s["y_lo"], i - 2)
                        for j in range(kt):
                            mm = split_product(pe, k.banks[i % 3][0:TS[t], 0:w],
                                               [h_in(j)[:, a, t * P:t * P + TS[t]] for a in range(2)],
                                               [v[:, j, :] for v in wh], j == 0, j == kt - 1)
                        mm.then_inc(s["y_mm"], 1)
                    continue
                for m in range(w // P):
                    i = g_at[c, r] + m
                    pair = k.pair[2 + i % 2]
                    if i >= 2:
                        pe.wait_ge(s["g_read"], i - 1)
                    if kind == "G":
                        v = y_at[c, r]
                        pe.wait_ge(s["y_lo"], TT * (v + 1))
                        for t in range(TT):
                            for a in range(2):
                                for h in range(2):
                                    mm = pe.matmul(pair[:, h, 0:HN], y[0:TS[t], v % 2, t, a, m * P:(m + 1) * P],
                                                   k.C[0:TS[t], r, t, h * HN:(h + 1) * HN],
                                                   start=(t == 0 and a == 0), stop=(t == TT - 1 and a == 1))
                    else:
                        pe.wait_ge(st.lo_done, 4 * c + 4)
                        wh = st.views(4 * c + 3)
                        for j in range(kt):
                            mm = split_product_wide(pe, pair, [v[:, j, m * P:(m + 1) * P] for v in wh],
                                                    lambda b_, h: h_in(j)[:, b_, h * HN:(h + 1) * HN], j == 0, j == kt - 1)
                    mm.then_inc(s["g_mm"], 1)

        @block.scalar
        def _(act):
            for kind, c, r in jobs:
                w = cuts[c][1]
                if kind == "Y":
                    v = y_at[c, r]
                    if v >= 2:
                        pc, pr = divmod(v - 2, RELS)
                        act.wait_ge(s["g_mm"], g_at[pc, pr] + cuts[pc][1] // P)
                    for t in range(TT):
                        i = TT * v + t
                        act.wait_ge(s["y_mm"], i + 1)
                        act.activation(y[0:TS[t], v % 2, t, 0, 0:w], k.banks[i % 3][0:TS[t], 0:w], ACT.Copy).then_inc(s["y_hi"], 1)
                elif kind == "G" and r == 2:
                    for m in range(w // P):
                        i = 2 * c + m
                        act.wait_ge(s["h_f"], i + 1)
                        act.activation(h_out(i)[:, 0, :], acc[:, m, :], ACT.Copy).then_inc(s["h_hi"], 1)

        @block.vector
        def _(dve):
            link = Link(dve, s["chain"])
            dve.wait_ge(s["small"], 16)
            for kind, c, r in jobs:
                w = cuts[c][1]
                if kind == "Y":
                    v = y_at[c, r]
                    for t in range(TT):
                        i = TT * v + t
                        dve.wait_ge(s["y_hi"], i + 1)
                        dve.tensor_tensor(y[0:TS[t], v % 2, t, 1, 0:w], k.banks[i % 3][0:TS[t], 0:w],
                                          y[0:TS[t], v % 2, t, 0, 0:w].bitcast(F32), ALU.subtract).then_inc(s["y_lo"], 1)
                    continue
                for m in range(w // P):
                    i = g_at[c, r] + m
                    src = k.pair[2 + i % 2][:, :, 0:HN]
                    sum_ = acc[:, m, :]
                    dve.wait_ge(s["g_mm"], i + 1)
                    if kind == "G" and r == 0:
                        if c > 0:
                            dve.wait_ge(s["h_lo"], 2 * (c - 1) + m + 1)
                        dve.tensor_tensor(halves(sum_), src, halves(k.inv[:, r, :]), ALU.mult).then_inc(s["g_read"], 1)
                        dve.wait_ge(s["g_read"], i + 1)
                    elif kind == "G":
                        dve.tensor_tensor(halves(part), src, halves(k.inv[:, r, :]), ALU.mult).then_inc(s["g_read"], 1)
                        dve.wait_ge(s["g_read"], i + 1)
                        link(dve.tensor_tensor(sum_, sum_, part, ALU.add))
                    else:
                        dve.scalar_tensor_tensor(halves(sum_), src, b[:, 2 * c + m:2 * c + m + 1], halves(sum_),
                                                 ALU.add, ALU.add).then_inc(s["g_read"], 1)
                        dve.wait_ge(s["g_read"], i + 1)
                    if kind == "G" and r == 2:
                        dve.tensor_scalar(sum_, sum_, 0.0, None, ALU.max).then_inc(s["h_f"], 1)
                        if m == w // P - 1:
                            for m2 in range(w // P):
                                o = 2 * c + m2
                                dve.wait_ge(s["h_hi"], o + 1)
                                dve.tensor_tensor(h_out(o)[:, 1, :], acc[:, m2, :], h_out(o)[:, 0, :].bitcast(F32),
                                                  ALU.subtract).then_inc(s["h_lo"], 1)


def phase_add_turned(k, name, h):
    with ExitStack() as ctx:
        k.begin(ctx)
        whole = k.sb(f"{name}_whole", [P, 2, NT], F32)
        s = signals(k, name, ("whole", "turned", "added"))
        block = ctx.enter_context(k.nc.Block())

        @block.gpsimd
        def _(pool):
            k.clear_last(pool)

        @block.vector
        def _(dve):
            def add(j):
                dve.wait_ge(s["turned"], j + 1)
                for t in range(TT):
                    x = k.x[0:TS[t], t, j * P:(j + 1) * P]
                    src = k.banks[2 * (j % 2) + t // 4][0:TS[t], (t % 4) * P:(t % 4 + 1) * P]
                    ins = dve.tensor_tensor(x, src, x, ALU.add)
                ins.then_inc(s["added"], 1)

            for j in range(KD):
                if j >= 2:
                    dve.wait_ge(s["turned"], j - 1)
                dve.tensor_tensor(whole[:, j % 2, :], h(j)[:, 0, :].bitcast(F32), h(j)[:, 1, :].bitcast(F32),
                                  ALU.add).then_inc(s["whole"], 1)
                if j >= 1:
                    add(j - 1)
            add(KD - 1)

        @block.tensor
        def _(pe):
            for j in range(KD):
                pe.wait_ge(s["whole"], j + 1)
                if j >= 2:
                    pe.wait_ge(s["added"], j - 1)
                for t in range(TT):
                    mm = pe.transpose(k.banks[2 * (j % 2) + t // 4][0:TS[t], (t % 4) * P:(t % 4 + 1) * P],
                                      whole[:, j % 2, t * P:t * P + TS[t]], k.ident[:])
                mm.then_inc(s["turned"], 1)


def phase_save(k, name):
    with ExitStack() as ctx:
        k.begin(ctx)
        saved = k.sem(f"{name}_saved")
        k.x_dram = k.nc.dram_tensor("x_dram", (NODES, D), F32).ap()
        block = ctx.enter_context(k.nc.Block())

        @block.gpsimd
        def _(pool):
            k.clear_last(pool)

        @block.sync
        def _(sp):
            for t in range(TT):
                sp.dma_start(k.x_dram[t * P:t * P + TS[t], :], k.x[0:TS[t], t, :]).then_inc(saved, 16)
            sp.wait_ge(saved, 16 * TT)


def gnn_block(k, I):
    with ExitStack() as ctx:
        k.enter(ctx)
        k.et = k.sb("et_sb", [P, 1, 2, NT], F32R)
        k.C = k.sb("counts", [P, RELS, TT, NT], F32R)
        k.inv = k.a[:].rearrange("p t d -> p (t d)")[:, 0:RELS * NT].rearrange("p (r n) -> p r n", r=RELS)
        k.total_dram = k.nc.dram_tensor("count_total_dram", (P, TT * NT), F32).ap()
        phase_counts(k, I["src"], I["dst"], I["edge_type_3"], I["L0_gnn_node_emb"], I["node_type_3"])
        k.enter(ctx)
        hb = k.sb("h_b", [P, K1, 2, NT], F32R)
        first = lambda j: k.xt[:, j, :, :] if j < KD else k.et[:, 0, :, :]
        second = lambda j: hb[:, j, :, :]
        phase_rgcn(k, "g1", first, second, I["L0_gnn_w_rel1"], I["L0_gnn_w_root1"], I["L0_gnn_b1"])
        phase_rgcn(k, "g2", second, first, I["L0_gnn_w_rel2"], I["L0_gnn_w_root2"], I["L0_gnn_b2"])
        phase_rgcn(k, "g3", first, second, I["L0_gnn_w_rel3"], I["L0_gnn_w_root3"], I["L0_gnn_b3"])
        phase_add_turned(k, "g4", second)



EMBEDS = (384, 576, 768)
RATIOS = (2, 3, 4)
assert all(r * e >= H_FF for r in RATIOS for e in EMBEDS)
GELU_C = float(np.sqrt(2.0 / np.pi))


def phase_ffn(k, name, w_fc, b_fc, w_proj, b_proj, alpha_e, alpha_r):
    with ExitStack() as ctx:
        k.begin(ctx)
        al = k.sb(f"{name}_al", [P, 6], F32)
        sum_r = k.sb(f"{name}_sum_r", [P, 1], F32)
        coef = k.sb(f"{name}_coef", [P, 3], F32)
        fc = k.sb(f"{name}_fc", [HP, 2, D], F32)
        pr = k.sb(f"{name}_pr", [P, KD, H_FF], F32)
        w0f = k.sb(f"{name}_w0f", [P, KD, H_FF], F32)
        w0 = k.sb(f"{name}_w0", [P, 2, KD, H_FF], F32R)
        w1f = k.sb(f"{name}_w1f", [HP, 2, D], F32)
        w1 = k.sb(f"{name}_w1", [HP, 2, 2, D], F32R)
        bf = k.sb(f"{name}_bf", [HP, 2], F32)
        bp = k.sb(f"{name}_bp", [P, D], F32)
        hf = k.sb(f"{name}_hf", [HP, 2, NT], F32)
        g1 = k.sb(f"{name}_g1", [HP, 2, NT], F32)
        g2 = k.sb(f"{name}_g2", [HP, 2, NT], F32)
        h = k.sb(f"{name}_h", [HP, 2, 2, NT], F32R)
        s = signals(k, name, (
            "loaded", "chain", "scaled", "turned", "w_f", "w_hi", "w_lo", "h_mm", "g_in", "g_tanh", "h_f", "h_hi",
            "h_lo", "o_mm", "o_read"))
        block = ctx.enter_context(k.nc.Block())

        @block.gpsimd
        def _(pool):
            k.clear_last(pool)
        fc_t = k.psum[:, 0:3, :]
        pr_t = [k.psum[0:HP, 3 + 2 * g:5 + 2 * g, 0:384] for g in range(2)]

        @block.sync
        def _(sp):
            sp.dma_start(al[:, 0:3], alpha_e.partition_broadcast(P)).then_inc(s["loaded"], 16)
            sp.dma_start(al[:, 3:6], alpha_r.partition_broadcast(P)).then_inc(s["loaded"], 16)
            sp.dma_start(fc[:], w_fc.rearrange("(g p) d -> p g d", p=HP)).then_inc(s["loaded"], 16)
            sp.dma_start(pr[:], w_proj.rearrange("(k p) h -> p k h", p=P)).then_inc(s["loaded"], 16)
            sp.dma_start(bf[:], b_fc.rearrange("(g p) -> p g", p=HP), allow_slow_non_contiguous=True).then_inc(s["loaded"], 16)
            sp.dma_start(bp[:], b_proj.partition_broadcast(P)).then_inc(s["loaded"], 16)

        @block.vector
        def _(dve):
            link = Link(dve, s["chain"])
            spans = ((0, EMBEDS[0]), (EMBEDS[0], EMBEDS[1]), (EMBEDS[1], EMBEDS[2]))
            dve.wait_ge(s["loaded"], 16 * 6)
            link(dve.tensor_reduce(sum_r[:], al[:, 3:6], AX.X, ALU.add))
            link(dve.tensor_scalar(coef[:], al[:, 0:3], sum_r[:, 0:1], None, ALU.mult))
            link(dve.tensor_tensor(coef[:, 1:2], coef[:, 1:2], coef[:, 2:3], ALU.add))
            link(dve.tensor_tensor(coef[:, 0:1], coef[:, 0:1], coef[:, 1:2], ALU.add))
            for i, (c0, c1) in enumerate(spans):
                dve.tensor_scalar(bp[:, c0:c1], bp[:, c0:c1], coef[:, i:i + 1], None, ALU.mult)
                ins = dve.tensor_scalar(fc[:, :, c0:c1], fc[:, :, c0:c1], coef[0:HP, i:i + 1], None, ALU.mult)
            link(ins)
            link(dve.tensor_scalar(bf[:], bf[:], coef[0:HP, 0:1], None, ALU.mult))
            ins = dve.tensor_copy(g1[:, 0, 0:1], coef[0:HP, 0:1])
            ins.then_inc(s["scaled"], 1)
            for t in range(TT):
                ins = dve.tensor_tensor(k.x[0:TS[t], t, :], k.x[0:TS[t], t, :], bp[0:TS[t], :], ALU.add)
            link(ins)
            dve.wait_ge(s["turned"], 1)
            for j in range(3):
                dve.tensor_copy(w0f[:, 2 * j:2 * j + 2, :].rearrange("p k h -> p (k h)"), fc_t[:, j, 0:2 * H_FF])
            for g in range(2):
                w = w1f[:, g, :]
                link(dve.tensor_copy(w.rearrange("p (b n) -> p b n", b=2), pr_t[g]))
                for i, (c0, c1) in enumerate(spans):
                    ins = dve.tensor_scalar(w[:, c0:c1], w[:, c0:c1], coef[0:HP, i:i + 1], None, ALU.mult)
            ins.then_inc(s["w_f"], 1)
            dve.wait_ge(s["w_hi"], 2)
            dve.tensor_tensor(w0[:, 1, :, :], w0f[:], w0[:, 0, :, :].bitcast(F32), ALU.subtract).then_inc(s["w_lo"], 1)
            dve.tensor_tensor(w1[:, 1, :, :], w1f[:], w1[:, 0, :, :].bitcast(F32), ALU.subtract).then_inc(s["w_lo"], 1)
            for g in range(2):
                dve.wait_ge(s["h_mm"], g + 1)
                link(dve.tensor_scalar(halves(hf[:, g, :]), k.pair[g][0:HP, :, 0:HN], bf[:, g:g + 1], None, ALU.add))
                link(dve.tensor_tensor(g1[:, g, :], hf[:, g, :], hf[:, g, :], ALU.mult))
                link(dve.tensor_scalar(g1[:, g, :], g1[:, g, :], 0.044715, 1.0, ALU.mult, ALU.add))
                dve.tensor_tensor(g1[:, g, :], g1[:, g, :], hf[:, g, :], ALU.mult).then_inc(s["g_in"], 1)
            for g in range(2):
                dve.wait_ge(s["g_tanh"], g + 1)
                link(dve.tensor_scalar(g2[:, g, :], g2[:, g, :], 0.5, 0.5, ALU.mult, ALU.add))
                dve.tensor_tensor(hf[:, g, :], hf[:, g, :], g2[:, g, :], ALU.mult).then_inc(s["h_f"], 1)
            for g in range(2):
                dve.wait_ge(s["h_hi"], g + 1)
                dve.tensor_tensor(h[:, g, 1, :], hf[:, g, :], h[:, g, 0, :].bitcast(F32), ALU.subtract).then_inc(s["h_lo"], 1)
            for i in range(2 * TT):
                t, c = divmod(i, 2)
                x = k.x[0:TS[t], t, c * 384:(c + 1) * 384]
                dve.wait_ge(s["o_mm"], i + 1)
                dve.tensor_tensor(x, k.banks[4 + i % 2][0:TS[t], 0:384], x, ALU.add).then_inc(s["o_read"], 1)

        @block.scalar
        def _(act):
            act.wait_ge(s["w_f"], 1)
            act.activation(w0[:, 0, :, :], w0f[:], ACT.Copy).then_inc(s["w_hi"], 1)
            act.activation(w1[:, 0, :, :], w1f[:], ACT.Copy).then_inc(s["w_hi"], 1)
            for g in range(2):
                act.wait_ge(s["g_in"], g + 1)
                act.activation(g2[:, g, :], g1[:, g, :], ACT.Tanh, scale=GELU_C).then_inc(s["g_tanh"], 1)
            for g in range(2):
                act.wait_ge(s["h_f"], g + 1)
                act.activation(h[:, g, 0, :], hf[:, g, :], ACT.Copy).then_inc(s["h_hi"], 1)

        @block.tensor
        def _(pe):
            pe.wait_ge(s["scaled"], 1)
            for j in range(KD):
                for g in range(2):
                    c0 = (j % 2) * H_FF + g * HP
                    pe.transpose(fc_t[:, j // 2, c0:c0 + HP], fc[:, g, j * P:(j + 1) * P], k.ident[0:HP, 0:HP])
            for g in range(2):
                for j in range(KD):
                    mm = pe.transpose(pr_t[g][:, j // 3, (j % 3) * P:(j % 3 + 1) * P], pr[:, j, g * HP:(g + 1) * HP],
                                      k.ident[:])
            mm.then_inc(s["turned"], 1)
            pe.wait_ge(s["w_lo"], 2)
            for g in range(2):
                for j in range(KD):
                    mm = split_product_wide(pe, k.pair[g][0:HP], [w0[:, a, j, g * HP:(g + 1) * HP] for a in range(2)],
                                            lambda b, hh: k.xt[:, j, b, hh * HN:(hh + 1) * HN], j == 0, j == KD - 1)
                mm.then_inc(s["h_mm"], 1)
            pe.wait_ge(s["h_lo"], 2)
            for i in range(2 * TT):
                t, c = divmod(i, 2)
                if i >= 2:
                    pe.wait_ge(s["o_read"], i - 1)
                for g in range(2):
                    mm = split_product(pe, k.banks[4 + i % 2][0:TS[t], 0:384],
                                       [h[:, g, a, t * P:t * P + TS[t]] for a in range(2)],
                                       [w1[:, a, g, c * 384:(c + 1) * 384] for a in range(2)], g == 0, g == 1)
                mm.then_inc(s["o_mm"], 1)



def phase_gcn(k, name, w, bias):
    chunks = [one_chunk(w, 256, c * 256) for c in range(3)]
    with ExitStack() as ctx:
        k.begin(ctx)
        st = Stream(k, f"{name}_w", chunks, WE_MIX, 2, 3)
        total = k.sb(f"{name}_total", [P, TT, NT], F32)
        adj = k.sb(f"{name}_adj", [P, TT, NT], F32R)
        ones = k.sb(f"{name}_ones", [P, 2], F32)
        y = k.sb(f"{name}_y", [P, TT, 2, D], F32R)
        yf = k.sb(f"{name}_yf", [P, 2, 256], F32)
        bp = k.sb(f"{name}_bp", [P, D], F32)
        s = signals(k, name, (
            "loaded", "chain", "ones_made", "deg_mm", "var_ready", "root_ready", "looped", "adj_made", "y_mm", "y_f",
            "y_hi", "y_lo", "o_mm", "o_read"))
        st.freed.update({c: (s["y_mm"], TT * (c + 1)) for c in range(3)})
        block = ctx.enter_context(k.nc.Block())

        @block.sync
        def _(sp):
            sp.dma_start(total[:].rearrange("p t n -> p (t n)"), k.total_dram).then_inc(s["loaded"], 16)
            sp.dma_start(bp[:], bias.partition_broadcast(P)).then_inc(s["loaded"], 16)
            stream_loads(sp, st)

        @block.gpsimd
        def _(pool):
            k.clear_last(pool)
            stream_splits(pool, st)

        @block.vector
        def _(dve):
            link = Link(dve, s["chain"])
            link(dve.memset(ones[:], 1.0))
            dve.wait_ge(s["loaded"], 32)
            for t in range(TT):
                ts = TS[t]
                ins = dve.tensor_tensor(total[0:ts, t, t * P:t * P + ts], total[0:ts, t, t * P:t * P + ts],
                                        k.ident[0:ts, 0:ts], ALU.add)
            ins.then_inc(s["looped"], 1)
            for t in range(TT):
                ins = dve.tensor_tensor(k.x[0:TS[t], t, :], k.x[0:TS[t], t, :], bp[0:TS[t], :], ALU.add)
            link(ins)
            dve.wait_ge(s["deg_mm"], 1)
            link(dve.memset(k.ve[:], 1.0))
            for t in range(TT):
                ins = dve.tensor_copy(k.ve[0:TS[t], t:t + 1], k.banks[7][0:TS[t], 2 * t:2 * t + 1])
            link(ins)
            rsqrt_of_ve(dve, link, k, s)

            def y_low(i):
                c, t = divmod(i, TT)
                dve.wait_ge(s["y_hi"], i + 1)
                dve.tensor_tensor(y[0:TS[t], t, 1, c * 256:(c + 1) * 256], yf[0:TS[t], i % 2, :],
                                  y[0:TS[t], t, 0, c * 256:(c + 1) * 256].bitcast(F32), ALU.subtract).then_inc(s["y_lo"], 1)

            for i in range(3 * TT):
                c, t = divmod(i, TT)
                dve.wait_ge(s["y_mm"], i + 1)
                if i >= 2:
                    dve.wait_ge(s["y_lo"], i - 1)
                dve.tensor_scalar(yf[0:TS[t], i % 2, :], k.banks[i % 2][0:TS[t], 0:256], k.rstd[0:TS[t], t:t + 1], None,
                                  ALU.mult).then_inc(s["y_f"], 1)
                if i >= 1:
                    y_low(i - 1)
            y_low(3 * TT - 1)
            for i in range(2 * TT):
                t, c = divmod(i, 2)
                x = k.x[0:TS[t], t, c * 384:(c + 1) * 384]
                dve.wait_ge(s["o_mm"], i + 1)
                dve.scalar_tensor_tensor(x, k.banks[2 + i % 2][0:TS[t], 0:384], k.rstd[0:TS[t], t:t + 1], x,
                                         ALU.mult, ALU.add).then_inc(s["o_read"], 1)

        @block.scalar
        def _(act):
            act.wait_ge(s["looped"], 1)
            act.activation(adj[:], total[:], ACT.Copy).then_inc(s["adj_made"], 1)
            act.wait_ge(s["var_ready"], 1)
            act.activation(k.root[:], k.ve[:], ACT.Sqrt).then_inc(s["root_ready"], 1)
            for i in range(3 * TT):
                c, t = divmod(i, TT)
                act.wait_ge(s["y_f"], i + 1)
                act.activation(y[0:TS[t], t, 0, c * 256:(c + 1) * 256], yf[0:TS[t], i % 2, :], ACT.Copy).then_inc(s["y_hi"], 1)

        @block.tensor
        def _(pe):
            pe.wait_ge(s["looped"], 1)
            for t in range(TT):
                for u in range(TT):
                    mm = pe.matmul(k.banks[7][0:TS[t], 2 * t:2 * t + 2], total[0:TS[u], u, t * P:t * P + TS[t]],
                                   ones[0:TS[u], :], start=(u == 0), stop=(u == TT - 1))
            mm.then_inc(s["deg_mm"], 1)
            for c in range(3):
                pe.wait_ge(st.lo_done, c + 1)
                wh = st.views(c)
                for t in range(TT):
                    i = c * TT + t
                    if i >= 2:
                        pe.wait_ge(s["y_f"], i - 1)
                    for j in range(KD):
                        mm = split_product(pe, k.banks[i % 2][0:TS[t], 0:256],
                                           [k.xt[:, j, a, t * P:t * P + TS[t]] for a in range(2)],
                                           [v[:, j, :] for v in wh], j == 0, j == KD - 1)
                    mm.then_inc(s["y_mm"], 1)
            pe.wait_ge(s["adj_made"], 1)
            pe.wait_ge(s["y_lo"], 3 * TT)
            for i in range(2 * TT):
                t, c = divmod(i, 2)
                if i >= 2:
                    pe.wait_ge(s["o_read"], i - 1)
                for u in range(TT):
                    for a in range(2):
                        mm = pe.matmul(k.banks[2 + i % 2][0:TS[t], 0:384], adj[0:TS[u], u, t * P:t * P + TS[t]],
                                       y[0:TS[u], u, a, c * 384:(c + 1) * 384],
                                       start=(u == 0 and a == 0), stop=(u == TT - 1 and a == 1))
                mm.then_inc(s["o_mm"], 1)



def phase_router(k, name, w_router, bias):
    with ExitStack() as ctx:
        k.begin(ctx)
        wf = k.sb(f"{name}_wf", [P, KD, EXPERTS], F32)
        w = k.sb(f"{name}_w", [P, 2, KD, EXPERTS], F32R)
        b = k.sb(f"{name}_b", [P, EXPERTS], F32)
        logits = k.sb(f"{name}_logits", [P, TT, EXPERTS], F32)
        top = k.sb(f"{name}_top", [P, TT, 8], F32)
        at_i = k.sb(f"{name}_at_i", [P, TT, 8], U32)
        at_f = k.sb(f"{name}_at_f", [P, TT, 8], F32)
        iota_i = k.sb(f"{name}_iota_i", [P, EXPERTS], I32)
        iota = k.sb(f"{name}_iota", [P, EXPERTS], F32)
        hot = k.sb(f"{name}_hot", [P, TT, 2, EXPERTS], F32)
        gap = k.sb(f"{name}_gap", [P, TT], F32)
        ex = k.sb(f"{name}_ex", [P, TT], F32)
        den = k.sb(f"{name}_den", [P, TT], F32)
        wt = k.sb(f"{name}_wt", [P, 2, TT], F32)
        s = signals(k, name, (
            "loaded", "chain", "iota_made", "w_hi", "w_lo", "mm", "gap_made", "ex_made"))
        block = ctx.enter_context(k.nc.Block())

        @block.sync
        def _(sp):
            sp.dma_start(wf[:], weight_view(w_router)).then_inc(s["loaded"], 16)
            sp.dma_start(b[:], bias.partition_broadcast(P)).then_inc(s["loaded"], 16)

        @block.gpsimd
        def _(pool):
            k.clear_last(pool)
            pool.iota(iota_i[:], [[1, EXPERTS]], base=0, channel_multiplier=0).then_inc(s["iota_made"], 1)

        @block.scalar
        def _(act):
            act.wait_ge(s["loaded"], 32)
            act.activation(w[:, 0, :, :], wf[:], ACT.Copy).then_inc(s["w_hi"], 1)
            act.wait_ge(s["gap_made"], 1)
            act.activation(ex[:], gap[:], ACT.Exp).then_inc(s["ex_made"], 1)

        @block.tensor
        def _(pe):
            pe.wait_ge(s["w_lo"], 1)
            for t in range(TT):
                for j in range(KD):
                    mm = split_product(pe, k.banks[0][0:TS[t], t * EXPERTS:(t + 1) * EXPERTS],
                                       [k.xt[:, j, a, t * P:t * P + TS[t]] for a in range(2)],
                                       [w[:, a, j, :] for a in range(2)], j == 0, j == KD - 1)
            mm.then_inc(s["mm"], 1)

        @block.vector
        def _(dve):
            link = Link(dve, s["chain"])
            dve.memset(logits[:], 0.0)
            dve.wait_ge(s["iota_made"], 1)
            link(dve.tensor_copy(iota[:], iota_i[:]))
            dve.wait_ge(s["w_hi"], 1)
            dve.tensor_tensor(w[:, 1, :, :], wf[:], w[:, 0, :, :].bitcast(F32), ALU.subtract).then_inc(s["w_lo"], 1)
            dve.wait_ge(s["mm"], 1)
            for t in range(TT):
                ts = TS[t]
                link(dve.tensor_tensor(logits[0:ts, t, :], k.banks[0][0:ts, t * EXPERTS:(t + 1) * EXPERTS], b[0:ts, :],
                                       ALU.add))
            for t in range(TT):
                link(dve.max(top[:, t, :], logits[:, t, :]))
                link(dve.max_index(at_i[:, t, :], top[:, t, :], logits[:, t, :]))
            link(dve.tensor_copy(at_f[:], at_i[:]))
            dve.tensor_tensor(gap[:], top[:, :, 1], top[:, :, 0], ALU.subtract).then_inc(s["gap_made"], 1)
            dve.wait_ge(s["ex_made"], 1)
            link(dve.tensor_scalar(den[:], ex[:], 1.0, None, ALU.add))
            link(dve.reciprocal(wt[:, 0, :], den[:]))
            link(dve.tensor_tensor(wt[:, 1, :], ex[:], wt[:, 0, :], ALU.mult))
            for t in range(TT):
                for r in range(2):
                    ins = dve.tensor_scalar(hot[:, t, r, :], iota[:], at_f[:, t, r:r + 1], wt[:, r, t:t + 1],
                                            ALU.is_equal, ALU.mult)
                link(ins)
                dve.tensor_tensor(k.combine[:, t, :], hot[:, t, 0, :], hot[:, t, 1, :], ALU.add)



GC = 384
FT = D // P


def phase_experts(k, name, shared, routed):
    wg_s, wu_s, wd_s = shared
    wg_r, wu_r, wd_r = routed
    RAW, SPL = 3, 4
    CH = 6
    with ExitStack() as ctx:
        k.begin(ctx)
        raw = k.sb(f"{name}_raw", [P, RAW, WE_MOE], F32)
        whi = k.sb(f"{name}_whi", [P, SPL, WE_MOE], F32R)
        wlo = k.sb(f"{name}_wlo", [P, SPL, WE_MOE], F32R)
        ht = k.sb(f"{name}_ht", [P, FT, 2, NT], F32R)
        act_g = k.sb(f"{name}_act_g", [P, 2, NT], F32)
        hf = k.sb(f"{name}_hf", [P, 2, NT], F32)
        s = signals(k, name, (
            "hi_done", "lo_done", "used", "gu_mm", "silu", "hf", "h_hi", "h_lo", "o_mm", "o_read"))
        loaded = [k.sem(f"{name}_loaded{i}") for i in range(RAW)]
        block = ctx.enter_context(k.nc.Block())

        def sources(wg, wu, wd, half):
            c = half * D
            g, u, d = (weight_view(v) for v in (wg, wu, wd))
            dh = d[:, half * FT:(half + 1) * FT, :]
            return [g[:, :, c:c + GC], u[:, :, c:c + GC], g[:, :, c + GC:c + 2 * GC], u[:, :, c + GC:c + 2 * GC],
                    dh[:, :, 0:GC], dh[:, :, GC:2 * GC]]

        def run(eng, unit):
            for half in range(2):
                unit(None, half, half, half == 0)
            with eng.Fori(0, EXPERTS) as e:
                for half in range(2):
                    unit(e, half, e * 2 + (2 + half), False)

        @block.sync
        def _(sp):
            def unit(e, half, n, first):
                if e is None:
                    src = sources(wg_s[0], wu_s[0], wd_s[0], half)
                else:
                    pick = [v[bass.ds(e, 1)].rearrange("a d f -> (a d) f") for v in (wg_r, wu_r, wd_r)]
                    src = sources(*pick, half)
                for i in range(CH):
                    if not (first and i < RAW):
                        sp.wait_ge(s["lo_done"], n * CH + (i - RAW + 1))
                    slot = (half * CH + i) % RAW
                    sp.dma_start(raw[:, slot, :].rearrange("p (k c) -> p k c", c=GC), src[i]).then_inc(loaded[slot], 16)

            run(sp, unit)

        @block.gpsimd
        def _(pool):
            k.clear_last(pool)
            def unit(e, half, n, first):
                for i in range(CH):
                    slot, spl = i % RAW, (half * CH + i) % SPL
                    pool.wait_ge(loaded[slot], n * (16 * CH // RAW) + 16 * (i // RAW + 1))
                    if not (first and i < SPL):
                        pool.wait_ge(s["used"], n * CH + (i - SPL + 1))
                    pool.tensor_tensor(whi[:, spl, :], raw[:, slot, :], k.one[:].broadcast_to([P, WE_MOE]), ALU.mult)\
                        .then_inc(s["hi_done"], 1)
                    pool.wait_ge(s["hi_done"], n * CH + (i + 1))
                    pool.tensor_tensor(wlo[:, spl, :], raw[:, slot, :], whi[:, spl, :].bitcast(F32),
                                       ALU.subtract).then_inc(s["lo_done"], 1)

            run(pool, unit)

        def banks_of(half, f):
            q = (f + half) % 2
            return k.pair[2 * q], k.pair[2 * q + 1]

        def out_bank(half, i):
            return k.banks[4 * ((FT + half) % 2) + i % 4]

        @block.tensor
        def _(pe):
            def views(half, i):
                spl = (half * CH + i) % SPL
                return [w[:, spl, :].rearrange("p (k c) -> p k c", c=GC) for w in (whi, wlo)]

            def unit(e, half, n, first):
                for c in range(2):
                    for f in range(3 * c, 3 * c + 3):
                        m = f - 3 * c
                        pg, pu = banks_of(half, f)
                        if f >= 2:
                            pe.wait_ge(s["hf"], n * FT + (f - 1))
                        elif not first and f == 0:
                            pe.wait_ge(s["hf"], n * FT)
                        elif not first:
                            pe.wait_ge(s["o_read"], n * (2 * TT))
                        for g, pair in ((0, pg), (1, pu)):
                            if m == 0:
                                pe.wait_ge(s["lo_done"], n * CH + (2 * c + g + 1))
                            wh = views(half, 2 * c + g)
                            for j in range(KD):
                                mm = split_product_wide(pe, pair, [w[:, j, m * P:(m + 1) * P] for w in wh],
                                                        lambda b, h: k.xt[:, j, b, h * HN:(h + 1) * HN],
                                                        j == 0, j == KD - 1)
                            if m == 2:
                                mm.then_inc(s["used"], 1)
                            else:
                                mm.then_inc(s["gu_mm"], 1)
                for c in range(2):
                    pe.wait_ge(s["lo_done"], n * CH + (5 + c))
                    wh = views(half, 4 + c)
                    for t in range(TT):
                        i = c * TT + t
                        if i == 0:
                            pe.wait_ge(s["hf"], n * FT + (FT - 1))
                        if i >= 4:
                            pe.wait_ge(s["o_read"], n * (2 * TT) + (i - 3))
                        for f in range(FT):
                            if i == 0:
                                pe.wait_ge(s["h_lo"], n * FT + (f + 1))
                            mm = split_product(pe, out_bank(half, i)[0:TS[t], 0:GC],
                                               [ht[:, f, a, t * P:t * P + TS[t]] for a in range(2)],
                                               [w[:, f, :] for w in wh], f == 0, f == FT - 1)
                        if t == TT - 1:
                            mm.then_inc(s["used"], 1)
                        else:
                            mm.then_inc(s["o_mm"], 1)

            run(pe, unit)

        def gate_ready(eng, n, f):
            c, m = divmod(f, 3)
            if m == 2:
                eng.wait_ge(s["used"], n * CH + (2 * c + 1))
            else:
                eng.wait_ge(s["gu_mm"], n * 8 + (4 * c + 2 * m + 1))

        def up_ready(eng, n, f):
            c, m = divmod(f, 3)
            if m == 2:
                eng.wait_ge(s["used"], n * CH + (2 * c + 2))
            else:
                eng.wait_ge(s["gu_mm"], n * 8 + (4 * c + 2 * m + 2))

        def out_ready(eng, n, i):
            c, t = divmod(i, TT)
            if t == TT - 1:
                eng.wait_ge(s["used"], n * CH + (5 + c))
            else:
                eng.wait_ge(s["o_mm"], n * (2 * TT - 2) + (c * (TT - 1) + t + 1))

        @block.scalar
        def _(act):
            def unit(e, half, n, first):
                for f in range(FT):
                    gate_ready(act, n, f)
                    if not (first and f < 2):
                        act.wait_ge(s["hf"], n * FT + (f - 1))
                    act.activation(halves(act_g[:, f % 2, :]), banks_of(half, f)[0][:, :, 0:HN], ACT.Silu).then_inc(s["silu"], 1)
                    act.wait_ge(s["hf"], n * FT + (f + 1))
                    if f == 0 and not first:
                        out_ready(act, n - 1 if e is None else n + (-1), 2 * TT - 1)
                    act.activation(ht[:, f, 0, :], hf[:, f % 2, :], ACT.Copy).then_inc(s["h_hi"], 1)

            run(act, unit)

        @block.vector
        def _(dve):
            def unit(e, half, n, first):
                def low(f):
                    dve.wait_ge(s["h_hi"], n * FT + (f + 1))
                    dve.tensor_tensor(ht[:, f, 1, :], hf[:, f % 2, :], ht[:, f, 0, :].bitcast(F32),
                                      ALU.subtract).then_inc(s["h_lo"], 1)

                for f in range(FT):
                    up_ready(dve, n, f)
                    dve.wait_ge(s["silu"], n * FT + (f + 1))
                    if not (first and f < 2):
                        dve.wait_ge(s["h_lo"], n * FT + (f - 1))
                    dve.tensor_tensor(halves(hf[:, f % 2, :]), banks_of(half, f)[1][:, :, 0:HN],
                                      halves(act_g[:, f % 2, :]), ALU.mult).then_inc(s["hf"], 1)
                    low(f)
                for i in range(2 * TT):
                    c, t = divmod(i, TT)
                    ts = TS[t]
                    x = k.x[0:ts, t, c * GC:(c + 1) * GC]
                    out_ready(dve, n, i)
                    if not first:
                        dve.wait_ge(s["o_read"], n * (2 * TT) + (i - 2 * TT + 1))
                    if e is None:
                        dve.tensor_tensor(x, out_bank(half, i)[0:ts, 0:GC], x, ALU.add).then_inc(s["o_read"], 1)
                    else:
                        dve.scalar_tensor_tensor(x, out_bank(half, i)[0:ts, 0:GC], k.combine[0:ts, t, bass.ds(e, 1)], x,
                                                 ALU.mult, ALU.add).then_inc(s["o_read"], 1)

            run(dve, unit)



SEM_SETS = (range(100, 160), range(160, 220))


class Kit:

    def __init__(self, nc, ctx):
        self.nc, self.outer, self.inner = nc, ctx, ctx
        self.phase, self.taken = 0, 0

    def enter(self, ctx):
        self.inner = ctx

    def begin(self, ctx):
        self.inner = ctx
        self.phase += 1
        self.taken = 0

    def sb(self, name, shape, dt):
        return self.inner.enter_context(self.nc.sbuf_tensor(name, shape, dt))

    def sem(self, name):
        num = SEM_SETS[self.phase % 2][self.taken]
        self.taken += 1
        return self.inner.enter_context(self.nc.semaphore(name, num=num))

    def clear_last(self, pool):
        if self.phase > 1:
            pool.sem_clear(SEM_SETS[(self.phase + 1) % 2])


def build(nc, I, out, stop=99):
    with ExitStack() as ctx:
        k = Kit(nc, ctx)
        k.x_in = I["x"]
        psum = ctx.enter_context(nc.psum_tensor("psum", [P, 8, 512], F32))
        k.psum = psum
        k.banks = [psum[:, b, :] for b in range(8)]
        k.pair = [psum[:, 2 * b:2 * b + 2, :] for b in range(4)]
        k.x = k.sb("x_sb", [P, TT, D], F32)
        k.a = k.sb("a_sb", [P, TT, D], F32)
        k.xt = k.sb("xt_sb", [P, KD, 2, NT], F32R)
        k.ident = k.sb("ident", [P, P], F32)
        k.one = k.sb("one", [P, 1], F32)
        k.bn = k.sb("bn", [P, TT, 2, 6], F32)
        k.mv = k.sb("mv", [P, TT, 2], F32)
        k.ve = k.sb("ve", [P, TT], F32)
        k.root = k.sb("root", [P, TT], F32)
        k.rstd = k.sb("rstd", [P, TT], F32)
        k.tmp5 = k.sb("tmp5", [P, TT], F32)
        k.combine = k.sb("combine", [P, TT, EXPERTS], F32)

        def first_norm():
            phase_norm(k, "n0", load_x=True)

        steps = [first_norm,
                 lambda: (phase_attend(k, "m0", False, I["L0_mix_W_qkv"], I["L0_mix_b_qkv"], I["L0_mix_random_features"]),
                          phase_project(k, "p0", False, I["L0_mix_W_proj"], I["L0_mix_b_proj"], I["x"])),
                 lambda: gnn_block(k, I),
                 lambda: (phase_norm(k, "n1"),
                          phase_ffn(k, "f0", I["L0_ffn_w_fc"], I["L0_ffn_b_fc"], I["L0_ffn_w_proj"], I["L0_ffn_b_proj"],
                                    I["L0_ffn_alpha_e"], I["L0_ffn_alpha_r"])),
                 lambda: (phase_norm(k, "n2"),
                          phase_save(k, "save"),
                          phase_attend(k, "m1", True, I["L1_mix_W_qkv"], None, I["L1_mix_random_features"]),
                          phase_project(k, "p1", True, I["L1_mix_W_proj"], I["L1_mix_b_proj"], k.x_dram,
                                        I["L1_mix_gamma"], I["L1_mix_beta"])),
                 lambda: phase_gcn(k, "gc", I["L1_gnn_W"], I["L1_gnn_b"]),
                 lambda: (phase_norm(k, "n3"),
                          phase_router(k, "ro", I["L1_ffn_W_router"], I["L1_ffn_expert_bias"]),
                          phase_experts(k, "ex", (I["L1_ffn_Wg_s"], I["L1_ffn_Wu_s"], I["L1_ffn_Wd_s"]),
                                        (I["L1_ffn_Wg_r"], I["L1_ffn_Wu_r"], I["L1_ffn_Wd_r"]))),
                 ]
        for step in steps[:stop]:
            step()
        k.begin(ctx)
        stored = k.sem("stored")
        block = ctx.enter_context(nc.Block())

        @block.sync
        def _(sp):
            for t in range(TT):
                sp.dma_start(out[t * P:t * P + TS[t], :], k.x[0:TS[t], t, :]).then_inc(stored, 16)
            sp.wait_ge(stored, 16 * TT)


def kernel(**inputs):
    import numpy as _np
    import concourse.bacc as _bacc
    from concourse import mybir as _mybir
    from concourse.bass_utils import run_bass_kernel_spmd as _run

    nc = _bacc.Bacc("TRN2", target_bir_lowering=False, num_devices=1)
    arrays, args = {}, {}
    for name, value in inputs.items():
        a = _np.ascontiguousarray(value)
        arrays[f"in_{name}"] = a
        args[name] = nc.dram_tensor(f"in_{name}", a.shape, _mybir.dt.from_np(a.dtype), kind="ExternalInput").ap()
    out = nc.dram_tensor("out_0", (NODES, D), F32, kind="ExternalOutput").ap()
    build(nc, args, out)
    r = _run(nc, [arrays], core_ids=[0])
    return r.results[0]["out_0"]
```

```python
from contextlib import ExitStack

import numpy as np
import concourse.bass as bass
from concourse import mybir

F32 = mybir.dt.float32
F32R = mybir.dt.float32r
BF16 = mybir.dt.bfloat16
F16 = mybir.dt.float16
I32 = mybir.dt.int32
U32 = mybir.dt.uint32
ALU = mybir.AluOpType
ACT = mybir.ActivationFunctionType
AX = mybir.AxisListType

P = 128
NODES = 625
TT = (NODES + P - 1) // P
TS = [min(P, NODES - P * t) for t in range(TT)]
HN = 314
NT = 2 * HN
D = 768
KD = D // P
EMB = 128
D1 = D + EMB
K1 = D1 // P
EDGES = 10000
EP = 125
ET = EDGES // EP
RELS = 3
HEADS = 12
PAIRS = HEADS // 2
DH = 64
VW = DH + 2
MF = 256
H_FF = 192
HP = 96
EXPERTS = 8
F_MOE = 1536
EPS = 1e-5
WE_MIX, WE_GNN, WE_MOE = KD * 256, K1 * 256, KD * 384


def weight_view(w):
    return w.rearrange("(k p) n -> p k n", p=P)


class Stream:

    def __init__(self, k, name, chunks, elems, raws, splits):
        self.chunks, self.raws, self.splits, self.one = chunks, raws, splits, k.one[:]
        self.raw = k.sb(f"{name}_raw", [P, raws, elems], F32)
        self.hi = k.sb(f"{name}_hi", [P, splits, elems], F32R)
        self.lo = k.sb(f"{name}_lo", [P, splits, elems], F32R)
        self.loaded = [k.sem(f"{name}_loaded{i}") for i in range(raws)]
        self.hi_done = k.sem(f"{name}_hi_done")
        self.lo_done = k.sem(f"{name}_lo_done")
        self.freed = {}

    def landed(self, n):
        return 16 * sum(len(c[2]) for i, c in enumerate(self.chunks[:n + 1]) if i % self.raws == n % self.raws)

    def views(self, n):
        kt, cols, _ = self.chunks[n]
        s = n % self.splits
        return [b[:, s, 0:kt * cols].rearrange("p (k c) -> p k c", c=cols) for b in (self.hi, self.lo)]


def stream_loads(sp, st):
    for n, (kt, cols, parts) in enumerate(st.chunks):
        if n >= st.raws:
            sp.wait_ge(st.lo_done, n - st.raws + 1)
        dst = st.raw[:, n % st.raws, 0:kt * cols].rearrange("p (k c) -> p k c", c=cols)
        for c0, c1, src in parts:
            sp.dma_start(dst[:, :, c0:c1], src).then_inc(st.loaded[n % st.raws], 16)


def stream_splits(pool, st):
    for n, (kt, cols, _) in enumerate(st.chunks):
        size = kt * cols
        raw = st.raw[:, n % st.raws, 0:size]
        hi, lo = st.hi[:, n % st.splits, 0:size], st.lo[:, n % st.splits, 0:size]
        pool.wait_ge(st.loaded[n % st.raws], st.landed(n))
        if n >= st.splits:
            pool.wait_ge(*st.freed[n - st.splits])
        pool.tensor_tensor(hi, raw, st.one.broadcast_to([P, size]), ALU.mult).then_inc(st.hi_done, 1)
        pool.wait_ge(st.hi_done, n + 1)
        pool.tensor_tensor(lo, raw, hi.bitcast(F32), ALU.subtract).then_inc(st.lo_done, 1)


def one_chunk(w, cols, c0):
    v = weight_view(w)
    return (v.shape[1], cols, [(0, cols, v[:, :, c0:c0 + cols])])


def split_product(pe, out, lhs, rhs, first, last):
    for i, (a, b) in enumerate(((0, 0), (0, 1), (1, 0))):
        mm = pe.matmul(out, lhs[a], rhs[b], start=(first and i == 0), stop=(last and i == 2))
    return mm


def split_product_wide(pe, bank_pair, lhs, rhs, first, last):
    for i, (a, b) in enumerate(((0, 0), (0, 1), (1, 0))):
        for h in range(2):
            mm = pe.matmul(bank_pair[:, h, 0:HN], lhs[a], rhs(b, h),
                           start=(first and i == 0), stop=(last and i == 2))
    return mm


def halves(t):
    return t.rearrange("p (h n) -> p h n", h=2)


def signals(k, phase, names):
    return {name: k.sem(f"{phase}_{name}") for name in names}


class Link:

    def __init__(self, eng, sem):
        self.eng, self.sem, self.n = eng, sem, 0

    def __call__(self, ins):
        self.n += 1
        ins.then_inc(self.sem, 1)
        self.eng.wait_ge(self.sem, self.n)



def turn_tile(pe, k, src, t):
    ts = TS[t]
    for j in range(KD):
        bank = k.banks[2 * (t % 2) + j // 4]
        mm = pe.transpose(bank[:, (j % 4) * P:(j % 4) * P + ts], src[0:ts, j * P:(j + 1) * P], k.ident[0:ts, 0:ts])
    return mm


def to_feature_major_act(act, k, dst, t, turned, hi_done):
    act.wait_ge(turned, t + 1)
    for b, (j0, j1) in enumerate(((0, 4), (4, KD))):
        src = k.banks[2 * (t % 2) + b][:, 0:(j1 - j0) * P].rearrange("p (j n) -> p j n", n=P)[:, :, 0:TS[t]]
        act.activation(dst[:, j0:j1, 0, t * P:t * P + TS[t]], src, ACT.Copy).then_inc(hi_done, 1)


def to_feature_major_dve(dve, k, dst, t, hi_done, lo_done):
    dve.wait_ge(hi_done, 2 * t + 2)
    for b, (j0, j1) in enumerate(((0, 4), (4, KD))):
        src = k.banks[2 * (t % 2) + b][:, 0:(j1 - j0) * P].rearrange("p (j n) -> p j n", n=P)[:, :, 0:TS[t]]
        ins = dve.tensor_tensor(dst[:, j0:j1, 1, t * P:t * P + TS[t]], src,
                                dst[:, j0:j1, 0, t * P:t * P + TS[t]].bitcast(F32), ALU.subtract)
    ins.then_inc(lo_done, 1)


def norm_stats(dve, link, k, src, mean_var):
    for t in range(TT):
        ts = TS[t]
        for h in range(2):
            ins = dve.bn_stats(k.bn[0:ts, t, h, :], src[0:ts, t, h * 384:(h + 1) * 384])
        link(ins)
        dve.bn_aggr(mean_var[0:ts, t, :], k.bn[0:ts, t, :, :].rearrange("p h s -> p (h s)"))


def phase_norm(k, name, load_x=False, keep=False):
    with ExitStack() as ctx:
        k.begin(ctx)
        slots = TT if keep else 2
        xn = k.a if keep else k.sb(f"{name}_xn", [P, slots, D], F32)
        s = signals(k, name, (
            "x_loaded", "consts", "chain", "var_ready", "root_ready", "xn_ready", "turned", "hi_done", "lo_done"))
        block = ctx.enter_context(k.nc.Block())

        @block.sync
        def _(sp):
            if load_x:
                for t in range(TT):
                    sp.dma_start(k.x[0:TS[t], t, :], k.x_in[t * P:t * P + TS[t], :]).then_inc(s["x_loaded"], 16)

        @block.gpsimd
        def _(pool):
            k.clear_last(pool)
            if load_x:
                pool.memset(k.one[:], 1.0)
                pool.memset(k.ident[:], 0.0).then_inc(s["consts"], 1)
                pool.wait_ge(s["consts"], 1)
                pool.affine_select(out=k.ident[:], in_=k.ident[:], compare_op=ALU.not_equal, fill=1.0, base=0,
                                   pattern=[[-1, P]], channel_multiplier=1).then_inc(s["consts"], 1)

        @block.vector
        def _(dve):
            link = Link(dve, s["chain"])
            if load_x:
                dve.memset(k.xt[:, :, :, NODES:NT].bitcast(F32), 0.0)
            if load_x:
                dve.memset(k.mv[:], 1.0)
                link(dve.memset(k.bn[:], 0.0))
                dve.wait_ge(s["x_loaded"], 16 * TT)
            norm_stats(dve, link, k, k.x, k.mv)
            rsqrt_of_var(dve, link, k, s)
            for t in range(TT):
                ts = TS[t]
                if t >= slots:
                    dve.wait_ge(s["turned"], t - 1)
                dve.tensor_scalar(xn[0:ts, t % slots, :], k.x[0:ts, t, :], k.mv[0:ts, t, 0:1], k.rstd[0:ts, t:t + 1],
                                  ALU.subtract, ALU.mult).then_inc(s["xn_ready"], 1)
                if t >= 1:
                    to_feature_major_dve(dve, k, k.xt, t - 1, s["hi_done"], s["lo_done"])
            to_feature_major_dve(dve, k, k.xt, TT - 1, s["hi_done"], s["lo_done"])

        @block.scalar
        def _(act):
            act.wait_ge(s["var_ready"], 1)
            act.activation(k.root[:], k.ve[:], ACT.Sqrt).then_inc(s["root_ready"], 1)
            for t in range(TT):
                to_feature_major_act(act, k, k.xt, t, s["turned"], s["hi_done"])

        @block.tensor
        def _(pe):
            if load_x:
                pe.wait_ge(s["consts"], 2)
            for t in range(TT):
                pe.wait_ge(s["xn_ready"], t + 1)
                if t >= 2:
                    pe.wait_ge(s["lo_done"], t - 1)
                turn_tile(pe, k, xn[:, t % slots, :], t).then_inc(s["turned"], 1)


def rsqrt_of_var(dve, link, k, s):
    link(dve.tensor_copy(k.ve[:, 0:1], k.mv[:, 0, 1:2]))
    link(dve.tensor_scalar(k.ve[:], k.mv[:, :, 1], EPS, None, ALU.add))
    rsqrt_of_ve(dve, link, k, s)


def rsqrt_of_ve(dve, link, k, s):
    dve.tensor_copy(k.tmp5[:], k.ve[:]).then_inc(s["var_ready"], 1)
    dve.wait_ge(s["root_ready"], 1)
    link(dve.reciprocal(k.rstd[:], k.root[:]))
    link(dve.tensor_tensor(k.tmp5[:], k.rstd[:], k.rstd[:], ALU.mult))
    link(dve.tensor_tensor(k.tmp5[:], k.tmp5[:], k.ve[:], ALU.mult))
    link(dve.tensor_scalar(k.tmp5[:], k.tmp5[:], -0.5, 1.5, ALU.mult, ALU.add))
    link(dve.tensor_tensor(k.rstd[:], k.rstd[:], k.tmp5[:], ALU.mult))



def phase_attend(k, name, second, w_qkv, b_qkv, rf):
    pw = weight_view(w_qkv)
    chunks = [(KD, 256, [(0, 256, pw[:, :, 2 * D + c * 256:2 * D + (c + 1) * 256])]) for c in range(3)]
    chunks += [(KD, 256, [(0, P, pw[:, :, p * P:(p + 1) * P]), (P, 2 * P, pw[:, :, D + p * P:D + (p + 1) * P])])
               for p in range(PAIRS)]
    FUNC = ACT.Exp if second else ACT.Relu
    KV_SCALE = 1.0 / MF if second else 1.0 / (DH * MF)
    with ExitStack() as ctx:
        k.begin(ctx)
        st = Stream(k, f"{name}_w", chunks, WE_MIX, 2, 2)
        vt = k.sb(f"{name}_v", [P, TT, 2, HEADS, VW], F32R)
        vf = k.sb(f"{name}_vf", [P, 2, 256], F32)
        qk = k.sb(f"{name}_qk", [P, 2, 2, NT], F32R)
        phik = k.sb(f"{name}_phik", [P, TT, 2, 512], F32R)
        phiq = k.sb(f"{name}_phiq", [P, 4, 2, NT], F32R)
        scratch = k.x[:].rearrange("p t d -> p (t d)")
        qkf = scratch[:, 0:2 * NT].rearrange("p (a n) -> p a n", a=2)
        pf = scratch[:, 2 * NT:4 * NT].rearrange("p (a n) -> p a n", a=2)
        sqf = scratch[:, 4 * NT:5 * NT]
        a_sb = k.a
        kv = k.sb(f"{name}_kv", [P, 2, 4, VW], F32R)
        kvf = k.sb(f"{name}_kvf", [P, 4, VW], F32)
        rfin = k.sb(f"{name}_rfin", [P, 2, DH], F32)
        rff = k.sb(f"{name}_rff", [P, 512], F32)
        rfbd = k.sb(f"{name}_rfbd", [P, 2, 512], F32R)
        if second:
            sq = k.sb(f"{name}_sq", [P, 2, 2, NT], F32R)
            nh = k.sb(f"{name}_nh", [P, 512], F32R)
            den = k.sb(f"{name}_den", [P, 2, 2], F32)
        else:
            bv = k.sb(f"{name}_bv", [P, D], F32)
            bq = k.sb(f"{name}_bq", [P, 2 * PAIRS], F32)
        s = signals(k, name, (
            "small", "consts", "chain", "rf_turned", "rf_bd", "rf_hi", "rf_ready", "v_mm", "v_f", "v_hi", "v_lo",
            "qk_mm", "qk_f", "qk_hi", "qk_lo", "sq_f", "sq_hi", "pk_mm", "pk_f", "pk_hi", "pk_lo",
            "pq_mm", "pq_f", "pq_hi", "pq_lo", "kv_mm", "kv_f", "kv_hi", "kv_lo", "at_mm", "at_out",
            ))
        smalls = 1 if second else 3
        st.freed.update({c: (s["v_mm"], TT * (c + 1)) for c in range(3)})
        st.freed.update({3 + p: (s["qk_mm"], 2 * (p + 1)) for p in range(PAIRS)})
        block = ctx.enter_context(k.nc.Block())
        kvb = k.banks[2]

        @block.sync
        def _(sp):
            sp.dma_start(rfin[:], rf.rearrange("(a p) d -> p a d", p=P)).then_inc(s["small"], 16)
            if not second:
                sp.dma_start(bv[:], b_qkv[2 * D:3 * D].partition_broadcast(P)).then_inc(s["small"], 16)
                sp.dma_start(bq[:], b_qkv[0:2 * D].rearrange("(j p) -> p j", p=P),
                             allow_slow_non_contiguous=True).then_inc(s["small"], 16)
            stream_loads(sp, st)

        @block.gpsimd
        def _(pool):
            k.clear_last(pool)
            stream_splits(pool, st)

        @block.tensor
        def _(pe):
            pe.wait_ge(s["small"], 16 * smalls)
            for a in range(2):
                mm = pe.transpose(k.banks[7][0:DH, a * P:(a + 1) * P], rfin[:, a, :], k.ident[:])
            mm.then_inc(s["rf_turned"], 1)
            for c in range(3):
                pe.wait_ge(st.lo_done, c + 1)
                wh = st.views(c)
                for t in range(TT):
                    i = c * TT + t
                    if i >= 2:
                        pe.wait_ge(s["v_f"], i - 1)
                    for j in range(KD):
                        mm = split_product(pe, k.banks[i % 2][0:TS[t], 0:256],
                                           [k.xt[:, j, a, t * P:t * P + TS[t]] for a in range(2)],
                                           [w[:, j, :] for w in wh], j == 0, j == KD - 1)
                    mm.then_inc(s["v_mm"], 1)

            def project_qk(p):
                n = 3 + p
                pe.wait_ge(st.lo_done, n + 1)
                wh = st.views(n)
                for a in range(2):
                    i = 2 * p + a
                    if i >= 2:
                        pe.wait_ge(s["qk_f"], i - 1)
                    if a == 1 and p >= 1:
                        pe.wait_ge(s["kv_f"], p)
                    for j in range(KD):
                        mm = split_product_wide(pe, k.pair[2 - a], [w[:, j, a * P:(a + 1) * P] for w in wh],
                                                lambda b, h: k.xt[:, j, b, h * HN:(h + 1) * HN], j == 0, j == KD - 1)
                    mm.then_inc(s["qk_mm"], 1)

            def features_k(p):
                pe.wait_ge(s["qk_lo"], 2 * p + 2)
                for t in range(TT):
                    i = p * TT + t
                    if i >= 2:
                        pe.wait_ge(s["pk_f"], i - 1)
                    if t < 2 and p >= 1:
                        pe.wait_ge(s["pq_f"], 4 * p)
                    out = k.banks[6 + t % 2][0:TS[t], 0:512]
                    mm = split_product(pe, out, [qk[:, 1, a, t * P:t * P + TS[t]] for a in range(2)],
                                       [rfbd[:, a, :] for a in range(2)], True, not second)
                    if second:
                        for a in range(2):
                            mm = pe.matmul(out, sq[:, 1, a, t * P:t * P + TS[t]], nh[:], start=False, stop=(a == 1))
                    mm.then_inc(s["pk_mm"], 1)

            def features_q(p):
                for m in range(4):
                    i = p * 4 + m
                    if i >= 2:
                        pe.wait_ge(s["pq_f"], i - 1)
                    if m == 0:
                        pe.wait_ge(s["at_out"], TT * p)
                    if m == 1:
                        pe.wait_ge(s["pk_f"], TT * (p + 1))
                    pair = k.pair[0] if m % 2 == 0 else k.pair[3]
                    mm = split_product_wide(pe, pair, [rfbd[:, a, m * P:(m + 1) * P] for a in range(2)],
                                            lambda b, h: qk[:, 0, b, h * HN:(h + 1) * HN], True, not second)
                    if second:
                        for a in range(2):
                            for h in range(2):
                                mm = pe.matmul(pair[:, h, 0:HN], nh[:, m * P:(m + 1) * P],
                                               sq[:, 0, a, h * HN:(h + 1) * HN], start=False, stop=(a == 1))
                    mm.then_inc(s["pq_mm"], 1)

            def keys_values(p):
                pe.wait_ge(s["pk_lo"], TT * (p + 1))
                pe.wait_ge(s["qk_f"], 2 * p + 2)
                for m in range(4):
                    for t in range(TT):
                        mm = split_product(pe, kvb[:, m * VW:(m + 1) * VW],
                                           [phik[0:TS[t], t, a, m * P:(m + 1) * P] for a in range(2)],
                                           [vt[0:TS[t], t, a, 2 * p + m // 2, :] for a in range(2)], t == 0, t == TT - 1)
                mm.then_inc(s["kv_mm"], 1)

            def attend(p):
                pe.wait_ge(s["kv_lo"], p + 1)
                pe.wait_ge(s["pq_lo"], 4 * (p + 1))
                for t in range(TT):
                    i = p * TT + t
                    if t >= 2:
                        pe.wait_ge(s["at_out"], i - 1)
                    for hd in range(2):
                        for m in range(2):
                            mm = split_product(pe, k.banks[t % 2][0:TS[t], hd * VW:(hd + 1) * VW],
                                               [phiq[:, 2 * hd + m, a, t * P:t * P + TS[t]] for a in range(2)],
                                               [kv[:, a, 2 * hd + m, :] for a in range(2)], m == 0, m == 1)
                    mm.then_inc(s["at_mm"], 1)

            pe.wait_ge(s["rf_ready"], 1)
            pe.wait_ge(s["v_lo"], 3 * TT)
            project_qk(0)
            for p in range(PAIRS):
                features_k(p)
                features_q(p)
                keys_values(p)
                if p + 1 < PAIRS:
                    project_qk(p + 1)
                attend(p)

        @block.scalar
        def _(act):
            def high(dst, src, after, at_least, done):
                act.wait_ge(after, at_least)
                act.activation(dst, src, ACT.Copy).then_inc(done, 1)

            high(rfbd[:, 0, :], rff[:], s["rf_bd"], 1, s["rf_hi"])
            for i in range(3 * TT):
                c, t = i // TT, i % TT
                high(vt[0:TS[t], t, 0, 4 * c:4 * c + 4, 0:DH],
                     vf[0:TS[t], i % 2, :].rearrange("p (h d) -> p h d", d=DH), s["v_f"], i + 1, s["v_hi"])

            def qk_high(p):
                for a in range(2):
                    i = 2 * p + a
                    if p >= 1 and a == 0:
                        act.wait_ge(s["pk_mm"], TT * p)
                        act.wait_ge(s["pq_mm"], 4 * p)
                    high(qk[:, a, 0, :], qkf[:, a, :], s["qk_f"], i + 1, s["qk_hi"])
                    if second:
                        high(sq[:, a, 0, :], sqf[:], s["sq_f"], i + 1, s["sq_hi"])

            qk_high(0)
            for p in range(PAIRS):
                for t in range(TT):
                    i = p * TT + t
                    if p >= 1 and t == 0:
                        act.wait_ge(s["kv_mm"], p)
                    act.wait_ge(s["pk_mm"], i + 1)
                    if t >= 2:
                        act.wait_ge(s["pk_lo"], i - 1)
                    elif p >= 1:
                        act.wait_ge(s["pq_lo"], 4 * p)
                    f = pf[0:TS[t], t % 2, 0:512]
                    act.activation(f, k.banks[6 + t % 2][0:TS[t], 0:512], FUNC).then_inc(s["pk_f"], 1)
                    high(phik[0:TS[t], t, 0, :], f, s["pk_f"], i + 1, s["pk_hi"])
                for m in range(4):
                    i = p * 4 + m
                    if p >= 1 and m == 0:
                        act.wait_ge(s["at_mm"], TT * p)
                    act.wait_ge(s["pq_mm"], i + 1)
                    if m >= 2:
                        act.wait_ge(s["pq_lo"], i - 1)
                    else:
                        act.wait_ge(s["pk_lo"], TT * (p + 1))
                    pair = k.pair[0] if m % 2 == 0 else k.pair[3]
                    f = pf[:, m % 2, :]
                    act.activation(halves(f), pair[:, :, 0:HN], FUNC).then_inc(s["pq_f"], 1)
                    high(phiq[:, m, 0, :], f, s["pq_f"], i + 1, s["pq_hi"])
                if p >= 1:
                    act.wait_ge(s["at_mm"], TT * p)
                act.wait_ge(s["kv_mm"], p + 1)
                if p >= 1:
                    act.wait_ge(s["kv_lo"], p)
                act.activation(kvf[:], kvb[:, 0:4 * VW].rearrange("p (m v) -> p m v", v=VW), ACT.Copy,
                               scale=KV_SCALE).then_inc(s["kv_f"], 1)
                high(kv[:, 0, :, :], kvf[:], s["kv_f"], p + 1, s["kv_hi"])
                if p + 1 < PAIRS:
                    qk_high(p + 1)
                if not second:
                    for t in range(TT):
                        act.wait_ge(s["at_mm"], p * TT + t + 1)
                        act.activation(a_sb[0:TS[t], t, p * P:(p + 1) * P].rearrange("p (h d) -> p h d", d=DH),
                                       k.banks[t % 2][0:TS[t], 0:2 * VW].rearrange("p (h d) -> p h d", d=VW)[:, :, 0:DH],
                                       ACT.Copy).then_inc(s["at_out"], 1)

        @block.vector
        def _(dve):
            link = Link(dve, s["chain"])
            dve.memset(vt[:, :, :, :, DH:VW].bitcast(F32), 0.0)
            link(dve.memset(rff[:], 0.0))
            link(dve.memset(vt[:, :, 0, :, DH:DH + 1].bitcast(F32), 1.0))
            if second:
                link(dve.memset(nh[:].bitcast(F32), 0.0))
                for hd in range(2):
                    link(dve.memset(nh[hd * DH:(hd + 1) * DH, hd * MF:(hd + 1) * MF].bitcast(F32), -0.5))
            dve.wait_ge(s["rf_turned"], 1)
            for hd in range(2):
                ins = dve.tensor_copy(rff[hd * DH:(hd + 1) * DH, hd * MF:(hd + 1) * MF], k.banks[7][0:DH, 0:MF])
                if hd == 0:
                    link(ins)
            ins.then_inc(s["rf_bd"], 1)
            dve.wait_ge(s["rf_hi"], 1)
            dve.tensor_tensor(rfbd[:, 1, :], rff[:], rfbd[:, 0, :].bitcast(F32), ALU.subtract).then_inc(s["rf_ready"], 1)
            dve.wait_ge(s["small"], 16 * smalls)

            def v_low(i):
                c, t = i // TT, i % TT
                dve.wait_ge(s["v_hi"], i + 1)
                dve.tensor_tensor(vt[0:TS[t], t, 1, 4 * c:4 * c + 4, 0:DH],
                                  vf[0:TS[t], i % 2, :].rearrange("p (h d) -> p h d", d=DH),
                                  vt[0:TS[t], t, 0, 4 * c:4 * c + 4, 0:DH].bitcast(F32), ALU.subtract).then_inc(s["v_lo"], 1)

            for i in range(3 * TT):
                c, t = i // TT, i % TT
                dve.wait_ge(s["v_mm"], i + 1)
                if i >= 2:
                    dve.wait_ge(s["v_lo"], i - 1)
                src, dst = k.banks[i % 2][0:TS[t], 0:256], vf[0:TS[t], i % 2, :]
                if second:
                    dve.tensor_copy(dst, src).then_inc(s["v_f"], 1)
                else:
                    dve.tensor_tensor(dst, src, bv[0:TS[t], c * 256:(c + 1) * 256], ALU.add).then_inc(s["v_f"], 1)
                if i >= 1:
                    v_low(i - 1)
            v_low(3 * TT - 1)

            def qk_parts(p):
                for a in range(2):
                    i = 2 * p + a
                    dve.wait_ge(s["qk_mm"], i + 1)
                    if p >= 1:
                        dve.wait_ge(s["qk_lo"], 2 * p)
                    src = k.pair[2 - a][:, :, 0:HN]
                    if second:
                        dve.tensor_copy(halves(qkf[:, a, :]), src).then_inc(s["qk_f"], 1)
                        dve.wait_ge(s["qk_f"], i + 1)
                        if i >= 1:
                            dve.wait_ge(s["sq_hi"], i)
                        dve.tensor_tensor(sqf[:], qkf[:, a, :], qkf[:, a, :], ALU.mult).then_inc(s["sq_f"], 1)
                        dve.wait_ge(s["sq_hi"], i + 1)
                        link(dve.tensor_tensor(sq[:, a, 1, :], sqf[:], sq[:, a, 0, :].bitcast(F32), ALU.subtract))
                    else:
                        dve.tensor_scalar(halves(qkf[:, a, :]), src, bq[:, a * PAIRS + p:a * PAIRS + p + 1], None,
                                          ALU.add).then_inc(s["qk_f"], 1)
                    dve.wait_ge(s["qk_hi"], i + 1)
                    dve.tensor_tensor(qk[:, a, 1, :], qkf[:, a, :], qk[:, a, 0, :].bitcast(F32),
                                      ALU.subtract).then_inc(s["qk_lo"], 1)

            qk_parts(0)
            for p in range(PAIRS):
                for t in range(TT):
                    dve.wait_ge(s["pk_hi"], p * TT + t + 1)
                    dve.tensor_tensor(phik[0:TS[t], t, 1, :], pf[0:TS[t], t % 2, 0:512],
                                      phik[0:TS[t], t, 0, :].bitcast(F32), ALU.subtract).then_inc(s["pk_lo"], 1)
                for m in range(4):
                    dve.wait_ge(s["pq_hi"], p * 4 + m + 1)
                    dve.tensor_tensor(phiq[:, m, 1, :], pf[:, m % 2, :], phiq[:, m, 0, :].bitcast(F32),
                                      ALU.subtract).then_inc(s["pq_lo"], 1)
                dve.wait_ge(s["kv_hi"], p + 1)
                dve.tensor_tensor(kv[:, 1, :, :], kvf[:], kv[:, 0, :, :].bitcast(F32), ALU.subtract).then_inc(s["kv_lo"], 1)
                if p + 1 < PAIRS:
                    qk_parts(p + 1)
                if second:
                    for t in range(TT):
                        ts = TS[t]
                        dve.wait_ge(s["at_mm"], p * TT + t + 1)
                        o = k.banks[t % 2][0:ts, 0:2 * VW].rearrange("p (h d) -> p h d", d=VW)
                        link(dve.tensor_scalar(den[0:ts, 0, :], o[:, :, DH], 1e-6, None, ALU.add))
                        link(dve.reciprocal(den[0:ts, 1, :], den[0:ts, 0, :]))
                        for hd in range(2):
                            ins = dve.tensor_scalar(a_sb[0:ts, t, (2 * p + hd) * DH:(2 * p + hd + 1) * DH],
                                                    o[:, hd, 0:DH], den[0:ts, 1, hd:hd + 1], None, ALU.mult)
                        ins.then_inc(s["at_out"], 1)
                        dve.wait_ge(s["at_out"], p * TT + t + 1)


def phase_project(k, name, second, w_proj, b_proj, x_src, gamma=None, beta=None):
    chunks = [one_chunk(w_proj, 256, c * 256) for c in range(3)]
    with ExitStack() as ctx:
        k.begin(ctx)
        st = Stream(k, f"{name}_w", chunks, WE_MIX, 2, 3)
        at = k.sb(f"{name}_at", [P, KD, 2, NT], F32R)
        bp = k.sb(f"{name}_bp", [P, D], F32)
        a_sb = k.a
        if second:
            gb = k.sb(f"{name}_gb", [P, 2, D], F32)
            y_sb = k.sb(f"{name}_y", [P, TT, D], F32)
        s = signals(k, name, (
            "small", "x_loaded", "chain", "turned", "t_hi", "t_lo", "proj_mm", "proj_out", "var_ready", "root_ready"))
        st.freed.update({c: (s["proj_mm"], TT * (c + 1)) for c in range(3)})
        smalls = 3 if second else 1
        block = ctx.enter_context(k.nc.Block())

        @block.sync
        def _(sp):
            stream_loads(sp, st)

        @block.gpsimd
        def _(pool):
            k.clear_last(pool)
            stream_splits(pool, st)

        @block.tensor
        def _(pe):
            for t in range(TT):
                if t >= 2:
                    pe.wait_ge(s["t_lo"], t - 1)
                turn_tile(pe, k, a_sb[:, t, :], t).then_inc(s["turned"], 1)
            pe.wait_ge(s["t_lo"], TT)
            for c in range(3):
                pe.wait_ge(st.lo_done, c + 1)
                wh = st.views(c)
                for t in range(TT):
                    i = c * TT + t
                    if i >= 2:
                        pe.wait_ge(s["proj_out"], i - 1)
                    for j in range(KD):
                        mm = split_product(pe, k.banks[4 + i % 2][0:TS[t], 0:256],
                                           [at[:, j, a, t * P:t * P + TS[t]] for a in range(2)],
                                           [w[:, j, :] for w in wh], j == 0, j == KD - 1)
                    mm.then_inc(s["proj_mm"], 1)

        @block.scalar
        def _(act):
            act.dma_start(bp[:], b_proj.partition_broadcast(P)).then_inc(s["small"], 16)
            if second:
                act.dma_start(gb[:, 0, :], gamma.partition_broadcast(P)).then_inc(s["small"], 16)
                act.dma_start(gb[:, 1, :], beta.partition_broadcast(P)).then_inc(s["small"], 16)
            for t in range(TT):
                act.dma_start(k.x[0:TS[t], t, :], x_src[t * P:t * P + TS[t], :]).then_inc(s["x_loaded"], 16)
            for t in range(TT):
                to_feature_major_act(act, k, at, t, s["turned"], s["t_hi"])
            if second:
                act.wait_ge(s["var_ready"], 1)
                act.activation(k.root[:], k.ve[:], ACT.Sqrt).then_inc(s["root_ready"], 1)

        @block.vector
        def _(dve):
            link = Link(dve, s["chain"])
            for t in range(TT):
                to_feature_major_dve(dve, k, at, t, s["t_hi"], s["t_lo"])
            dve.wait_ge(s["small"], 16 * smalls)
            dve.wait_ge(s["x_loaded"], 16 * TT)
            y_all = y_sb if second else k.x
            if second:
                for t in range(TT):
                    ins = dve.tensor_scalar(y_sb[0:TS[t], t, :], k.x[0:TS[t], t, :], k.mv[0:TS[t], t, 0:1],
                                            k.rstd[0:TS[t], t:t + 1], ALU.subtract, ALU.mult)
                link(ins)
            for t in range(TT):
                ins = dve.tensor_tensor(y_all[0:TS[t], t, :], y_all[0:TS[t], t, :], bp[0:TS[t], :], ALU.add)
            link(ins)
            for i in range(3 * TT):
                c, t = i // TT, i % TT
                y = y_all[0:TS[t], t, c * 256:(c + 1) * 256]
                dve.wait_ge(s["proj_mm"], i + 1)
                dve.tensor_tensor(y, k.banks[4 + i % 2][0:TS[t], 0:256], y, ALU.add).then_inc(s["proj_out"], 1)
            if second:
                dve.wait_ge(s["proj_out"], 3 * TT)
                norm_stats(dve, link, k, y_sb, k.mv)
                rsqrt_of_var(dve, link, k, s)
                for op in range(4):
                    for t in range(TT):
                        ts = TS[t]
                        y = y_sb[0:ts, t, :]
                        if op == 0:
                            ins = dve.tensor_scalar(y, y, k.mv[0:ts, t, 0:1], k.rstd[0:ts, t:t + 1], ALU.subtract, ALU.mult)
                        elif op == 3:
                            ins = dve.tensor_tensor(k.x[0:ts, t, :], k.x[0:ts, t, :], y, ALU.add)
                        else:
                            ins = dve.tensor_tensor(y, y, gb[0:ts, op - 1, :], ALU.mult if op == 1 else ALU.add)
                    link(ins)



UNROLL = 4
SW = TT * P


BASE = 256
TO_INT = 1.5 * 2 ** 23


def count_pieces():
    pieces, seen = [], set()
    for s in range(TT):
        c0 = s * NT
        while c0 < (s + 1) * NT:
            c1 = min((s + 1) * NT, (c0 // 512 + 1) * 512)
            pieces.append((s, c0, c1, c0 // 512 not in seen))
            seen.add(c0 // 512)
            c0 = c1
    return pieces


def phase_counts(k, src, dst, edge_type, node_emb, node_type):
    flat = k.psum[:].rearrange("p b n -> p (b n)")
    with ExitStack() as ctx:
        k.begin(ctx)
        edges_i = k.sb("edges_i", [EP, 3, ET], I32)
        edges_f = k.sb("edges_f", [EP, 3, ET], F32)
        over = k.sb("count_over", [P, 2], F32R)
        iota_i = k.sb("iota_i", [P, SW], I32)
        iota = k.sb("iota", [P, SW], F16)
        weight = k.sb("edge_weight", [EP, 1 + RELS, ET], F32)
        rounds = k.sb("count_rounds", [P, 1], I32)
        checks = k.sb("count_checks", [P, 4], F32)
        shift = k.sb("digit_shift", [P, 1], F32)
        quot = k.sb("digit_quot", [P, 2, NT], F32)
        upper = k.sb("digit_upper", [P, 2, NT], F32)
        quot2 = k.sb("digit_quot2", [P, 2, NT], F32)
        src_hot = k.sb("src_hot", [EP, UNROLL, SW], BF16)
        dst_hot = k.sb("dst_hot", [EP, UNROLL, NT], BF16)
        total = k.sb("count_total", [P, TT, NT], F32)
        ones_f = k.sb("ones_f", [P, P], F32)
        ones = k.sb("ones_r", [P, P], F32R)
        pos = k.sb("count_pos", [P, NT], F32)
        cnt = k.sb("count_rel", [P, NT], F32)
        emb_sb = k.sb("node_emb", [RELS, EMB], F32)
        type_i = k.sb("type_i", [RELS, NODES], I32)
        type_f = k.sb("type_f", [RELS, NODES], F32)
        own = k.sb("own_type", [RELS, 1], F32)
        onehot = k.sb("type_onehot", [RELS, NT], F32)
        s = signals(k, "c", (
            "loaded", "iota_made", "chain", "hot", "tile_mm", "copied", "ones_made", "sum_mm", "sum_read",
            "total_made", "saved", "quot", "upper", "low", "quot2",
            "over_made", "shift_made", "top_digit", "all_copied", "check_mm", "rounds_made", "emb_loaded", "own_made", "emb_made", "emb_ready", "emb_hi"))
        block = ctx.enter_context(k.nc.Block())
        pieces = count_pieces()

        @block.sync
        def _(sp):
            for i, e in enumerate((src, dst, edge_type)):
                sp.dma_start(edges_i[:, i, :], e.rearrange("(p j) -> p j", p=EP)).then_inc(s["loaded"], 16)
            sp.dma_start(emb_sb[:], node_emb).then_inc(s["emb_loaded"], 16)
            for r in range(RELS):
                sp.dma_start(type_i[r:r + 1, :], node_type.rearrange("(a n) -> a n", a=1)).then_inc(s["emb_loaded"], 16)
            sp.wait_ge(s["total_made"], 2)
            sp.dma_start(k.total_dram, total[:].rearrange("p t n -> p (t n)")).then_inc(s["saved"], 16)
            sp.wait_ge(s["saved"], 16)

        @block.gpsimd
        def _(pool):
            k.clear_last(pool)
            pool.iota(iota_i[:], [[1, SW]], base=0, channel_multiplier=0).then_inc(s["iota_made"], 1)
            pool.iota(own[:], [[0, 1]], base=0, channel_multiplier=1,
                      allow_small_or_imprecise_dtypes=True).then_inc(s["own_made"], 1)

        @block.vector
        def _(dve):
            link = Link(dve, s["chain"])
            dve.memset(ones_f[:], 1.0).then_inc(s["ones_made"], 1)
            link(dve.memset(onehot[:], 0.0))
            dve.wait_ge(s["iota_made"], 1)
            dve.tensor_copy(iota[:], iota_i[:])
            dve.wait_ge(s["loaded"], 48)
            link(dve.tensor_copy(edges_f[:], edges_i[:]))
            dve.memset(shift[:], -(BASE / 2 - 1) / BASE).then_inc(s["shift_made"], 1)
            for r in range(RELS):
                ins = dve.tensor_scalar(weight[:, 1 + r, :], edges_f[:, 2, :], float(r), None, ALU.is_equal)
                link(ins)
            link(dve.scalar_tensor_tensor(weight[:, 0, :], weight[:, 2, :], float(BASE), weight[:, 1, :], ALU.mult, ALU.add))
            link(dve.scalar_tensor_tensor(weight[:, 0, :], weight[:, 3, :], float(BASE ** 2), weight[:, 0, :],
                                          ALU.mult, ALU.add))

            by_slot = edges_f[:].rearrange("e f (g u) -> e f u g", u=UNROLL)
            weight_by_slot = weight[:].rearrange("e r (g u) -> e u (r g)", u=UNROLL)

            def one_hots(r, g, u, seq, wait):
                if wait:
                    dve.wait_ge(s["tile_mm"], seq - UNROLL + 1)
                dve.tensor_scalar(src_hot[:, u, :], iota[0:EP, :], by_slot[:, 0, u, bass.ds(g, 1)], None, ALU.is_equal)
                dve.tensor_scalar(dst_hot[:, u, :], iota[0:EP, 0:NT], by_slot[:, 1, u, bass.ds(g, 1)],
                                  weight_by_slot[:, u, bass.ds(r * (ET // UNROLL) + g, 1)], ALU.is_equal, ALU.mult).then_inc(s["hot"], 1)

            def all_one_hots(r, wait):
                for u in range(UNROLL):
                    one_hots(r, 0, u, r * ET + u, wait)
                with dve.Fori(1, ET // UNROLL) as g:
                    for u in range(UNROLL):
                        one_hots(r, g, u, g * UNROLL + (r * ET + u), True)

            all_one_hots(0, False)
            for t in range(TT):
                up = upper[:, t % 2, :]
                dve.wait_ge(s["quot"], t + 1)
                if t >= 2:
                    dve.wait_ge(s["quot2"], t - 1)
                dve.tensor_scalar(up, quot[:, t % 2, :], TO_INT, -TO_INT, ALU.add, ALU.add).then_inc(s["upper"], 1)
                dve.wait_ge(s["upper"], t + 1)
                dve.scalar_tensor_tensor(k.C[:, 0, t, :], up, -float(BASE), total[:, t, :],
                                         ALU.mult, ALU.add).then_inc(s["low"], 1)
                dve.wait_ge(s["quot2"], t + 1)
                dve.tensor_scalar(k.C[:, 2, t, :], quot2[:, t % 2, :], TO_INT, -TO_INT, ALU.add, ALU.add)\
                    .then_inc(s["top_digit"], 1)
                dve.wait_ge(s["top_digit"], t + 1)
                dve.scalar_tensor_tensor(k.C[:, 1, t, :], k.C[:, 2, t, :].bitcast(F32), -float(BASE), up,
                                         ALU.mult, ALU.add).then_inc(s["copied"], 1)
            dve.wait_ge(s["copied"], TT)
            link(dve.tensor_reduce(checks[:, 0:1], k.C[:, 2, :, :].bitcast(F32).rearrange("p t n -> p (t n)"),
                                   AX.X, ALU.max))
            dve.tensor_scalar(over[:], checks[:, 0:1].broadcast_to([P, 2]), float(BASE), None, ALU.is_ge)\
                .then_inc(s["over_made"], 1)
            dve.wait_ge(s["check_mm"], 1)
            dve.tensor_copy(checks[:, 1:2], k.banks[7][:, 0:1])
            link(dve.tensor_reduce(checks[:, 2:3], k.pair[0][:, :, 0:HN], AX.XY, ALU.add))
            link(dve.tensor_scalar(checks[:, 2:3], checks[:, 2:3], float(EDGES), None, ALU.not_equal))
            link(dve.tensor_tensor(checks[:, 2:3], checks[:, 1:2], checks[:, 2:3], ALU.add))
            link(dve.tensor_scalar(checks[:, 3:4], checks[:, 2:3], 0.5, float(RELS), ALU.is_gt, ALU.mult))
            dve.tensor_copy(rounds[:], checks[:, 3:4]).then_inc(s["rounds_made"], 1)
            dve.wait_ge(s["rounds_made"], 1)
            again = dve.value_load(rounds[0:1, 0:1], min_val=0, max_val=RELS)
            with dve.Fori(0, again) as r:
                all_one_hots(r + 1, True)
            for r in range(RELS):
                dve.wait_ge(s["sum_mm"], r + 1)
                sums = k.pair[r][:, :, 0:HN]
                link(dve.tensor_scalar(halves(pos[:]), sums, 0.0, None, ALU.is_gt))
                link(dve.tensor_scalar(halves(cnt[:]), sums, 1.0, None, ALU.max))
                link(dve.reciprocal(cnt[:], cnt[:]))
                link(dve.tensor_tensor(k.inv[:, r, :], cnt[:], pos[:], ALU.mult))
            dve.tensor_tensor(total[:], k.C[:, 0, :, :].bitcast(F32), k.C[:, 1, :, :].bitcast(F32), ALU.add).then_inc(s["total_made"], 1)
            dve.wait_ge(s["total_made"], 1)
            dve.tensor_tensor(total[:], total[:], k.C[:, 2, :, :].bitcast(F32), ALU.add).then_inc(s["total_made"], 1)
            dve.wait_ge(s["emb_loaded"], 64)
            link(dve.tensor_copy(type_f[:], type_i[:]))
            dve.wait_ge(s["own_made"], 1)
            dve.tensor_scalar(onehot[:, 0:NODES], type_f[:], own[:, 0:1], None, ALU.is_equal).then_inc(s["emb_made"], 1)
            dve.wait_ge(s["emb_hi"], 1)
            dve.tensor_tensor(halves(k.et[:, 0, 1, :]), k.pair[3][:, :, 0:HN], halves(k.et[:, 0, 0, :].bitcast(F32)),
                              ALU.subtract)

        @block.scalar
        def _(act):
            act.wait_ge(s["ones_made"], 1)
            act.activation(ones[:], ones_f[:], ACT.Copy).then_inc(s["ones_made"], 1)
            act.wait_ge(s["shift_made"], 1)
            act.wait_ge(s["tile_mm"], ET)
            def second_quotient(t):
                act.wait_ge(s["upper"], t + 1)
                if t >= 2:
                    act.wait_ge(s["top_digit"], t - 1)
                act.activation(quot2[:, t % 2, :], upper[:, t % 2, :], ACT.Identity, bias=shift[:, 0:1],
                               scale=1.0 / BASE).then_inc(s["quot2"], 1)

            for t in range(TT):
                if t >= 2:
                    act.wait_ge(s["upper"], t - 1)
                act.activation(total[:, t, :], flat[:, t * NT:(t + 1) * NT], ACT.Copy).then_inc(s["sum_read"], 1)
                act.wait_ge(s["sum_read"], t + 1)
                act.activation(quot[:, t % 2, :], total[:, t, :], ACT.Identity, bias=shift[:, 0:1],
                               scale=1.0 / BASE).then_inc(s["quot"], 1)
                if t >= 1:
                    second_quotient(t - 1)
            second_quotient(TT - 1)
            act.wait_ge(s["rounds_made"], 1)
            again = act.value_load(rounds[0:1, 0:1], min_val=0, max_val=RELS)
            with act.Fori(0, again) as r:
                act.wait_ge(s["tile_mm"], ET * r + 2 * ET)
                for t in range(TT):
                    act.activation(k.C[:, bass.ds(r, 1), t, :].rearrange("p a n -> p (a n)"),
                                   flat[:, t * NT:(t + 1) * NT], ACT.Copy).then_inc(s["copied"], 1)
            act.activation(ones_f[:, 0:1], ones_f[:, 1:2], ACT.Copy).then_inc(s["all_copied"], 1)
            act.wait_ge(s["emb_ready"], 1)
            act.activation(halves(k.et[:, 0, 0, :]), k.pair[3][:, :, 0:HN], ACT.Copy).then_inc(s["emb_hi"], 1)

        @block.tensor
        def _(pe):
            def count(u, seq, first, last):
                pe.wait_ge(s["hot"], seq + 1)
                for t, c0, c1, opens in pieces:
                    mm = pe.matmul(flat[:, c0:c1], src_hot[:, u, t * P:(t + 1) * P],
                                   dst_hot[:, u, c0 - t * NT:c1 - t * NT], start=(first and opens), stop=last,
                                   skip_group_check=True)
                return mm

            def count_all(r):
                for u in range(UNROLL):
                    count(u, r * ET + u, u == 0, False).then_inc(s["tile_mm"], 1)
                with pe.Fori(1, ET // UNROLL - 1) as g:
                    for u in range(UNROLL):
                        count(u, g * UNROLL + (r * ET + u), False, False).then_inc(s["tile_mm"], 1)
                for u in range(UNROLL):
                    count(u, r * ET + ET - UNROLL + u, False, u == UNROLL - 1).then_inc(s["tile_mm"], 1)

            count_all(0)
            pe.wait_ge(s["ones_made"], 2)
            pe.wait_ge(s["copied"], TT)
            for r in range(RELS):
                for t in range(TT):
                    for h in range(2):
                        pe.matmul(k.pair[0][:, h, 0:HN], ones[:], k.C[:, r, t, h * HN:(h + 1) * HN],
                                  start=(r == 0 and t == 0), stop=(r == RELS - 1 and t == TT - 1))
            pe.wait_ge(s["over_made"], 1)
            pe.matmul(k.banks[7][:, 0:2], ones[:], over[:], start=True, stop=True).then_inc(s["check_mm"], 1)
            pe.wait_ge(s["rounds_made"], 1)
            again = pe.value_load(rounds[0:1, 0:1], min_val=0, max_val=RELS)
            with pe.Fori(0, again) as r:
                pe.wait_ge(s["copied"], r * TT + TT)
                count_all(r + 1)
            pe.wait_ge(s["all_copied"], 1)
            for r in range(RELS):
                for t in range(TT):
                    for h in range(2):
                        mm = pe.matmul(k.pair[r][:, h, 0:HN], ones[:], k.C[:, r, t, h * HN:(h + 1) * HN],
                                       start=(t == 0), stop=(t == TT - 1))
                mm.then_inc(s["sum_mm"], 1)
            pe.wait_ge(s["emb_made"], 1)
            for h in range(2):
                mm = pe.matmul(k.pair[3][:, h, 0:HN], emb_sb[:], onehot[:, h * HN:(h + 1) * HN], start=True, stop=True)
            mm.then_inc(s["emb_ready"], 1)



def phase_rgcn(k, name, h_in, h_out, w_rel, w_root, bias):
    d_in, d_out = w_root.shape
    kt, mt = d_in // P, d_out // P
    cuts = [(c, min(256, d_out - c)) for c in range(0, d_out, 256)]
    chunks = [(kt, w, [(0, w, weight_view(m)[:, :, c:c + w])])
              for c, w in cuts for m in (w_rel[0], w_rel[1], w_rel[2], w_root)]
    with ExitStack() as ctx:
        k.begin(ctx)
        st = Stream(k, f"{name}_w", chunks, kt * 256, 2, 2)
        y = k.sb(f"{name}_y", [P, 2, TT, 2, 256], F32R)
        room = k.a[:].rearrange("p t d -> p (t d)")
        acc = room[:, RELS * NT:(RELS + 2) * NT].rearrange("p (m n) -> p m n", m=2)
        part = room[:, (RELS + 2) * NT:(RELS + 3) * NT]
        b = k.sb(f"{name}_b", [P, mt], F32)
        s = signals(k, name, (
            "small", "chain", "y_mm", "y_hi", "y_lo", "g_mm", "g_read", "h_f", "h_hi", "h_lo"))
        jobs = [(kind, c, r) for c in range(len(cuts))
                for kind, r in (("Y", 0), ("Y", 1), ("G", 0), ("Y", 2), ("G", 1), ("R", 3), ("G", 2))]
        y_at = {(c, r): RELS * c + r for c in range(len(cuts)) for r in range(RELS)}
        g_at, g_count = {}, 0
        for kind, c, r in jobs:
            if kind != "Y":
                g_at[c, r] = g_count
                g_count += cuts[c][1] // P
        for c in range(len(cuts)):
            for r in range(RELS):
                st.freed[4 * c + r] = (s["y_mm"], TT * (y_at[c, r] + 1))
            st.freed[4 * c + 3] = (s["g_mm"], g_at[c, 3] + cuts[c][1] // P)
        block = ctx.enter_context(k.nc.Block())

        @block.sync
        def _(sp):
            sp.dma_start(b[:], bias.rearrange("(m p) -> p m", p=P), allow_slow_non_contiguous=True).then_inc(s["small"], 16)
            stream_loads(sp, st)

        @block.gpsimd
        def _(pool):
            k.clear_last(pool)
            stream_splits(pool, st)

        @block.tensor
        def _(pe):
            for kind, c, r in jobs:
                w = cuts[c][1]
                if kind == "Y":
                    pe.wait_ge(st.lo_done, 4 * c + r + 1)
                    wh = st.views(4 * c + r)
                    for t in range(TT):
                        i = TT * y_at[c, r] + t
                        if i >= 3:
                            pe.wait_ge(s["y_lo"], i - 2)
                        for j in range(kt):
                            mm = split_product(pe, k.banks[i % 3][0:TS[t], 0:w],
                                               [h_in(j)[:, a, t * P:t * P + TS[t]] for a in range(2)],
                                               [v[:, j, :] for v in wh], j == 0, j == kt - 1)
                        mm.then_inc(s["y_mm"], 1)
                    continue
                for m in range(w // P):
                    i = g_at[c, r] + m
                    pair = k.pair[2 + i % 2]
                    if i >= 2:
                        pe.wait_ge(s["g_read"], i - 1)
                    if kind == "G":
                        v = y_at[c, r]
                        pe.wait_ge(s["y_lo"], TT * (v + 1))
                        for t in range(TT):
                            for a in range(2):
                                for h in range(2):
                                    mm = pe.matmul(pair[:, h, 0:HN], y[0:TS[t], v % 2, t, a, m * P:(m + 1) * P],
                                                   k.C[0:TS[t], r, t, h * HN:(h + 1) * HN],
                                                   start=(t == 0 and a == 0), stop=(t == TT - 1 and a == 1))
                    else:
                        pe.wait_ge(st.lo_done, 4 * c + 4)
                        wh = st.views(4 * c + 3)
                        for j in range(kt):
                            mm = split_product_wide(pe, pair, [v[:, j, m * P:(m + 1) * P] for v in wh],
                                                    lambda b_, h: h_in(j)[:, b_, h * HN:(h + 1) * HN], j == 0, j == kt - 1)
                    mm.then_inc(s["g_mm"], 1)

        @block.scalar
        def _(act):
            for kind, c, r in jobs:
                w = cuts[c][1]
                if kind == "Y":
                    v = y_at[c, r]
                    if v >= 2:
                        pc, pr = divmod(v - 2, RELS)
                        act.wait_ge(s["g_mm"], g_at[pc, pr] + cuts[pc][1] // P)
                    for t in range(TT):
                        i = TT * v + t
                        act.wait_ge(s["y_mm"], i + 1)
                        act.activation(y[0:TS[t], v % 2, t, 0, 0:w], k.banks[i % 3][0:TS[t], 0:w], ACT.Copy).then_inc(s["y_hi"], 1)
                elif kind == "G" and r == 2:
                    for m in range(w // P):
                        i = 2 * c + m
                        act.wait_ge(s["h_f"], i + 1)
                        act.activation(h_out(i)[:, 0, :], acc[:, m, :], ACT.Copy).then_inc(s["h_hi"], 1)

        @block.vector
        def _(dve):
            link = Link(dve, s["chain"])
            dve.wait_ge(s["small"], 16)
            for kind, c, r in jobs:
                w = cuts[c][1]
                if kind == "Y":
                    v = y_at[c, r]
                    for t in range(TT):
                        i = TT * v + t
                        dve.wait_ge(s["y_hi"], i + 1)
                        dve.tensor_tensor(y[0:TS[t], v % 2, t, 1, 0:w], k.banks[i % 3][0:TS[t], 0:w],
                                          y[0:TS[t], v % 2, t, 0, 0:w].bitcast(F32), ALU.subtract).then_inc(s["y_lo"], 1)
                    continue
                for m in range(w // P):
                    i = g_at[c, r] + m
                    src = k.pair[2 + i % 2][:, :, 0:HN]
                    sum_ = acc[:, m, :]
                    dve.wait_ge(s["g_mm"], i + 1)
                    if kind == "G" and r == 0:
                        if c > 0:
                            dve.wait_ge(s["h_lo"], 2 * (c - 1) + m + 1)
                        dve.tensor_tensor(halves(sum_), src, halves(k.inv[:, r, :]), ALU.mult).then_inc(s["g_read"], 1)
                        dve.wait_ge(s["g_read"], i + 1)
                    elif kind == "G":
                        dve.tensor_tensor(halves(part), src, halves(k.inv[:, r, :]), ALU.mult).then_inc(s["g_read"], 1)
                        dve.wait_ge(s["g_read"], i + 1)
                        link(dve.tensor_tensor(sum_, sum_, part, ALU.add))
                    else:
                        dve.scalar_tensor_tensor(halves(sum_), src, b[:, 2 * c + m:2 * c + m + 1], halves(sum_),
                                                 ALU.add, ALU.add).then_inc(s["g_read"], 1)
                        dve.wait_ge(s["g_read"], i + 1)
                    if kind == "G" and r == 2:
                        dve.tensor_scalar(sum_, sum_, 0.0, None, ALU.max).then_inc(s["h_f"], 1)
                        if m == w // P - 1:
                            for m2 in range(w // P):
                                o = 2 * c + m2
                                dve.wait_ge(s["h_hi"], o + 1)
                                dve.tensor_tensor(h_out(o)[:, 1, :], acc[:, m2, :], h_out(o)[:, 0, :].bitcast(F32),
                                                  ALU.subtract).then_inc(s["h_lo"], 1)


def phase_add_turned(k, name, h):
    with ExitStack() as ctx:
        k.begin(ctx)
        whole = k.sb(f"{name}_whole", [P, 2, NT], F32)
        s = signals(k, name, ("whole", "turned", "added"))
        block = ctx.enter_context(k.nc.Block())

        @block.gpsimd
        def _(pool):
            k.clear_last(pool)

        @block.vector
        def _(dve):
            def add(j):
                dve.wait_ge(s["turned"], j + 1)
                for t in range(TT):
                    x = k.x[0:TS[t], t, j * P:(j + 1) * P]
                    src = k.banks[2 * (j % 2) + t // 4][0:TS[t], (t % 4) * P:(t % 4 + 1) * P]
                    ins = dve.tensor_tensor(x, src, x, ALU.add)
                ins.then_inc(s["added"], 1)

            for j in range(KD):
                if j >= 2:
                    dve.wait_ge(s["turned"], j - 1)
                dve.tensor_tensor(whole[:, j % 2, :], h(j)[:, 0, :].bitcast(F32), h(j)[:, 1, :].bitcast(F32),
                                  ALU.add).then_inc(s["whole"], 1)
                if j >= 1:
                    add(j - 1)
            add(KD - 1)

        @block.tensor
        def _(pe):
            for j in range(KD):
                pe.wait_ge(s["whole"], j + 1)
                if j >= 2:
                    pe.wait_ge(s["added"], j - 1)
                for t in range(TT):
                    mm = pe.transpose(k.banks[2 * (j % 2) + t // 4][0:TS[t], (t % 4) * P:(t % 4 + 1) * P],
                                      whole[:, j % 2, t * P:t * P + TS[t]], k.ident[:])
                mm.then_inc(s["turned"], 1)


def phase_save(k, name):
    with ExitStack() as ctx:
        k.begin(ctx)
        saved = k.sem(f"{name}_saved")
        k.x_dram = k.nc.dram_tensor("x_dram", (NODES, D), F32).ap()
        block = ctx.enter_context(k.nc.Block())

        @block.gpsimd
        def _(pool):
            k.clear_last(pool)

        @block.sync
        def _(sp):
            for t in range(TT):
                sp.dma_start(k.x_dram[t * P:t * P + TS[t], :], k.x[0:TS[t], t, :]).then_inc(saved, 16)
            sp.wait_ge(saved, 16 * TT)


def gnn_block(k, I):
    with ExitStack() as ctx:
        k.enter(ctx)
        k.et = k.sb("et_sb", [P, 1, 2, NT], F32R)
        k.C = k.sb("counts", [P, RELS, TT, NT], F32R)
        k.inv = k.a[:].rearrange("p t d -> p (t d)")[:, 0:RELS * NT].rearrange("p (r n) -> p r n", r=RELS)
        k.total_dram = k.nc.dram_tensor("count_total_dram", (P, TT * NT), F32).ap()
        phase_counts(k, I["src"], I["dst"], I["edge_type_3"], I["L0_gnn_node_emb"], I["node_type_3"])
        k.enter(ctx)
        hb = k.sb("h_b", [P, K1, 2, NT], F32R)
        first = lambda j: k.xt[:, j, :, :] if j < KD else k.et[:, 0, :, :]
        second = lambda j: hb[:, j, :, :]
        phase_rgcn(k, "g1", first, second, I["L0_gnn_w_rel1"], I["L0_gnn_w_root1"], I["L0_gnn_b1"])
        phase_rgcn(k, "g2", second, first, I["L0_gnn_w_rel2"], I["L0_gnn_w_root2"], I["L0_gnn_b2"])
        phase_rgcn(k, "g3", first, second, I["L0_gnn_w_rel3"], I["L0_gnn_w_root3"], I["L0_gnn_b3"])
        phase_add_turned(k, "g4", second)



EMBEDS = (384, 576, 768)
RATIOS = (2, 3, 4)
assert all(r * e >= H_FF for r in RATIOS for e in EMBEDS)
GELU_C = float(np.sqrt(2.0 / np.pi))


def phase_ffn(k, name, w_fc, b_fc, w_proj, b_proj, alpha_e, alpha_r):
    with ExitStack() as ctx:
        k.begin(ctx)
        al = k.sb(f"{name}_al", [P, 6], F32)
        sum_r = k.sb(f"{name}_sum_r", [P, 1], F32)
        coef = k.sb(f"{name}_coef", [P, 3], F32)
        fc = k.sb(f"{name}_fc", [HP, 2, D], F32)
        pr = k.sb(f"{name}_pr", [P, KD, H_FF], F32)
        w0f = k.sb(f"{name}_w0f", [P, KD, H_FF], F32)
        w0 = k.sb(f"{name}_w0", [P, 2, KD, H_FF], F32R)
        w1f = k.sb(f"{name}_w1f", [HP, 2, D], F32)
        w1 = k.sb(f"{name}_w1", [HP, 2, 2, D], F32R)
        bf = k.sb(f"{name}_bf", [HP, 2], F32)
        bp = k.sb(f"{name}_bp", [P, D], F32)
        hf = k.sb(f"{name}_hf", [HP, 2, NT], F32)
        g1 = k.sb(f"{name}_g1", [HP, 2, NT], F32)
        g2 = k.sb(f"{name}_g2", [HP, 2, NT], F32)
        h = k.sb(f"{name}_h", [HP, 2, 2, NT], F32R)
        s = signals(k, name, (
            "loaded", "chain", "scaled", "turned", "w_f", "w_hi", "w_lo", "h_mm", "g_in", "g_tanh", "h_f", "h_hi",
            "h_lo", "o_mm", "o_read"))
        block = ctx.enter_context(k.nc.Block())

        @block.gpsimd
        def _(pool):
            k.clear_last(pool)
        fc_t = k.psum[:, 0:3, :]
        pr_t = [k.psum[0:HP, 3 + 2 * g:5 + 2 * g, 0:384] for g in range(2)]

        @block.sync
        def _(sp):
            sp.dma_start(al[:, 0:3], alpha_e.partition_broadcast(P)).then_inc(s["loaded"], 16)
            sp.dma_start(al[:, 3:6], alpha_r.partition_broadcast(P)).then_inc(s["loaded"], 16)
            sp.dma_start(fc[:], w_fc.rearrange("(g p) d -> p g d", p=HP)).then_inc(s["loaded"], 16)
            sp.dma_start(pr[:], w_proj.rearrange("(k p) h -> p k h", p=P)).then_inc(s["loaded"], 16)
            sp.dma_start(bf[:], b_fc.rearrange("(g p) -> p g", p=HP), allow_slow_non_contiguous=True).then_inc(s["loaded"], 16)
            sp.dma_start(bp[:], b_proj.partition_broadcast(P)).then_inc(s["loaded"], 16)

        @block.vector
        def _(dve):
            link = Link(dve, s["chain"])
            spans = ((0, EMBEDS[0]), (EMBEDS[0], EMBEDS[1]), (EMBEDS[1], EMBEDS[2]))
            dve.wait_ge(s["loaded"], 16 * 6)
            link(dve.tensor_reduce(sum_r[:], al[:, 3:6], AX.X, ALU.add))
            link(dve.tensor_scalar(coef[:], al[:, 0:3], sum_r[:, 0:1], None, ALU.mult))
            link(dve.tensor_tensor(coef[:, 1:2], coef[:, 1:2], coef[:, 2:3], ALU.add))
            link(dve.tensor_tensor(coef[:, 0:1], coef[:, 0:1], coef[:, 1:2], ALU.add))
            for i, (c0, c1) in enumerate(spans):
                dve.tensor_scalar(bp[:, c0:c1], bp[:, c0:c1], coef[:, i:i + 1], None, ALU.mult)
                ins = dve.tensor_scalar(fc[:, :, c0:c1], fc[:, :, c0:c1], coef[0:HP, i:i + 1], None, ALU.mult)
            link(ins)
            link(dve.tensor_scalar(bf[:], bf[:], coef[0:HP, 0:1], None, ALU.mult))
            ins = dve.tensor_copy(g1[:, 0, 0:1], coef[0:HP, 0:1])
            ins.then_inc(s["scaled"], 1)
            for t in range(TT):
                ins = dve.tensor_tensor(k.x[0:TS[t], t, :], k.x[0:TS[t], t, :], bp[0:TS[t], :], ALU.add)
            link(ins)
            dve.wait_ge(s["turned"], 1)
            for j in range(3):
                dve.tensor_copy(w0f[:, 2 * j:2 * j + 2, :].rearrange("p k h -> p (k h)"), fc_t[:, j, 0:2 * H_FF])
            for g in range(2):
                w = w1f[:, g, :]
                link(dve.tensor_copy(w.rearrange("p (b n) -> p b n", b=2), pr_t[g]))
                for i, (c0, c1) in enumerate(spans):
                    ins = dve.tensor_scalar(w[:, c0:c1], w[:, c0:c1], coef[0:HP, i:i + 1], None, ALU.mult)
            ins.then_inc(s["w_f"], 1)
            dve.wait_ge(s["w_hi"], 2)
            dve.tensor_tensor(w0[:, 1, :, :], w0f[:], w0[:, 0, :, :].bitcast(F32), ALU.subtract).then_inc(s["w_lo"], 1)
            dve.tensor_tensor(w1[:, 1, :, :], w1f[:], w1[:, 0, :, :].bitcast(F32), ALU.subtract).then_inc(s["w_lo"], 1)
            for g in range(2):
                dve.wait_ge(s["h_mm"], g + 1)
                link(dve.tensor_scalar(halves(hf[:, g, :]), k.pair[g][0:HP, :, 0:HN], bf[:, g:g + 1], None, ALU.add))
                link(dve.tensor_tensor(g1[:, g, :], hf[:, g, :], hf[:, g, :], ALU.mult))
                link(dve.tensor_scalar(g1[:, g, :], g1[:, g, :], 0.044715, 1.0, ALU.mult, ALU.add))
                dve.tensor_tensor(g1[:, g, :], g1[:, g, :], hf[:, g, :], ALU.mult).then_inc(s["g_in"], 1)
            for g in range(2):
                dve.wait_ge(s["g_tanh"], g + 1)
                link(dve.tensor_scalar(g2[:, g, :], g2[:, g, :], 0.5, 0.5, ALU.mult, ALU.add))
                dve.tensor_tensor(hf[:, g, :], hf[:, g, :], g2[:, g, :], ALU.mult).then_inc(s["h_f"], 1)
            for g in range(2):
                dve.wait_ge(s["h_hi"], g + 1)
                dve.tensor_tensor(h[:, g, 1, :], hf[:, g, :], h[:, g, 0, :].bitcast(F32), ALU.subtract).then_inc(s["h_lo"], 1)
            for i in range(2 * TT):
                t, c = divmod(i, 2)
                x = k.x[0:TS[t], t, c * 384:(c + 1) * 384]
                dve.wait_ge(s["o_mm"], i + 1)
                dve.tensor_tensor(x, k.banks[4 + i % 2][0:TS[t], 0:384], x, ALU.add).then_inc(s["o_read"], 1)

        @block.scalar
        def _(act):
            act.wait_ge(s["w_f"], 1)
            act.activation(w0[:, 0, :, :], w0f[:], ACT.Copy).then_inc(s["w_hi"], 1)
            act.activation(w1[:, 0, :, :], w1f[:], ACT.Copy).then_inc(s["w_hi"], 1)
            for g in range(2):
                act.wait_ge(s["g_in"], g + 1)
                act.activation(g2[:, g, :], g1[:, g, :], ACT.Tanh, scale=GELU_C).then_inc(s["g_tanh"], 1)
            for g in range(2):
                act.wait_ge(s["h_f"], g + 1)
                act.activation(h[:, g, 0, :], hf[:, g, :], ACT.Copy).then_inc(s["h_hi"], 1)

        @block.tensor
        def _(pe):
            pe.wait_ge(s["scaled"], 1)
            for j in range(KD):
                for g in range(2):
                    c0 = (j % 2) * H_FF + g * HP
                    pe.transpose(fc_t[:, j // 2, c0:c0 + HP], fc[:, g, j * P:(j + 1) * P], k.ident[0:HP, 0:HP])
            for g in range(2):
                for j in range(KD):
                    mm = pe.transpose(pr_t[g][:, j // 3, (j % 3) * P:(j % 3 + 1) * P], pr[:, j, g * HP:(g + 1) * HP],
                                      k.ident[:])
            mm.then_inc(s["turned"], 1)
            pe.wait_ge(s["w_lo"], 2)
            for g in range(2):
                for j in range(KD):
                    mm = split_product_wide(pe, k.pair[g][0:HP], [w0[:, a, j, g * HP:(g + 1) * HP] for a in range(2)],
                                            lambda b, hh: k.xt[:, j, b, hh * HN:(hh + 1) * HN], j == 0, j == KD - 1)
                mm.then_inc(s["h_mm"], 1)
            pe.wait_ge(s["h_lo"], 2)
            for i in range(2 * TT):
                t, c = divmod(i, 2)
                if i >= 2:
                    pe.wait_ge(s["o_read"], i - 1)
                for g in range(2):
                    mm = split_product(pe, k.banks[4 + i % 2][0:TS[t], 0:384],
                                       [h[:, g, a, t * P:t * P + TS[t]] for a in range(2)],
                                       [w1[:, a, g, c * 384:(c + 1) * 384] for a in range(2)], g == 0, g == 1)
                mm.then_inc(s["o_mm"], 1)



def phase_gcn(k, name, w, bias):
    chunks = [one_chunk(w, 256, c * 256) for c in range(3)]
    with ExitStack() as ctx:
        k.begin(ctx)
        st = Stream(k, f"{name}_w", chunks, WE_MIX, 2, 3)
        total = k.sb(f"{name}_total", [P, TT, NT], F32)
        adj = k.sb(f"{name}_adj", [P, TT, NT], F32R)
        ones = k.sb(f"{name}_ones", [P, 2], F32)
        y = k.sb(f"{name}_y", [P, TT, 2, D], F32R)
        yf = k.sb(f"{name}_yf", [P, 2, 256], F32)
        bp = k.sb(f"{name}_bp", [P, D], F32)
        s = signals(k, name, (
            "loaded", "chain", "ones_made", "deg_mm", "var_ready", "root_ready", "looped", "adj_made", "y_mm", "y_f",
            "y_hi", "y_lo", "o_mm", "o_read"))
        st.freed.update({c: (s["y_mm"], TT * (c + 1)) for c in range(3)})
        block = ctx.enter_context(k.nc.Block())

        @block.sync
        def _(sp):
            sp.dma_start(total[:].rearrange("p t n -> p (t n)"), k.total_dram).then_inc(s["loaded"], 16)
            sp.dma_start(bp[:], bias.partition_broadcast(P)).then_inc(s["loaded"], 16)
            stream_loads(sp, st)

        @block.gpsimd
        def _(pool):
            k.clear_last(pool)
            stream_splits(pool, st)

        @block.vector
        def _(dve):
            link = Link(dve, s["chain"])
            link(dve.memset(ones[:], 1.0))
            dve.wait_ge(s["loaded"], 32)
            for t in range(TT):
                ts = TS[t]
                ins = dve.tensor_tensor(total[0:ts, t, t * P:t * P + ts], total[0:ts, t, t * P:t * P + ts],
                                        k.ident[0:ts, 0:ts], ALU.add)
            ins.then_inc(s["looped"], 1)
            for t in range(TT):
                ins = dve.tensor_tensor(k.x[0:TS[t], t, :], k.x[0:TS[t], t, :], bp[0:TS[t], :], ALU.add)
            link(ins)
            dve.wait_ge(s["deg_mm"], 1)
            link(dve.memset(k.ve[:], 1.0))
            for t in range(TT):
                ins = dve.tensor_copy(k.ve[0:TS[t], t:t + 1], k.banks[7][0:TS[t], 2 * t:2 * t + 1])
            link(ins)
            rsqrt_of_ve(dve, link, k, s)

            def y_low(i):
                c, t = divmod(i, TT)
                dve.wait_ge(s["y_hi"], i + 1)
                dve.tensor_tensor(y[0:TS[t], t, 1, c * 256:(c + 1) * 256], yf[0:TS[t], i % 2, :],
                                  y[0:TS[t], t, 0, c * 256:(c + 1) * 256].bitcast(F32), ALU.subtract).then_inc(s["y_lo"], 1)

            for i in range(3 * TT):
                c, t = divmod(i, TT)
                dve.wait_ge(s["y_mm"], i + 1)
                if i >= 2:
                    dve.wait_ge(s["y_lo"], i - 1)
                dve.tensor_scalar(yf[0:TS[t], i % 2, :], k.banks[i % 2][0:TS[t], 0:256], k.rstd[0:TS[t], t:t + 1], None,
                                  ALU.mult).then_inc(s["y_f"], 1)
                if i >= 1:
                    y_low(i - 1)
            y_low(3 * TT - 1)
            for i in range(2 * TT):
                t, c = divmod(i, 2)
                x = k.x[0:TS[t], t, c * 384:(c + 1) * 384]
                dve.wait_ge(s["o_mm"], i + 1)
                dve.scalar_tensor_tensor(x, k.banks[2 + i % 2][0:TS[t], 0:384], k.rstd[0:TS[t], t:t + 1], x,
                                         ALU.mult, ALU.add).then_inc(s["o_read"], 1)

        @block.scalar
        def _(act):
            act.wait_ge(s["looped"], 1)
            act.activation(adj[:], total[:], ACT.Copy).then_inc(s["adj_made"], 1)
            act.wait_ge(s["var_ready"], 1)
            act.activation(k.root[:], k.ve[:], ACT.Sqrt).then_inc(s["root_ready"], 1)
            for i in range(3 * TT):
                c, t = divmod(i, TT)
                act.wait_ge(s["y_f"], i + 1)
                act.activation(y[0:TS[t], t, 0, c * 256:(c + 1) * 256], yf[0:TS[t], i % 2, :], ACT.Copy).then_inc(s["y_hi"], 1)

        @block.tensor
        def _(pe):
            pe.wait_ge(s["looped"], 1)
            for t in range(TT):
                for u in range(TT):
                    mm = pe.matmul(k.banks[7][0:TS[t], 2 * t:2 * t + 2], total[0:TS[u], u, t * P:t * P + TS[t]],
                                   ones[0:TS[u], :], start=(u == 0), stop=(u == TT - 1))
            mm.then_inc(s["deg_mm"], 1)
            for c in range(3):
                pe.wait_ge(st.lo_done, c + 1)
                wh = st.views(c)
                for t in range(TT):
                    i = c * TT + t
                    if i >= 2:
                        pe.wait_ge(s["y_f"], i - 1)
                    for j in range(KD):
                        mm = split_product(pe, k.banks[i % 2][0:TS[t], 0:256],
                                           [k.xt[:, j, a, t * P:t * P + TS[t]] for a in range(2)],
                                           [v[:, j, :] for v in wh], j == 0, j == KD - 1)
                    mm.then_inc(s["y_mm"], 1)
            pe.wait_ge(s["adj_made"], 1)
            pe.wait_ge(s["y_lo"], 3 * TT)
            for i in range(2 * TT):
                t, c = divmod(i, 2)
                if i >= 2:
                    pe.wait_ge(s["o_read"], i - 1)
                for u in range(TT):
                    for a in range(2):
                        mm = pe.matmul(k.banks[2 + i % 2][0:TS[t], 0:384], adj[0:TS[u], u, t * P:t * P + TS[t]],
                                       y[0:TS[u], u, a, c * 384:(c + 1) * 384],
                                       start=(u == 0 and a == 0), stop=(u == TT - 1 and a == 1))
                mm.then_inc(s["o_mm"], 1)



CAP = 320
assert CAP % 2 == 0 and 2 * CAP >= NODES
OVER = 2 * NODES // (CAP + 1)
JOBS = EXPERTS + OVER
JC = JOBS + 1
MARK = 1024.0
assert MARK - CAP > NODES or MARK > NODES
ST = (P, P, CAP - 2 * P)


def phase_router(k, name, w_router, bias):
    with ExitStack() as ctx:
        k.begin(ctx)
        wf = k.sb(f"{name}_wf", [P, KD, EXPERTS], F32)
        w = k.sb(f"{name}_w", [P, 2, KD, EXPERTS], F32R)
        b = k.sb(f"{name}_b", [P, EXPERTS], F32)
        logits = k.sb(f"{name}_logits", [P, TT, EXPERTS], F32)
        top = k.sb(f"{name}_top", [P, TT, 8], F32)
        at_i = k.sb(f"{name}_at_i", [P, TT, 8], U32)
        at_f = k.sb(f"{name}_at_f", [P, TT, 8], F32)
        iota_i = k.sb(f"{name}_iota_i", [P, CAP], I32)
        iota = k.sb(f"{name}_iota", [P, EXPERTS], F32)
        slot_i = k.sb(f"{name}_slot_i", [P, len(ST)], I32)
        hot = k.sb(f"{name}_hot", [P, TT, 4, EXPERTS], F32)
        gap = k.sb(f"{name}_gap", [P, TT], F32)
        ex = k.sb(f"{name}_ex", [P, TT], F32)
        den = k.sb(f"{name}_den", [P, TT], F32)
        wt = k.sb(f"{name}_wt", [P, 2, TT], F32)
        sel = k.sb(f"{name}_sel", [P, TT, EXPERTS], F32)
        selb = k.sb(f"{name}_selb", [P, TT, EXPERTS], BF16)
        ones = k.sb(f"{name}_ones", [P, P], BF16)
        weight = k.sb(f"{name}_weight", [P, TT, JC], F32)
        over = k.sb(f"{name}_over", [P, EXPERTS], F32)
        before = k.sb(f"{name}_before", [P, EXPERTS + 1], F32)
        which = k.sb(f"{name}_which", [P, OVER, EXPERTS], F32)
        prod = k.sb(f"{name}_prod", [P, 4, TT, EXPERTS], F32)
        seen = k.sb(f"{name}_seen", [P, TT], F32)
        expert_f = k.sb(f"{name}_expert_f", [P, JC], F32)
        count_f = k.sb(f"{name}_count_f", [P, 1], F32)
        s = signals(k, name, (
            "loaded", "chain", "iota_made", "later_made", "w_hi", "w_lo", "mm", "gap_made", "ex_made", "sel_made",
            "rank_mm", "weight_made", "weight_hi"))
        block = ctx.enter_context(k.nc.Block())

        @block.sync
        def _(sp):
            sp.dma_start(wf[:], weight_view(w_router)).then_inc(s["loaded"], 16)
            sp.dma_start(b[:], bias.partition_broadcast(P)).then_inc(s["loaded"], 16)

        @block.gpsimd
        def _(pool):
            k.clear_last(pool)
            pool.iota(iota_i[:], [[1, CAP]], base=0, channel_multiplier=0)
            pool.iota(slot_i[:], [[P, len(ST)]], base=int(MARK), channel_multiplier=1).then_inc(s["iota_made"], 1)
            pool.memset(k.later[:], 1.0).then_inc(s["later_made"], 1)
            pool.wait_ge(s["later_made"], 1)
            pool.affine_select(out=k.later[:], in_=k.later[:], compare_op=ALU.is_gt, fill=0.0, base=0,
                               pattern=[[-P, TT], [1, NT]], channel_multiplier=-1).then_inc(s["later_made"], 1)
            pool.wait_ge(s["later_made"], 2)
            pool.affine_select(out=k.later[:], in_=k.later[:], compare_op=ALU.not_equal, fill=MARK, base=0,
                               pattern=[[-P, TT], [1, NT]], channel_multiplier=-1).then_inc(s["later_made"], 1)

        @block.scalar
        def _(act):
            act.wait_ge(s["loaded"], 32)
            act.activation(w[:, 0, :, :], wf[:], ACT.Copy).then_inc(s["w_hi"], 1)
            act.wait_ge(s["gap_made"], 1)
            act.activation(ex[:], gap[:], ACT.Exp).then_inc(s["ex_made"], 1)
            act.wait_ge(s["weight_made"], 1)
            act.activation(k.job_w[:, :, :, 0], weight[:], ACT.Copy).then_inc(s["weight_hi"], 1)

        @block.tensor
        def _(pe):
            pe.wait_ge(s["w_lo"], 1)
            for t in range(TT):
                for j in range(KD):
                    mm = split_product(pe, k.banks[0][0:TS[t], t * EXPERTS:(t + 1) * EXPERTS],
                                       [k.xt[:, j, a, t * P:t * P + TS[t]] for a in range(2)],
                                       [w[:, a, j, :] for a in range(2)], j == 0, j == KD - 1)
            mm.then_inc(s["mm"], 1)
            pe.wait_ge(s["later_made"], 3)
            pe.wait_ge(s["sel_made"], 1)
            for t in range(TT):
                for u in range(t + 1):
                    pe.matmul(k.banks[1][0:TS[t], t * EXPERTS:(t + 1) * EXPERTS], k.later[0:TS[u], u, t * P:t * P + TS[t]],
                              selb[0:TS[u], u, :], start=(u == 0), stop=(u == t))
            for u in range(TT):
                mm = pe.matmul(k.banks[2][:, 0:EXPERTS], ones[0:TS[u], :], selb[0:TS[u], u, :],
                               start=(u == 0), stop=(u == TT - 1))
            mm.then_inc(s["rank_mm"], 1)

        @block.vector
        def _(dve):
            link = Link(dve, s["chain"])
            dve.memset(logits[:], 0.0)
            dve.memset(ones[:], 1.0)
            dve.memset(weight[:], 0.0)
            dve.memset(k.job_rank[:], 0.0)
            dve.memset(k.job_sel[:], 0.0)
            dve.memset(k.job_off[:], 0.0)
            dve.memset(before[:], 0.0)
            link(dve.memset(expert_f[:], 0.0))
            dve.wait_ge(s["iota_made"], 1)
            dve.tensor_copy(iota[:], iota_i[:, 0:EXPERTS])
            dve.tensor_scalar(k.iota_slot[:], iota_i[:], MARK, None, ALU.add)
            link(dve.tensor_copy(k.slot_id[:], slot_i[:]))
            dve.wait_ge(s["w_hi"], 1)
            dve.tensor_tensor(w[:, 1, :, :], wf[:], w[:, 0, :, :].bitcast(F32), ALU.subtract).then_inc(s["w_lo"], 1)
            dve.wait_ge(s["mm"], 1)
            for t in range(TT):
                ts = TS[t]
                ins = dve.tensor_tensor(logits[0:ts, t, :], k.banks[0][0:ts, t * EXPERTS:(t + 1) * EXPERTS], b[0:ts, :],
                                        ALU.add)
            link(ins)
            for t in range(TT):
                ins = dve.max(top[:, t, :], logits[:, t, :])
            link(ins)
            for t in range(TT):
                ins = dve.max_index(at_i[:, t, :], top[:, t, :], logits[:, t, :])
            link(ins)
            link(dve.tensor_copy(at_f[:], at_i[:]))
            dve.tensor_tensor(gap[:], top[:, :, 1], top[:, :, 0], ALU.subtract).then_inc(s["gap_made"], 1)
            for t in range(TT):
                for r in range(2):
                    ins = dve.tensor_scalar(hot[:, t, r, :], iota[:], at_f[:, t, r:r + 1], None, ALU.is_equal)
            link(ins)
            link(dve.tensor_tensor(sel[:], hot[:, :, 0, :], hot[:, :, 1, :], ALU.add))
            dve.tensor_copy(k.job_sel[:, :, 0:EXPERTS], sel[:])
            dve.tensor_copy(selb[:], sel[:]).then_inc(s["sel_made"], 1)
            dve.wait_ge(s["ex_made"], 1)
            link(dve.tensor_scalar(den[:], ex[:], 1.0, None, ALU.add))
            link(dve.reciprocal(wt[:, 0, :], den[:]))
            link(dve.tensor_tensor(wt[:, 1, :], ex[:], wt[:, 0, :], ALU.mult))
            for t in range(TT):
                for r in range(2):
                    ins = dve.tensor_scalar(hot[:, t, 2 + r, :], hot[:, t, r, :], wt[:, r, t:t + 1], None, ALU.mult)
            link(ins)
            link(dve.tensor_tensor(weight[:, :, 0:EXPERTS], hot[:, :, 2, :], hot[:, :, 3, :], ALU.add))
            dve.wait_ge(s["rank_mm"], 1)
            for t in range(TT):
                dve.tensor_copy(k.job_rank[0:TS[t], t, 0:EXPERTS], k.banks[1][0:TS[t], t * EXPERTS:(t + 1) * EXPERTS])
            dve.tensor_copy(expert_f[:, 0:EXPERTS], iota[:])
            link(dve.tensor_scalar(over[:], k.banks[2][:, 0:EXPERTS], float(CAP), None, ALU.is_gt))
            for e in range(EXPERTS):
                link(dve.tensor_tensor(before[:, e + 1:e + 2], before[:, e:e + 1], over[:, e:e + 1], ALU.add))
            for q in range(OVER):
                j = EXPERTS + q
                link(dve.tensor_scalar(which[:, q, :], before[:, 0:EXPERTS], float(q), None, ALU.is_equal))
                link(dve.tensor_tensor(which[:, q, :], which[:, q, :], over[:], ALU.mult))
                dve.tensor_tensor(prod[:, 0, 0, :], which[:, q, :], iota[:], ALU.mult)
                for i, src in enumerate((k.job_rank[:, :, 0:EXPERTS], weight[:, :, 0:EXPERTS], sel[:])):
                    ins = dve.tensor_tensor(prod[:, 1 + i, :, :], src,
                                            which[:, q:q + 1, :].broadcast_to([P, TT, EXPERTS]), ALU.mult)
                link(ins)
                dve.tensor_reduce(expert_f[:, j:j + 1], prod[:, 0, 0, :], AX.X, ALU.add)
                for i, dst in enumerate((k.job_rank[:, :, j], weight[:, :, j], seen[:])):
                    ins = dve.tensor_reduce(dst, prod[:, 1 + i, :, :], AX.X, ALU.add)
                link(ins)
                link(dve.tensor_copy(k.job_sel[:, :, j], seen[:]))
            dve.tensor_scalar(k.job_rank[:, :, EXPERTS:JOBS], k.job_rank[:, :, EXPERTS:JOBS], -float(CAP), None, ALU.add)
            dve.memset(k.job_off[:, EXPERTS:JOBS], -float(CAP))
            dve.tensor_copy(k.job_expert[:], expert_f[:])
            link(dve.tensor_scalar(count_f[:], before[:, EXPERTS:EXPERTS + 1], float(EXPERTS), None, ALU.add))
            dve.tensor_copy(k.job_count[:], count_f[:]).then_inc(s["weight_made"], 1)
            dve.wait_ge(s["weight_hi"], 1)
            dve.tensor_tensor(k.job_w[:, :, :, 1], weight[:], k.job_w[:, :, :, 0].bitcast(F32), ALU.subtract)



GC = 384
FT = D // P


def phase_shared_expert(k, name, wg, wu, wd):
    RAW, SPL = 3, 4
    CH = 6
    with ExitStack() as ctx:
        k.begin(ctx)
        raw = k.sb(f"{name}_raw", [P, RAW, WE_MOE], F32)
        whi = k.sb(f"{name}_whi", [P, SPL, WE_MOE], F32R)
        wlo = k.sb(f"{name}_wlo", [P, SPL, WE_MOE], F32R)
        ht = k.sb(f"{name}_ht", [P, FT, 2, NT], F32R)
        act_g = k.sb(f"{name}_act_g", [P, 2, NT], F32)
        hf = k.sb(f"{name}_hf", [P, 2, NT], F32)
        s = signals(k, name, (
            "hi_done", "lo_done", "used", "gu_mm", "silu", "hf", "h_hi", "h_lo", "o_mm", "o_read"))
        loaded = [k.sem(f"{name}_loaded{i}") for i in range(RAW)]
        block = ctx.enter_context(k.nc.Block())

        def sources(wg, wu, wd, half):
            c = half * D
            g, u, d = (weight_view(v) for v in (wg, wu, wd))
            dh = d[:, half * FT:(half + 1) * FT, :]
            return [g[:, :, c:c + GC], u[:, :, c:c + GC], g[:, :, c + GC:c + 2 * GC], u[:, :, c + GC:c + 2 * GC],
                    dh[:, :, 0:GC], dh[:, :, GC:2 * GC]]

        def run(eng, unit):
            for half in range(2):
                unit(half, half, half == 0)

        @block.sync
        def _(sp):
            def unit(half, n, first):
                src = sources(wg[0], wu[0], wd[0], half)
                for i in range(CH):
                    if not (first and i < RAW):
                        sp.wait_ge(s["lo_done"], n * CH + (i - RAW + 1))
                    slot = (half * CH + i) % RAW
                    sp.dma_start(raw[:, slot, :].rearrange("p (k c) -> p k c", c=GC), src[i]).then_inc(loaded[slot], 16)

            run(sp, unit)

        @block.gpsimd
        def _(pool):
            k.clear_last(pool)
            def unit(half, n, first):
                for i in range(CH):
                    slot, spl = i % RAW, (half * CH + i) % SPL
                    pool.wait_ge(loaded[slot], n * (16 * CH // RAW) + 16 * (i // RAW + 1))
                    if not (first and i < SPL):
                        pool.wait_ge(s["used"], n * CH + (i - SPL + 1))
                    pool.tensor_tensor(whi[:, spl, :], raw[:, slot, :], k.one[:].broadcast_to([P, WE_MOE]), ALU.mult)\
                        .then_inc(s["hi_done"], 1)
                    pool.wait_ge(s["hi_done"], n * CH + (i + 1))
                    pool.tensor_tensor(wlo[:, spl, :], raw[:, slot, :], whi[:, spl, :].bitcast(F32),
                                       ALU.subtract).then_inc(s["lo_done"], 1)

            run(pool, unit)

        def banks_of(half, f):
            q = (f + half) % 2
            return k.pair[2 * q], k.pair[2 * q + 1]

        def out_bank(half, i):
            return k.banks[4 * ((FT + half) % 2) + i % 4]

        @block.tensor
        def _(pe):
            def views(half, i):
                spl = (half * CH + i) % SPL
                return [w[:, spl, :].rearrange("p (k c) -> p k c", c=GC) for w in (whi, wlo)]

            def unit(half, n, first):
                for c in range(2):
                    for f in range(3 * c, 3 * c + 3):
                        m = f - 3 * c
                        pg, pu = banks_of(half, f)
                        if f >= 2:
                            pe.wait_ge(s["hf"], n * FT + (f - 1))
                        elif not first and f == 0:
                            pe.wait_ge(s["hf"], n * FT)
                        elif not first:
                            pe.wait_ge(s["o_read"], n * (2 * TT))
                        for g, pair in ((0, pg), (1, pu)):
                            if m == 0:
                                pe.wait_ge(s["lo_done"], n * CH + (2 * c + g + 1))
                            wh = views(half, 2 * c + g)
                            for j in range(KD):
                                mm = split_product_wide(pe, pair, [w[:, j, m * P:(m + 1) * P] for w in wh],
                                                        lambda b, h: k.xt[:, j, b, h * HN:(h + 1) * HN],
                                                        j == 0, j == KD - 1)
                            if m == 2:
                                mm.then_inc(s["used"], 1)
                            else:
                                mm.then_inc(s["gu_mm"], 1)
                for c in range(2):
                    pe.wait_ge(s["lo_done"], n * CH + (5 + c))
                    wh = views(half, 4 + c)
                    for t in range(TT):
                        i = c * TT + t
                        if i == 0:
                            pe.wait_ge(s["hf"], n * FT + (FT - 1))
                        if i >= 4:
                            pe.wait_ge(s["o_read"], n * (2 * TT) + (i - 3))
                        for f in range(FT):
                            if i == 0:
                                pe.wait_ge(s["h_lo"], n * FT + (f + 1))
                            mm = split_product(pe, out_bank(half, i)[0:TS[t], 0:GC],
                                               [ht[:, f, a, t * P:t * P + TS[t]] for a in range(2)],
                                               [w[:, f, :] for w in wh], f == 0, f == FT - 1)
                        if t == TT - 1:
                            mm.then_inc(s["used"], 1)
                        else:
                            mm.then_inc(s["o_mm"], 1)

            run(pe, unit)

        def gate_ready(eng, n, f):
            c, m = divmod(f, 3)
            if m == 2:
                eng.wait_ge(s["used"], n * CH + (2 * c + 1))
            else:
                eng.wait_ge(s["gu_mm"], n * 8 + (4 * c + 2 * m + 1))

        def up_ready(eng, n, f):
            c, m = divmod(f, 3)
            if m == 2:
                eng.wait_ge(s["used"], n * CH + (2 * c + 2))
            else:
                eng.wait_ge(s["gu_mm"], n * 8 + (4 * c + 2 * m + 2))

        def out_ready(eng, n, i):
            c, t = divmod(i, TT)
            if t == TT - 1:
                eng.wait_ge(s["used"], n * CH + (5 + c))
            else:
                eng.wait_ge(s["o_mm"], n * (2 * TT - 2) + (c * (TT - 1) + t + 1))

        @block.scalar
        def _(act):
            def unit(half, n, first):
                for f in range(FT):
                    gate_ready(act, n, f)
                    if not (first and f < 2):
                        act.wait_ge(s["hf"], n * FT + (f - 1))
                    act.activation(halves(act_g[:, f % 2, :]), banks_of(half, f)[0][:, :, 0:HN], ACT.Silu).then_inc(s["silu"], 1)
                    act.wait_ge(s["hf"], n * FT + (f + 1))
                    if f == 0 and not first:
                        out_ready(act, n - 1, 2 * TT - 1)
                    act.activation(ht[:, f, 0, :], hf[:, f % 2, :], ACT.Copy).then_inc(s["h_hi"], 1)

            run(act, unit)

        @block.vector
        def _(dve):
            def unit(half, n, first):
                def low(f):
                    dve.wait_ge(s["h_hi"], n * FT + (f + 1))
                    dve.tensor_tensor(ht[:, f, 1, :], hf[:, f % 2, :], ht[:, f, 0, :].bitcast(F32),
                                      ALU.subtract).then_inc(s["h_lo"], 1)

                for f in range(FT):
                    up_ready(dve, n, f)
                    dve.wait_ge(s["silu"], n * FT + (f + 1))
                    if not (first and f < 2):
                        dve.wait_ge(s["h_lo"], n * FT + (f - 1))
                    dve.tensor_tensor(halves(hf[:, f % 2, :]), banks_of(half, f)[1][:, :, 0:HN],
                                      halves(act_g[:, f % 2, :]), ALU.mult).then_inc(s["hf"], 1)
                    low(f)
                for i in range(2 * TT):
                    c, t = divmod(i, TT)
                    ts = TS[t]
                    x = k.x[0:ts, t, c * GC:(c + 1) * GC]
                    out_ready(dve, n, i)
                    if not first:
                        dve.wait_ge(s["o_read"], n * (2 * TT) + (i - 2 * TT + 1))
                    dve.tensor_tensor(x, out_bank(half, i)[0:ts, 0:GC], x, ALU.add).then_inc(s["o_read"], 1)

            run(dve, unit)



HF = F_MOE // 2 // P
RC = 256
OC = D // RC
HC = HF + OC
NC = 2 * HC
OUTS = 2 * OC * len(ST)
WE = KD * RC
RING = 3
assert NC % RING == 0 and HF == KD


def phase_routed_experts(k, name, wg, wu, wd):
    with ExitStack() as ctx:
        k.begin(ctx)
        raw = k.sb(f"{name}_raw", [P, RING, WE], F32)
        whi = k.sb(f"{name}_whi", [P, RING, WE], F32R)
        wlo = k.sb(f"{name}_wlo", [P, RING, WE], F32R)
        xn = k.sb(f"{name}_xn", [P, TT, 2, D], F32R)
        ht = k.sb(f"{name}_ht", [P, HF, 2, CAP], F32R)
        act_g = k.sb(f"{name}_act_g", [P, 2, CAP], F32)
        hf = k.sb(f"{name}_hf", [P, 2, CAP], F32)
        y_hl = k.sb(f"{name}_y_hl", [P, OC, 2, len(ST), RC], F32R)
        sel_b = k.sb(f"{name}_sel_b", [P, TT, P], BF16)
        w_slot = k.sb(f"{name}_w_slot", [P, len(ST)], F32)
        flat = k.xt[:].rearrange("p j a n -> p (j a n)")
        at = [0, KD * 2 * CAP, KD * 2 * CAP + len(ST) * NT, KD * 2 * CAP + len(ST) * NT + TT * CAP]
        xg = flat[:, at[0]:at[1]].rearrange("p (j a n) -> p j a n", j=KD, a=2)
        to_node = flat[:, at[1]:at[2]].rearrange("p (i n) -> p i n", n=NT)
        to_slot = flat[:, at[2]:at[3]].rearrange("p (t n) -> p t n", n=CAP)
        y_all = k.a[:].rearrange("p t d -> p (t d)")
        y0 = y_all[:, 0:len(ST) * D].rearrange("p (c i n) -> p c i n", c=OC, i=len(ST))
        yf = k.sb(f"{name}_yf", [P, len(ST), RC], F32)
        s = signals(k, name, (
            "chain", "split_hi", "xn_ready", "hi_done", "lo_done", "g_mm", "u_mm", "y_mm", "silu", "hf", "h_hi", "h_lo",
            "y_read", "y_hi", "y_lo", "aux_mm", "aux_hi", "aux_read", "slot_made", "sel_made", "mapped"))
        loaded = [k.sem(f"{name}_loaded{i}") for i in range(RING)]
        block = ctx.enter_context(k.nc.Block())

        AUX = 1 + 3 * TT + KD
        AUX_AT = {"map": 0, "scatter0": 1, "scatter1": 1 + TT, "gather": 1 + 2 * TT, "scatter2": 1 + 2 * TT + KD}

        def aux_bank(i):
            return k.banks[6 + (i + 1) % 2]

        def run(eng, body):
            count = eng.value_load(k.job_count[0:1, 0:1], min_val=EXPERTS, max_val=JOBS)
            body(0, True)
            with eng.Fori(1, count) as j:
                body(j, False)

        def is_hidden(i):
            return i % HC < HF

        def wait_chunk_read(eng, j, i):
            half, r = divmod(i, HC)
            if is_hidden(i):
                eng.wait_ge(s["u_mm"], j * (2 * HF) + (half * HF + r + 1))
            else:
                eng.wait_ge(s["y_mm"], j * OUTS + (half * OC + r - HF + 1) * len(ST))

        @block.sync
        def _(sp):
            def body(j, first):
                e = sp.value_load(k.job_expert[0:1, bass.ds(j, 1)], min_val=0, max_val=EXPERTS - 1)
                g, u, d = [v[bass.ds(e, 1)].rearrange("a (q p) f -> p (a q) f", p=P) for v in (wg, wu, wd)]
                for i in range(NC):
                    half, r = divmod(i, HC)
                    slot = i % RING
                    if not (first and i < RING):
                        sp.wait_ge(s["lo_done"], j * NC + (i - RING + 1))
                    if is_hidden(i):
                        c = (half * HF + r) * P
                        dst = raw[:, slot, :].rearrange("p (k c) -> p k c", c=2 * P)
                        sp.dma_start(dst[:, :, 0:P], g[:, :, c:c + P]).then_inc(loaded[slot], 16)
                        sp.dma_start(dst[:, :, P:2 * P], u[:, :, c:c + P]).then_inc(loaded[slot], 16)
                    else:
                        c = (r - HF) * RC
                        dst = raw[:, slot, :].rearrange("p (k c) -> p k c", c=RC)
                        src = d[:, half * HF:(half + 1) * HF, c:c + RC]
                        for a in range(2):
                            sp.dma_start(dst[:, 3 * a:3 * a + 3, :], src[:, 3 * a:3 * a + 3, :])\
                                .then_inc(loaded[slot], 16)

            run(sp, body)

        @block.gpsimd
        def _(pool):
            k.clear_last(pool)

            def body(j, first):
                for i in range(NC):
                    pool.wait_ge(s["hi_done"], j * NC + (i + 1))
                    pool.tensor_tensor(wlo[:, i % RING, :], raw[:, i % RING, :], whi[:, i % RING, :].bitcast(F32),
                                       ALU.subtract).then_inc(s["lo_done"], 1)

            run(pool, body)

        @block.scalar
        def _(act):
            def weights_high(j, i, first):
                slot = i % RING
                act.wait_ge(loaded[slot], j * (32 * NC // RING) + 32 * (i // RING + 1))
                if not (first and i < RING):
                    wait_chunk_read(act, j, i - RING)
                act.activation(whi[:, slot, :], raw[:, slot, :], ACT.Copy).then_inc(s["hi_done"], 1)

            def gather_high(n):
                for q in range(KD):
                    act.wait_ge(s["aux_mm"], n + (q + 1))
                    act.activation(xg[:, q, 0, :], aux_bank(AUX_AT["gather"] + q)[:, 0:CAP], ACT.Copy)\
                        .then_inc(s["aux_hi"], 1)

            def body(j, first):
                for i in range(NC):
                    half, r = divmod(i, HC)
                    if i + 2 < NC:
                        weights_high(j, i + 2, first)
                    if is_hidden(i):
                        f = half * HF + r
                        act.wait_ge(s["g_mm"], j * (2 * HF) + (f + 1))
                        if not (first and f < 2):
                            act.wait_ge(s["hf"], j * (2 * HF) + (f - 1))
                        act.activation(act_g[:, f % 2, :], k.banks[2 * (f % 2)][:, 0:CAP], ACT.Silu)\
                            .then_inc(s["silu"], 1)
                        act.wait_ge(s["hf"], j * (2 * HF) + (f + 1))
                        if r == 0 and not (first and half == 0):
                            act.wait_ge(s["y_mm"], j * OUTS + half * OC * len(ST))
                        act.activation(ht[:, r, 0, :], hf[:, f % 2, :], ACT.Copy).then_inc(s["h_hi"], 1)
                    elif half == 1:
                        c = r - HF
                        if c == 0 and not first:
                            act.wait_ge(s["aux_mm"], j * AUX + KD)
                        act.wait_ge(s["y_read"], j * OUTS + (OC + c + 1) * len(ST))
                        act.activation(y_hl[:, c, 0, :, :], yf[:], ACT.Copy).then_inc(s["y_hi"], 1)
                gather_high(j * AUX + (KD + AUX_AT["gather"]))

            for t in range(TT):
                act.activation(xn[0:TS[t], t, 0, :], k.a[0:TS[t], t, :], ACT.Copy).then_inc(s["split_hi"], 1)
            count = act.value_load(k.job_count[0:1, 0:1], min_val=EXPERTS, max_val=JOBS)
            for i in range(2):
                weights_high(0, i, True)
            gather_high(0)
            body(0, True)
            with act.Fori(1, count) as j:
                for i in range(2):
                    weights_high(j, i, False)
                body(j, False)

        @block.vector
        def _(dve):
            link = Link(dve, s["chain"])

            def make_slots(j):
                for t in range(TT):
                    ins = dve.tensor_scalar(to_slot[0:TS[t], t, :], k.iota_slot[0:TS[t], :],
                                            k.job_rank[0:TS[t], t, bass.ds(j, 1)], None, ALU.is_equal)
                ins.then_inc(s["slot_made"], 1)

            def make_sel(j):
                dve.tensor_copy(sel_b[:], k.job_sel[:, :, bass.ds(j, 1)].broadcast_to([P, TT, P])).then_inc(s["sel_made"], 1)

            def gather_low(n):
                for q in range(KD):
                    dve.wait_ge(s["aux_hi"], (n[0] * KD) + (n[1] + q + 1))
                    dve.tensor_tensor(xg[:, q, 1, :], aux_bank(AUX_AT["gather"] + q)[:, 0:CAP],
                                      xg[:, q, 0, :].bitcast(F32), ALU.subtract).then_inc(s["aux_read"], 1)

            def scatter_add(j, c):
                base = AUX_AT[f"scatter{c}"]
                for t in range(TT):
                    x = k.x[0:TS[t], t, c * RC:(c + 1) * RC]
                    dve.wait_ge(s["aux_mm"], j * AUX + (KD + base + t + 1))
                    dve.tensor_tensor(x, aux_bank(base + t)[0:TS[t], 0:RC], x, ALU.add).then_inc(s["aux_read"], 1)

            def body(j, first):
                for i in range(NC):
                    half, r = divmod(i, HC)
                    if is_hidden(i):
                        f = half * HF + r
                        dve.wait_ge(s["u_mm"], j * (2 * HF) + (f + 1))
                        dve.wait_ge(s["silu"], j * (2 * HF) + (f + 1))
                        if not (first and f < 2):
                            dve.wait_ge(s["h_lo"], j * (2 * HF) + (f - 1))
                        dve.tensor_tensor(hf[:, f % 2, :], k.banks[2 * (f % 2) + 1][:, 0:CAP], act_g[:, f % 2, :],
                                          ALU.mult).then_inc(s["hf"], 1)
                        dve.wait_ge(s["h_hi"], j * (2 * HF) + (f + 1))
                        dve.tensor_tensor(ht[:, r, 1, :], hf[:, f % 2, :], ht[:, r, 0, :].bitcast(F32),
                                          ALU.subtract).then_inc(s["h_lo"], 1)
                        if f == 4:
                            dve.wait_ge(s["aux_mm"], j * AUX + (KD + 1))
                            for m in range(len(ST)):
                                dve.tensor_scalar(halves(to_node[0:ST[m], m, :]), k.pair[3][0:ST[m], :, 0:HN],
                                                  k.job_off[0:ST[m], bass.ds(j, 1)], k.slot_id[0:ST[m], m:m + 1],
                                                  ALU.add, ALU.is_equal).then_inc(s["mapped"], 1)
                            for m in range(len(ST)):
                                o = k.banks[6][0:ST[m], 400 + 2 * m:402 + 2 * m]
                                dve.wait_ge(s["mapped"], j * (2 * len(ST)) + (len(ST) + m))
                                ins = dve.tensor_copy(w_slot[0:ST[m], m:m + 1], o[:, 0:1])
                                ins.then_inc(s["mapped"], 1)
                            dve.wait_ge(s["mapped"], j * (2 * len(ST)) + 2 * len(ST))
                            for m in range(len(ST)):
                                o = k.banks[6][0:ST[m], 400 + 2 * m:402 + 2 * m]
                                ins = dve.tensor_tensor(w_slot[0:ST[m], m:m + 1], o[:, 1:2], w_slot[0:ST[m], m:m + 1],
                                                        ALU.add)
                            ins.then_inc(s["aux_read"], 1)
                        if f == 7:
                            make_slots(j + 1)
                            make_sel(j + 1)
                        continue
                    c = r - HF
                    for m in range(len(ST)):
                        n = (half * OC + c) * len(ST) + m
                        o = k.banks[4 + n % 2][0:ST[m], 0:RC]
                        dve.wait_ge(s["y_mm"], j * OUTS + (n + 1))
                        if half == 0:
                            if m == 0 and c == 0:
                                dve.wait_ge(s["aux_read"], j * AUX + (KD + 1))
                            dve.tensor_scalar(y0[0:ST[m], c, m, :], o, w_slot[0:ST[m], m:m + 1], None,
                                              ALU.mult).then_inc(s["y_read"], 1)
                        else:
                            if m == 0 and not (first and c == 0):
                                dve.wait_ge(s["y_lo"], j * OC + c)
                            if m == 0 and c == 0:
                                dve.wait_ge(s["y_read"], j * OUTS + OC * len(ST))
                            dve.scalar_tensor_tensor(yf[0:ST[m], m, :], o, w_slot[0:ST[m], m:m + 1],
                                                     y0[0:ST[m], c, m, :], ALU.mult, ALU.add).then_inc(s["y_read"], 1)
                    if half == 1:
                        dve.wait_ge(s["y_read"], j * OUTS + (OC + c + 1) * len(ST))
                        dve.wait_ge(s["y_hi"], j * OC + (c + 1))
                        dve.tensor_tensor(y_hl[:, c, 1, :, :], yf[:], y_hl[:, c, 0, :, :].bitcast(F32),
                                          ALU.subtract).then_inc(s["y_lo"], 1)
                        if c > 0:
                            scatter_add(j, c - 1)
                gather_low((j, KD))
                scatter_add(j, OC - 1)

            for t in range(TT):
                dve.wait_ge(s["split_hi"], t + 1)
                ins = dve.tensor_tensor(xn[0:TS[t], t, 1, :], k.a[0:TS[t], t, :], xn[0:TS[t], t, 0, :].bitcast(F32),
                                        ALU.subtract)
            ins.then_inc(s["xn_ready"], 1)
            link(dve.memset(yf[:], 0.0))
            make_slots(0)
            make_sel(0)
            gather_low((0, 0))
            run(dve, body)

        @block.tensor
        def _(pe):
            def gather(j, n):
                pe.wait_ge(s["slot_made"], j + 1)
                for q in range(KD):
                    if q >= 2 or n is not None:
                        pe.wait_ge(s["aux_read"], (0 if n is None else n) + (q - 1))
                    for t in range(TT):
                        for a in range(2):
                            mm = pe.matmul(aux_bank(AUX_AT["gather"] + q)[:, 0:CAP], xn[0:TS[t], t, a, q * P:(q + 1) * P],
                                           to_slot[0:TS[t], t, :], start=(t == 0 and a == 0), stop=(t == TT - 1 and a == 1))
                    mm.then_inc(s["aux_mm"], 1)

            def map_nodes(j):
                pe.wait_ge(s["aux_read"], j * AUX + KD)
                pe.wait_ge(s["sel_made"], j + 1)
                for t in range(TT):
                    for h in range(2):
                        pe.matmul(k.pair[3][:, h, 0:HN], sel_b[0:TS[t], t, :], k.later[0:TS[t], t, h * HN:(h + 1) * HN],
                                  start=(t == 0), stop=(t == TT - 1))
                for m in range(len(ST)):
                    for t in range(TT):
                        mm = pe.matmul(k.banks[6][0:ST[m], 400 + 2 * m:402 + 2 * m],
                                       to_slot[0:TS[t], t, m * P:m * P + ST[m]],
                                       k.job_w[0:TS[t], t, bass.ds(j, 1), :].rearrange("p a w -> p (a w)"),
                                       start=(t == 0), stop=(t == TT - 1))
                mm.then_inc(s["aux_mm"], 1)

            def scatter(j, c):
                base = AUX_AT[f"scatter{c}"]
                pe.wait_ge(s["y_lo"], j * OC + (c + 1))
                for t in range(TT):
                    pe.wait_ge(s["aux_read"], j * AUX + (KD + base + t - (0 if base + t == 1 else 1)))
                    for m in range(len(ST)):
                        for a in range(2):
                            mm = pe.matmul(aux_bank(base + t)[0:TS[t], 0:RC], to_node[0:ST[m], m, t * P:t * P + TS[t]],
                                           y_hl[0:ST[m], c, a, m, :], start=(m == 0 and a == 0),
                                           stop=(m == len(ST) - 1 and a == 1))
                    mm.then_inc(s["aux_mm"], 1)

            def body(j, first):
                for i in range(NC):
                    half, r = divmod(i, HC)
                    wh = [w[:, i % RING, :] for w in (whi, wlo)]
                    pe.wait_ge(s["lo_done"], j * NC + (i + 1))
                    if is_hidden(i):
                        f = half * HF + r
                        if not (first and f < 2):
                            pe.wait_ge(s["hf"], j * (2 * HF) + (f - 1))
                        if f == 0:
                            pe.wait_ge(s["aux_read"], j * AUX + KD)
                        for g in range(2):
                            out = k.banks[2 * (f % 2) + g][:, 0:CAP]
                            for q in range(KD):
                                mm = split_product(pe, out,
                                                   [w[:, (2 * q + g) * P:(2 * q + g + 1) * P] for w in wh],
                                                   [xg[:, q, a, :] for a in range(2)], q == 0, q == KD - 1)
                            mm.then_inc(s["u_mm"] if g else s["g_mm"], 1)
                        if f == 3:
                            map_nodes(j)
                        continue
                    c = r - HF
                    for m in range(len(ST)):
                        n = (half * OC + c) * len(ST) + m
                        o = k.banks[4 + n % 2][0:ST[m], 0:RC]
                        if not (first and n < 2):
                            pe.wait_ge(s["y_read"], j * OUTS + (n - 1))
                        for f in range(HF):
                            if c == 0 and m == 0:
                                pe.wait_ge(s["h_lo"], j * (2 * HF) + (half * HF + f + 1))
                            mm = split_product(pe, o, [ht[:, f, a, m * P:m * P + ST[m]] for a in range(2)],
                                               [w[:, f * RC:(f + 1) * RC] for w in wh], f == 0, f == HF - 1)
                        mm.then_inc(s["y_mm"], 1)
                    if half == 1 and c > 0:
                        scatter(j, c - 1)
                gather(j + 1, j * AUX + (KD + AUX_AT["gather"]))
                scatter(j, OC - 1)

            pe.wait_ge(s["xn_ready"], 1)
            gather(0, None)
            run(pe, body)


def experts_block(k, I):
    with ExitStack() as ctx:
        k.enter(ctx)
        phase_norm(k, "n3", keep=True)
        k.enter(ctx)
        k.job_rank = k.sb("job_rank", [P, TT, JC], F32)
        k.job_w = k.sb("job_w", [P, TT, JC, 2], F32R)
        k.job_sel = k.sb("job_sel", [P, TT, JC], BF16)
        k.job_off = k.sb("job_off", [P, JC], F32)
        k.job_expert = k.sb("job_expert", [P, JC], I32)
        k.job_count = k.sb("job_count", [P, 1], I32)
        k.slot_id = k.sb("slot_id", [P, len(ST)], F32)
        k.iota_slot = k.sb("iota_slot", [P, CAP], F32)
        k.later = k.sb("later", [P, TT, NT], BF16)
        phase_router(k, "ro", I["L1_ffn_W_router"], I["L1_ffn_expert_bias"])
        phase_shared_expert(k, "se", I["L1_ffn_Wg_s"], I["L1_ffn_Wu_s"], I["L1_ffn_Wd_s"])
        phase_routed_experts(k, "re", I["L1_ffn_Wg_r"], I["L1_ffn_Wu_r"], I["L1_ffn_Wd_r"])



SEM_SETS = (range(100, 160), range(160, 220))


class Kit:

    def __init__(self, nc, ctx):
        self.nc, self.outer, self.inner = nc, ctx, ctx
        self.phase, self.taken = 0, 0

    def enter(self, ctx):
        self.inner = ctx

    def begin(self, ctx):
        self.inner = ctx
        self.phase += 1
        self.taken = 0

    def sb(self, name, shape, dt):
        return self.inner.enter_context(self.nc.sbuf_tensor(name, shape, dt))

    def sem(self, name):
        num = SEM_SETS[self.phase % 2][self.taken]
        self.taken += 1
        return self.inner.enter_context(self.nc.semaphore(name, num=num))

    def clear_last(self, pool):
        if self.phase > 1:
            pool.sem_clear(SEM_SETS[(self.phase + 1) % 2])


def build(nc, I, out, stop=99):
    with ExitStack() as ctx:
        k = Kit(nc, ctx)
        k.x_in = I["x"]
        psum = ctx.enter_context(nc.psum_tensor("psum", [P, 8, 512], F32))
        k.psum = psum
        k.banks = [psum[:, b, :] for b in range(8)]
        k.pair = [psum[:, 2 * b:2 * b + 2, :] for b in range(4)]
        k.x = k.sb("x_sb", [P, TT, D], F32)
        k.a = k.sb("a_sb", [P, TT, D], F32)
        k.xt = k.sb("xt_sb", [P, KD, 2, NT], F32R)
        k.ident = k.sb("ident", [P, P], F32)
        k.one = k.sb("one", [P, 1], F32)
        k.bn = k.sb("bn", [P, TT, 2, 6], F32)
        k.mv = k.sb("mv", [P, TT, 2], F32)
        k.ve = k.sb("ve", [P, TT], F32)
        k.root = k.sb("root", [P, TT], F32)
        k.rstd = k.sb("rstd", [P, TT], F32)
        k.tmp5 = k.sb("tmp5", [P, TT], F32)

        def first_norm():
            phase_norm(k, "n0", load_x=True)

        steps = [first_norm,
                 lambda: (phase_attend(k, "m0", False, I["L0_mix_W_qkv"], I["L0_mix_b_qkv"], I["L0_mix_random_features"]),
                          phase_project(k, "p0", False, I["L0_mix_W_proj"], I["L0_mix_b_proj"], I["x"])),
                 lambda: gnn_block(k, I),
                 lambda: (phase_norm(k, "n1"),
                          phase_ffn(k, "f0", I["L0_ffn_w_fc"], I["L0_ffn_b_fc"], I["L0_ffn_w_proj"], I["L0_ffn_b_proj"],
                                    I["L0_ffn_alpha_e"], I["L0_ffn_alpha_r"])),
                 lambda: (phase_norm(k, "n2"),
                          phase_save(k, "save"),
                          phase_attend(k, "m1", True, I["L1_mix_W_qkv"], None, I["L1_mix_random_features"]),
                          phase_project(k, "p1", True, I["L1_mix_W_proj"], I["L1_mix_b_proj"], k.x_dram,
                                        I["L1_mix_gamma"], I["L1_mix_beta"])),
                 lambda: phase_gcn(k, "gc", I["L1_gnn_W"], I["L1_gnn_b"]),
                 lambda: experts_block(k, I),
                 ]
        for step in steps[:stop]:
            step()
        k.begin(ctx)
        stored = k.sem("stored")
        block = ctx.enter_context(nc.Block())

        @block.sync
        def _(sp):
            for t in range(TT):
                sp.dma_start(out[t * P:t * P + TS[t], :], k.x[0:TS[t], t, :]).then_inc(stored, 16)
            sp.wait_ge(stored, 16 * TT)


def kernel(**inputs):
    import numpy as _np
    import concourse.bacc as _bacc
    from concourse import mybir as _mybir
    from concourse.bass_utils import run_bass_kernel_spmd as _run

    nc = _bacc.Bacc("TRN2", target_bir_lowering=False, num_devices=1)
    arrays, args = {}, {}
    for name, value in inputs.items():
        a = _np.ascontiguousarray(value)
        arrays[f"in_{name}"] = a
        args[name] = nc.dram_tensor(f"in_{name}", a.shape, _mybir.dt.from_np(a.dtype), kind="ExternalInput").ap()
    out = nc.dram_tensor("out_0", (NODES, D), F32, kind="ExternalOutput").ap()
    build(nc, args, out)
    r = _run(nc, [arrays], core_ids=[0])
    return r.results[0]["out_0"]
```

```python
from contextlib import ExitStack

import numpy as np
import concourse.bass as bass
from concourse import mybir

F32 = mybir.dt.float32
F32R = mybir.dt.float32r
BF16 = mybir.dt.bfloat16
F16 = mybir.dt.float16
I32 = mybir.dt.int32
U32 = mybir.dt.uint32
ALU = mybir.AluOpType
ACT = mybir.ActivationFunctionType
AX = mybir.AxisListType

P = 128
NODES = 625
TT = (NODES + P - 1) // P
TS = [min(P, NODES - P * t) for t in range(TT)]
HN = 314
NT = 2 * HN
D = 768
KD = D // P
EMB = 128
D1 = D + EMB
K1 = D1 // P
EDGES = 10000
EP = 125
ET = EDGES // EP
RELS = 3
HEADS = 12
PAIRS = HEADS // 2
DH = 64
VW = DH + 2
MF = 256
H_FF = 192
HP = 96
EXPERTS = 8
F_MOE = 1536
EPS = 1e-5
WE_MIX, WE_GNN, WE_MOE = KD * 256, K1 * 256, KD * 384


RING_SLOTS = 2


def weight_view(w):
    return w.rearrange("(k p) n -> p k n", p=P)


class Ring:

    def __init__(self, k):
        self.one = k.one[:]
        self.raw = k.sb("ring_raw", [P, RING_SLOTS, WE_GNN], F32)
        self.hi = k.sb("ring_hi", [P, RING_SLOTS, WE_GNN], F32R)
        self.lo = k.sb("ring_lo", [P, RING_SLOTS, WE_GNN], F32R)
        self.loaded = [k.lasting_sem(f"ring_loaded{i}") for i in range(RING_SLOTS)]
        self.hi_done = k.lasting_sem("ring_hi_done")
        self.lo_done = k.lasting_sem("ring_lo_done")
        self.parts = []

    def landed(self, g):
        return 16 * sum(self.parts[g % RING_SLOTS:g + 1:RING_SLOTS])


class Stream:

    def __init__(self, ring, chunks):
        self.ring, self.chunks, self.base = ring, chunks, len(ring.parts)
        ring.parts += [len(parts) for _, _, parts in chunks]
        self.freed = {}
        self.next = None

    def split(self, n):
        return self.ring.lo_done, self.base + n + 1

    def views(self, n):
        kt, cols, _ = self.chunks[n]
        slot = (self.base + n) % RING_SLOTS
        return [b[:, slot, 0:kt * cols].rearrange("p (k c) -> p k c", c=cols) for b in (self.ring.hi, self.ring.lo)]


def load_chunk(sp, st, n):
    g, ring = st.base + n, st.ring
    kt, cols, parts = st.chunks[n]
    if g >= RING_SLOTS:
        sp.wait_ge(ring.lo_done, g - RING_SLOTS + 1)
    dst = ring.raw[:, g % RING_SLOTS, 0:kt * cols].rearrange("p (k c) -> p k c", c=cols)
    for c0, c1, src in parts:
        sp.dma_start(dst[:, :, c0:c1], src).then_inc(ring.loaded[g % RING_SLOTS], 16)


def split_chunk(pool, st, n):
    g, ring = st.base + n, st.ring
    size = st.chunks[n][0] * st.chunks[n][1]
    raw, hi, lo = [b[:, g % RING_SLOTS, 0:size] for b in (ring.raw, ring.hi, ring.lo)]
    pool.wait_ge(ring.loaded[g % RING_SLOTS], ring.landed(g))
    pool.tensor_tensor(hi, raw, ring.one.broadcast_to([P, size]), ALU.mult).then_inc(ring.hi_done, 1)
    pool.wait_ge(ring.hi_done, g + 1)
    pool.tensor_tensor(lo, raw, hi.bitcast(F32), ALU.subtract).then_inc(ring.lo_done, 1)


def preload(sp, st):
    for n in range(RING_SLOTS):
        load_chunk(sp, st, n)


def stream_loads(sp, st):
    for n in range(RING_SLOTS, len(st.chunks)):
        load_chunk(sp, st, n)
    if st.next:
        preload(sp, st.next)


def stream_splits(pool, st):
    for n in range(1, len(st.chunks)):
        if n >= RING_SLOTS:
            pool.wait_ge(*st.freed[n - RING_SLOTS])
        split_chunk(pool, st, n)
    if st.next:
        pool.wait_ge(*st.freed[len(st.chunks) - RING_SLOTS])
        split_chunk(pool, st.next, 0)


def one_chunk(w, cols, c0):
    v = weight_view(w)
    return (v.shape[1], cols, [(0, cols, v[:, :, c0:c0 + cols])])


def attend_chunks(w_qkv):
    pw = weight_view(w_qkv)
    chunks = [(KD, 256, [(0, 256, pw[:, :, 2 * D + c * 256:2 * D + (c + 1) * 256])]) for c in range(3)]
    return chunks + [(KD, 256, [(0, P, pw[:, :, p * P:(p + 1) * P]), (P, 2 * P, pw[:, :, D + p * P:D + (p + 1) * P])])
                     for p in range(PAIRS)]


def square_chunks(w):
    return [one_chunk(w, 256, c * 256) for c in range(D // 256)]


def column_cuts(d_out):
    return [(c, min(256, d_out - c)) for c in range(0, d_out, 256)]


def rgcn_chunks(w_rel, w_root):
    d_in, d_out = w_root.shape
    return [(d_in // P, w, [(0, w, weight_view(m)[:, :, c:c + w])])
            for c, w in column_cuts(d_out) for m in (w_rel[0], w_rel[1], w_rel[2], w_root)]


def split_product(pe, out, lhs, rhs, first, last):
    for i, (a, b) in enumerate(((0, 0), (0, 1), (1, 0))):
        mm = pe.matmul(out, lhs[a], rhs[b], start=(first and i == 0), stop=(last and i == 2))
    return mm


def split_product_wide(pe, bank_pair, lhs, rhs, first, last):
    for i, (a, b) in enumerate(((0, 0), (0, 1), (1, 0))):
        for h in range(2):
            mm = pe.matmul(bank_pair[:, h, 0:HN], lhs[a], rhs(b, h),
                           start=(first and i == 0), stop=(last and i == 2))
    return mm


def halves(t):
    return t.rearrange("p (h n) -> p h n", h=2)


def feature_major(t):
    return t[:].rearrange("p t d -> p (t d)")[:, 0:KD * NT].rearrange("p (j n) -> p j n", n=NT)


def signals(k, phase, names):
    return {name: k.sem(f"{phase}_{name}") for name in names}


class Link:

    def __init__(self, eng, sem):
        self.eng, self.sem, self.n = eng, sem, 0

    def __call__(self, ins):
        self.n += 1
        ins.then_inc(self.sem, 1)
        self.eng.wait_ge(self.sem, self.n)



def turn_tile(pe, k, src, t):
    ts = TS[t]
    for j in range(KD):
        bank = k.banks[2 * (t % 2) + j // 4]
        mm = pe.transpose(bank[:, (j % 4) * P:(j % 4) * P + ts], src[0:ts, j * P:(j + 1) * P], k.ident[0:ts, 0:ts])
    return mm


def to_feature_major_act(act, k, dst, t, turned, hi_done):
    act.wait_ge(turned, t + 1)
    for b, (j0, j1) in enumerate(((0, 4), (4, KD))):
        src = k.banks[2 * (t % 2) + b][:, 0:(j1 - j0) * P].rearrange("p (j n) -> p j n", n=P)[:, :, 0:TS[t]]
        act.activation(dst[:, j0:j1, 0, t * P:t * P + TS[t]], src, ACT.Copy).then_inc(hi_done, 1)


def to_feature_major_dve(dve, k, dst, t, hi_done, lo_done):
    dve.wait_ge(hi_done, 2 * t + 2)
    for b, (j0, j1) in enumerate(((0, 4), (4, KD))):
        src = k.banks[2 * (t % 2) + b][:, 0:(j1 - j0) * P].rearrange("p (j n) -> p j n", n=P)[:, :, 0:TS[t]]
        ins = dve.tensor_tensor(dst[:, j0:j1, 1, t * P:t * P + TS[t]], src,
                                dst[:, j0:j1, 0, t * P:t * P + TS[t]].bitcast(F32), ALU.subtract)
    ins.then_inc(lo_done, 1)


def norm_stats(dve, link, k, src, mean_var):
    for t in range(TT):
        ts = TS[t]
        for h in range(2):
            ins = dve.bn_stats(k.bn[0:ts, t, h, :], src[0:ts, t, h * 384:(h + 1) * 384])
        link(ins)
        dve.bn_aggr(mean_var[0:ts, t, :], k.bn[0:ts, t, :, :].rearrange("p h s -> p (h s)"))


def phase_norm(k, name, load_x=False, keep=False):
    with ExitStack() as ctx:
        k.begin(ctx)
        slots = TT if keep else 2
        xn = k.a if keep else k.sb(f"{name}_xn", [P, slots, D], F32)
        s = signals(k, name, (
            "x_loaded", "consts", "ones_made", "chain", "var_ready", "root_ready", "xn_ready", "turned", "hi_done", "lo_done"))
        block = ctx.enter_context(k.nc.Block())

        @block.sync
        def _(sp):
            if load_x:
                for t in range(TT):
                    sp.dma_start(k.x[0:TS[t], t, :], k.x_in[t * P:t * P + TS[t], :]).then_inc(s["x_loaded"], 16)
                preload(sp, k.streams["m0"])

        @block.gpsimd
        def _(pool):
            k.clear_last(pool)
            if load_x:
                pool.memset(k.one[:], 1.0).then_inc(s["ones_made"], 1)
                pool.wait_ge(s["ones_made"], 1)
                pool.memset(k.ident[:], 0.0).then_inc(s["consts"], 1)
                pool.wait_ge(s["consts"], 1)
                pool.affine_select(out=k.ident[:], in_=k.ident[:], compare_op=ALU.not_equal, fill=1.0, base=0,
                                   pattern=[[-1, P]], channel_multiplier=1).then_inc(s["consts"], 1)
                split_chunk(pool, k.streams["m0"], 0)

        @block.vector
        def _(dve):
            link = Link(dve, s["chain"])
            if load_x:
                dve.memset(k.xt[:, :, :, NODES:NT].bitcast(F32), 0.0)
            if load_x:
                dve.memset(k.mv[:], 1.0)
                link(dve.memset(k.bn[:], 0.0))
                dve.wait_ge(s["x_loaded"], 16 * TT)
            norm_stats(dve, link, k, k.x, k.mv)
            rsqrt_of_var(dve, link, k, s)
            for t in range(TT):
                ts = TS[t]
                if t >= slots:
                    dve.wait_ge(s["turned"], t - 1)
                dve.tensor_scalar(xn[0:ts, t % slots, :], k.x[0:ts, t, :], k.mv[0:ts, t, 0:1], k.rstd[0:ts, t:t + 1],
                                  ALU.subtract, ALU.mult).then_inc(s["xn_ready"], 1)
                if t >= 1:
                    to_feature_major_dve(dve, k, k.xt, t - 1, s["hi_done"], s["lo_done"])
            to_feature_major_dve(dve, k, k.xt, TT - 1, s["hi_done"], s["lo_done"])

        @block.scalar
        def _(act):
            act.wait_ge(s["var_ready"], 1)
            act.activation(k.root[:], k.ve[:], ACT.Sqrt).then_inc(s["root_ready"], 1)
            for t in range(TT):
                to_feature_major_act(act, k, k.xt, t, s["turned"], s["hi_done"])

        @block.tensor
        def _(pe):
            if load_x:
                pe.wait_ge(s["consts"], 2)
            for t in range(TT):
                pe.wait_ge(s["xn_ready"], t + 1)
                if t >= 2:
                    pe.wait_ge(s["lo_done"], t - 1)
                turn_tile(pe, k, xn[:, t % slots, :], t).then_inc(s["turned"], 1)


def rsqrt_of_var(dve, link, k, s):
    link(dve.tensor_copy(k.ve[:, 0:1], k.mv[:, 0, 1:2]))
    link(dve.tensor_scalar(k.ve[:], k.mv[:, :, 1], EPS, None, ALU.add))
    rsqrt_of_ve(dve, link, k, s)


def rsqrt_of_ve(dve, link, k, s):
    dve.tensor_copy(k.tmp5[:], k.ve[:]).then_inc(s["var_ready"], 1)
    dve.wait_ge(s["root_ready"], 1)
    link(dve.reciprocal(k.rstd[:], k.root[:]))
    link(dve.tensor_tensor(k.tmp5[:], k.rstd[:], k.rstd[:], ALU.mult))
    link(dve.tensor_tensor(k.tmp5[:], k.tmp5[:], k.ve[:], ALU.mult))
    link(dve.tensor_scalar(k.tmp5[:], k.tmp5[:], -0.5, 1.5, ALU.mult, ALU.add))
    link(dve.tensor_tensor(k.rstd[:], k.rstd[:], k.tmp5[:], ALU.mult))



def phase_attend(k, name, second, b_qkv, rf):
    FUNC = ACT.Exp if second else ACT.Relu
    KV_SCALE = 1.0 / MF if second else 1.0 / (DH * MF)
    with ExitStack() as ctx:
        k.begin(ctx)
        st = k.streams[name]
        vt = k.sb(f"{name}_v", [P, TT, 2, HEADS, VW], F32R)
        early = k.a[:].rearrange("p t d -> p (t d)")
        vf = early[:, 0:512].rearrange("p (a n) -> p a n", a=2)
        qk = k.sb(f"{name}_qk", [P, 2, 2, NT], F32R)
        phik = k.sb(f"{name}_phik", [P, TT, 2, 512], F32R)
        phiq = k.sb(f"{name}_phiq", [P, 4, 2, NT], F32R)
        scratch = k.x[:].rearrange("p t d -> p (t d)")
        qkf = scratch[:, 0:2 * NT].rearrange("p (a n) -> p a n", a=2)
        pf = scratch[:, 2 * NT:4 * NT].rearrange("p (a n) -> p a n", a=2)
        sqf = scratch[:, 4 * NT:5 * NT]
        at_f = feature_major(k.a)
        KINDS = 2 if second else 1
        kv = k.sb(f"{name}_kv", [P, 2, KINDS, 4, P], F32R)
        kvf = k.sb(f"{name}_kvf", [P, 4, VW], F32)
        rff = early[:, 512:1024]
        rfin = early[:, 1024:1024 + 2 * DH].rearrange("p (a d) -> p a d", a=2)
        rfbd = k.sb(f"{name}_rfbd", [P, 2, 512], F32R)
        if second:
            sq = k.sb(f"{name}_sq", [P, 2, 2, NT], F32R)
            nh = k.sb(f"{name}_nh", [P, 512], F32R)
            den = scratch[:, 5 * NT:6 * NT]
            tiny = k.sb(f"{name}_tiny", [P, 1], F32)
        else:
            bv = k.sb(f"{name}_bv", [P, D], F32)
            bq = k.sb(f"{name}_bq", [P, 2 * PAIRS], F32)
        s = signals(k, name, (
            "small", "consts", "chain", "rf_turned", "rf_bd", "rf_hi", "rf_ready", "v_mm", "v_f", "v_hi", "v_lo",
            "qk_mm", "qk_f", "qk_hi", "qk_lo", "sq_f", "sq_hi", "pk_mm", "pk_f", "pk_hi", "pk_lo",
            "pq_mm", "pq_f", "pq_hi", "pq_lo", "kv_mm", "kv_f", "kv_hi", "kv_lo", "den_mm", "den_read", "at_mm", "at_out",
            ))
        smalls = 1 if second else 3
        st.freed.update({c: (s["v_mm"], TT * (c + 1)) for c in range(3)})
        st.freed.update({3 + p: (s["qk_mm"], 2 * (p + 1)) for p in range(PAIRS)})
        block = ctx.enter_context(k.nc.Block())
        kvb = k.banks[6]

        def kv_parts(part):
            pieces = []
            for kind in range(KINDS):
                for hd in range(2):
                    own = slice(hd * DH, (hd + 1) * DH)
                    src = kvf[:, 2 * hd:2 * hd + 2, DH:DH + 1].broadcast_to([P, 2, DH]) if kind else \
                        kvf[:, 2 * hd:2 * hd + 2, 0:DH]
                    pieces.append((kv[:, part, kind, 2 * hd:2 * hd + 2, own], src))
            return pieces

        @block.sync
        def _(sp):
            sp.dma_start(rfin, rf.rearrange("(a p) d -> p a d", p=P)).then_inc(s["small"], 16)
            if not second:
                sp.dma_start(bv[:], b_qkv[2 * D:3 * D].partition_broadcast(P)).then_inc(s["small"], 16)
                sp.dma_start(bq[:], b_qkv[0:2 * D].rearrange("(j p) -> p j", p=P),
                             allow_slow_non_contiguous=True).then_inc(s["small"], 16)
            stream_loads(sp, st)

        @block.gpsimd
        def _(pool):
            k.clear_last(pool)
            stream_splits(pool, st)

        @block.tensor
        def _(pe):
            pe.wait_ge(s["small"], 16 * smalls)
            for a in range(2):
                mm = pe.transpose(k.banks[7][0:DH, a * P:(a + 1) * P], rfin[:, a, :], k.ident[:])
            mm.then_inc(s["rf_turned"], 1)
            for c in range(3):
                pe.wait_ge(*st.split(c))
                wh = st.views(c)
                for t in range(TT):
                    i = c * TT + t
                    if i >= 2:
                        pe.wait_ge(s["v_f"], i - 1)
                    for j in range(KD):
                        mm = split_product(pe, k.banks[i % 2][0:TS[t], 0:256],
                                           [k.xt[:, j, a, t * P:t * P + TS[t]] for a in range(2)],
                                           [w[:, j, :] for w in wh], j == 0, j == KD - 1)
                    mm.then_inc(s["v_mm"], 1)

            def project_unit(p, u):
                if p == PAIRS:
                    return
                a, j = divmod(u, KD)
                n, i = 3 + p, 2 * p + a
                if u == 0:
                    pe.wait_ge(*st.split(n))
                if j == 0 and i >= 2:
                    pe.wait_ge(s["qk_f"], i - 1)
                mm = split_product_wide(pe, k.pair[2 - a], [w[:, j, a * P:(a + 1) * P] for w in st.views(n)],
                                        lambda b, h: k.xt[:, j, b, h * HN:(h + 1) * HN], j == 0, j == KD - 1)
                if j == KD - 1:
                    mm.then_inc(s["qk_mm"], 1)

            def features_k(p):
                pe.wait_ge(s["qk_lo"], 2 * p + 2)
                for t in range(TT):
                    i = p * TT + t
                    if i >= 2:
                        pe.wait_ge(s["pk_f"], i - 1)
                    if t < 2 and p >= 1:
                        pe.wait_ge(s["kv_f"], p)
                        if second:
                            pe.wait_ge(s["den_read"], p)
                    out = k.banks[6 + t % 2][0:TS[t], 0:512]
                    mm = split_product(pe, out, [qk[:, 1, a, t * P:t * P + TS[t]] for a in range(2)],
                                       [rfbd[:, a, :] for a in range(2)], True, not second)
                    if second:
                        for a in range(2):
                            mm = pe.matmul(out, sq[:, 1, a, t * P:t * P + TS[t]], nh[:], start=False, stop=(a == 1))
                    mm.then_inc(s["pk_mm"], 1)
                    project_unit(p + 1, t)

            def features_q(p):
                for m in range(4):
                    i = p * 4 + m
                    if i >= 2:
                        pe.wait_ge(s["pq_f"], i - 1)
                    if m == 0:
                        pe.wait_ge(s["at_out"], p)
                    if m == 1:
                        pe.wait_ge(s["pk_f"], TT * (p + 1))
                    pair = k.pair[0] if m % 2 == 0 else k.pair[3]
                    mm = split_product_wide(pe, pair, [rfbd[:, a, m * P:(m + 1) * P] for a in range(2)],
                                            lambda b, h: qk[:, 0, b, h * HN:(h + 1) * HN], True, not second)
                    if second:
                        for a in range(2):
                            for h in range(2):
                                mm = pe.matmul(pair[:, h, 0:HN], nh[:, m * P:(m + 1) * P],
                                               sq[:, 0, a, h * HN:(h + 1) * HN], start=False, stop=(a == 1))
                    mm.then_inc(s["pq_mm"], 1)
                    project_unit(p + 1, TT + m)

            def keys_values(p):
                pe.wait_ge(s["pk_lo"], TT * (p + 1))
                pe.wait_ge(s["pq_f"], 4 * (p + 1))
                for m in range(4):
                    for t in range(TT):
                        mm = split_product(pe, kvb[:, m * VW:(m + 1) * VW],
                                           [phik[0:TS[t], t, a, m * P:(m + 1) * P] for a in range(2)],
                                           [vt[0:TS[t], t, a, 2 * p + m // 2, :] for a in range(2)], t == 0, t == TT - 1)
                mm.then_inc(s["kv_mm"], 1)

            def attend(p):
                pe.wait_ge(s["kv_lo"], p + 1)
                pe.wait_ge(s["pq_lo"], 4 * (p + 1))
                for kind in reversed(range(KINDS)):
                    pair = k.pair[3 * kind]
                    for m in range(4):
                        mm = split_product_wide(pe, pair, [kv[:, a, kind, m, :] for a in range(2)],
                                                lambda b, h: phiq[:, m, b, h * HN:(h + 1) * HN], m == 0, m == 3)
                    mm.then_inc(s["den_mm"] if kind else s["at_mm"], 1)

            pe.wait_ge(s["rf_ready"], 1)
            pe.wait_ge(s["v_lo"], 3 * TT)
            for u in range(2 * KD):
                project_unit(0, u)
            for p in range(PAIRS):
                features_k(p)
                features_q(p)
                project_unit(p + 1, TT + 4)
                keys_values(p)
                for u in range(TT + 5, 2 * KD):
                    project_unit(p + 1, u)
                attend(p)

        @block.scalar
        def _(act):
            def high(dst, src, after, at_least, done):
                act.wait_ge(after, at_least)
                act.activation(dst, src, ACT.Copy).then_inc(done, 1)

            high(rfbd[:, 0, :], rff, s["rf_bd"], 1, s["rf_hi"])
            for i in range(3 * TT):
                c, t = i // TT, i % TT
                high(vt[0:TS[t], t, 0, 4 * c:4 * c + 4, 0:DH],
                     vf[0:TS[t], i % 2, :].rearrange("p (h d) -> p h d", d=DH), s["v_f"], i + 1, s["v_hi"])

            def qk_high(p):
                for a in range(2):
                    i = 2 * p + a
                    if p >= 1 and a == 0:
                        act.wait_ge(s["pk_mm"], TT * p)
                        act.wait_ge(s["pq_mm"], 4 * p)
                    high(qk[:, a, 0, :], qkf[:, a, :], s["qk_f"], i + 1, s["qk_hi"])
                    if second:
                        high(sq[:, a, 0, :], sqf[:], s["sq_f"], i + 1, s["sq_hi"])

            qk_high(0)
            for p in range(PAIRS):
                for t in range(TT):
                    i = p * TT + t
                    if p >= 1 and t == 0:
                        act.wait_ge(s["kv_mm"], p)
                    act.wait_ge(s["pk_mm"], i + 1)
                    if t >= 2:
                        act.wait_ge(s["pk_lo"], i - 1)
                    elif p >= 1:
                        act.wait_ge(s["pq_lo"], 4 * p)
                    f = pf[0:TS[t], t % 2, 0:512]
                    act.activation(f, k.banks[6 + t % 2][0:TS[t], 0:512], FUNC).then_inc(s["pk_f"], 1)
                    high(phik[0:TS[t], t, 0, :], f, s["pk_f"], i + 1, s["pk_hi"])
                for m in range(4):
                    i = p * 4 + m
                    if p >= 1 and m == 0:
                        act.wait_ge(s["at_mm"], p)
                    act.wait_ge(s["pq_mm"], i + 1)
                    if m >= 2:
                        act.wait_ge(s["pq_lo"], i - 1)
                    else:
                        act.wait_ge(s["pk_lo"], TT * (p + 1))
                    pair = k.pair[0] if m % 2 == 0 else k.pair[3]
                    f = pf[:, m % 2, :]
                    act.activation(halves(f), pair[:, :, 0:HN], FUNC).then_inc(s["pq_f"], 1)
                    high(phiq[:, m, 0, :], f, s["pq_f"], i + 1, s["pq_hi"])
                if p >= 1:
                    act.wait_ge(s["at_mm"], p)
                act.wait_ge(s["kv_mm"], p + 1)
                if p >= 1:
                    act.wait_ge(s["kv_lo"], p)
                act.activation(kvf[:], kvb[:, 0:4 * VW].rearrange("p (m v) -> p m v", v=VW), ACT.Copy,
                               scale=KV_SCALE).then_inc(s["kv_f"], 1)
                act.wait_ge(s["kv_f"], p + 1)
                for dst, src in kv_parts(0):
                    ins = act.activation(dst, src, ACT.Copy)
                ins.then_inc(s["kv_hi"], 1)
                if p + 1 < PAIRS:
                    qk_high(p + 1)
                if second:
                    act.wait_ge(s["den_mm"], p + 1)
                    if p >= 1:
                        act.wait_ge(s["at_out"], p)
                    act.activation(halves(den), k.pair[3][:, :, 0:HN], ACT.Identity, bias=tiny[:, 0:1])\
                        .then_inc(s["den_read"], 1)
                else:
                    act.wait_ge(s["at_mm"], p + 1)
                    act.activation(halves(at_f[:, p, :]), k.pair[0][:, :, 0:HN], ACT.Copy).then_inc(s["at_out"], 1)

        @block.vector
        def _(dve):
            link = Link(dve, s["chain"])
            dve.memset(vt[:, :, :, :, DH:VW].bitcast(F32), 0.0)
            dve.memset(kv[:].bitcast(F32), 0.0)
            if second:
                dve.memset(tiny[:], 1e-6)
            link(dve.memset(rff, 0.0))
            link(dve.memset(vt[:, :, 0, :, DH:DH + 1].bitcast(F32), 1.0))
            if second:
                link(dve.memset(nh[:].bitcast(F32), 0.0))
                for hd in range(2):
                    link(dve.memset(nh[hd * DH:(hd + 1) * DH, hd * MF:(hd + 1) * MF].bitcast(F32), -0.5))
            dve.wait_ge(s["rf_turned"], 1)
            for hd in range(2):
                ins = dve.tensor_copy(rff[hd * DH:(hd + 1) * DH, hd * MF:(hd + 1) * MF], k.banks[7][0:DH, 0:MF])
                if hd == 0:
                    link(ins)
            ins.then_inc(s["rf_bd"], 1)
            dve.wait_ge(s["rf_hi"], 1)
            dve.tensor_tensor(rfbd[:, 1, :], rff, rfbd[:, 0, :].bitcast(F32), ALU.subtract).then_inc(s["rf_ready"], 1)
            dve.wait_ge(s["small"], 16 * smalls)

            def v_low(i):
                c, t = i // TT, i % TT
                dve.wait_ge(s["v_hi"], i + 1)
                dve.tensor_tensor(vt[0:TS[t], t, 1, 4 * c:4 * c + 4, 0:DH],
                                  vf[0:TS[t], i % 2, :].rearrange("p (h d) -> p h d", d=DH),
                                  vt[0:TS[t], t, 0, 4 * c:4 * c + 4, 0:DH].bitcast(F32), ALU.subtract).then_inc(s["v_lo"], 1)

            for i in range(3 * TT):
                c, t = i // TT, i % TT
                dve.wait_ge(s["v_mm"], i + 1)
                if i >= 2:
                    dve.wait_ge(s["v_lo"], i - 1)
                src, dst = k.banks[i % 2][0:TS[t], 0:256], vf[0:TS[t], i % 2, :]
                if second:
                    dve.tensor_copy(dst, src).then_inc(s["v_f"], 1)
                else:
                    dve.tensor_tensor(dst, src, bv[0:TS[t], c * 256:(c + 1) * 256], ALU.add).then_inc(s["v_f"], 1)
                if i >= 1:
                    v_low(i - 1)
            v_low(3 * TT - 1)

            def qk_parts(p):
                for a in range(2):
                    i = 2 * p + a
                    dve.wait_ge(s["qk_mm"], i + 1)
                    if p >= 1:
                        dve.wait_ge(s["qk_lo"], 2 * p)
                    src = k.pair[2 - a][:, :, 0:HN]
                    if second:
                        dve.tensor_copy(halves(qkf[:, a, :]), src).then_inc(s["qk_f"], 1)
                        dve.wait_ge(s["qk_f"], i + 1)
                        if i >= 1:
                            dve.wait_ge(s["sq_hi"], i)
                        dve.tensor_tensor(sqf[:], qkf[:, a, :], qkf[:, a, :], ALU.mult).then_inc(s["sq_f"], 1)
                        dve.wait_ge(s["sq_hi"], i + 1)
                        link(dve.tensor_tensor(sq[:, a, 1, :], sqf[:], sq[:, a, 0, :].bitcast(F32), ALU.subtract))
                    else:
                        dve.tensor_scalar(halves(qkf[:, a, :]), src, bq[:, a * PAIRS + p:a * PAIRS + p + 1], None,
                                          ALU.add).then_inc(s["qk_f"], 1)
                    dve.wait_ge(s["qk_hi"], i + 1)
                    dve.tensor_tensor(qk[:, a, 1, :], qkf[:, a, :], qk[:, a, 0, :].bitcast(F32),
                                      ALU.subtract).then_inc(s["qk_lo"], 1)

            qk_parts(0)
            for p in range(PAIRS):
                for t in range(TT):
                    dve.wait_ge(s["pk_hi"], p * TT + t + 1)
                    dve.tensor_tensor(phik[0:TS[t], t, 1, :], pf[0:TS[t], t % 2, 0:512],
                                      phik[0:TS[t], t, 0, :].bitcast(F32), ALU.subtract).then_inc(s["pk_lo"], 1)
                for m in range(4):
                    dve.wait_ge(s["pq_hi"], p * 4 + m + 1)
                    dve.tensor_tensor(phiq[:, m, 1, :], pf[:, m % 2, :], phiq[:, m, 0, :].bitcast(F32),
                                      ALU.subtract).then_inc(s["pq_lo"], 1)
                dve.wait_ge(s["kv_hi"], p + 1)
                for (dst, src), (hi, _) in zip(kv_parts(1), kv_parts(0)):
                    ins = dve.tensor_tensor(dst, src, hi.bitcast(F32), ALU.subtract)
                ins.then_inc(s["kv_lo"], 1)
                if p + 1 < PAIRS:
                    qk_parts(p + 1)
                if second:
                    dve.wait_ge(s["den_read"], p + 1)
                    link(dve.reciprocal(den, den))
                    dve.wait_ge(s["at_mm"], p + 1)
                    dve.tensor_tensor(halves(at_f[:, p, :]), k.pair[0][:, :, 0:HN], halves(den), ALU.mult)\
                        .then_inc(s["at_out"], 1)


def phase_project(k, name, second, b_proj, x_src, gamma=None, beta=None):
    with ExitStack() as ctx:
        k.begin(ctx)
        st = k.streams[name]
        at = k.sb(f"{name}_at", [P, KD, 2, NT], F32R)
        bp = k.sb(f"{name}_bp", [P, D], F32)
        at_f = feature_major(k.a)
        if second:
            gb = k.sb(f"{name}_gb", [P, 2, D], F32)
            y_sb = k.sb(f"{name}_y", [P, TT, D], F32)
        s = signals(k, name, (
            "small", "x_loaded", "chain", "t_hi", "t_lo", "proj_mm", "proj_out", "var_ready", "root_ready"))
        st.freed.update({c: (s["proj_mm"], TT * (c + 1)) for c in range(3)})
        smalls = 3 if second else 1
        block = ctx.enter_context(k.nc.Block())

        @block.sync
        def _(sp):
            stream_loads(sp, st)

        @block.gpsimd
        def _(pool):
            k.clear_last(pool)
            stream_splits(pool, st)

        @block.tensor
        def _(pe):
            for c in range(3):
                pe.wait_ge(*st.split(c))
                wh = st.views(c)
                for t in range(TT):
                    i = c * TT + t
                    if i >= 2:
                        pe.wait_ge(s["proj_out"], i - 1)
                    for j in range(KD):
                        if i == 0:
                            pe.wait_ge(s["t_lo"], j + 1)
                        mm = split_product(pe, k.banks[4 + i % 2][0:TS[t], 0:256],
                                           [at[:, j, a, t * P:t * P + TS[t]] for a in range(2)],
                                           [w[:, j, :] for w in wh], j == 0, j == KD - 1)
                    mm.then_inc(s["proj_mm"], 1)

        @block.scalar
        def _(act):
            act.dma_start(bp[:], b_proj.partition_broadcast(P)).then_inc(s["small"], 16)
            if second:
                act.dma_start(gb[:, 0, :], gamma.partition_broadcast(P)).then_inc(s["small"], 16)
                act.dma_start(gb[:, 1, :], beta.partition_broadcast(P)).then_inc(s["small"], 16)
            for t in range(TT):
                act.dma_start(k.x[0:TS[t], t, :], x_src[t * P:t * P + TS[t], :]).then_inc(s["x_loaded"], 16)
            for t in range(KD):
                act.activation(at[:, t, 0, :], at_f[:, t, :], ACT.Copy).then_inc(s["t_hi"], 1)
            if second:
                act.wait_ge(s["var_ready"], 1)
                act.activation(k.root[:], k.ve[:], ACT.Sqrt).then_inc(s["root_ready"], 1)

        @block.vector
        def _(dve):
            link = Link(dve, s["chain"])
            for j in range(KD):
                dve.wait_ge(s["t_hi"], j + 1)
                dve.tensor_tensor(at[:, j, 1, :], at_f[:, j, :], at[:, j, 0, :].bitcast(F32), ALU.subtract)\
                    .then_inc(s["t_lo"], 1)
            dve.wait_ge(s["small"], 16 * smalls)
            dve.wait_ge(s["x_loaded"], 16 * TT)
            y_all = y_sb if second else k.x
            if second:
                for t in range(TT):
                    ins = dve.tensor_scalar(y_sb[0:TS[t], t, :], k.x[0:TS[t], t, :], k.mv[0:TS[t], t, 0:1],
                                            k.rstd[0:TS[t], t:t + 1], ALU.subtract, ALU.mult)
                link(ins)
            for t in range(TT):
                ins = dve.tensor_tensor(y_all[0:TS[t], t, :], y_all[0:TS[t], t, :], bp[0:TS[t], :], ALU.add)
            link(ins)
            for i in range(3 * TT):
                c, t = i // TT, i % TT
                y = y_all[0:TS[t], t, c * 256:(c + 1) * 256]
                dve.wait_ge(s["proj_mm"], i + 1)
                dve.tensor_tensor(y, k.banks[4 + i % 2][0:TS[t], 0:256], y, ALU.add).then_inc(s["proj_out"], 1)
            if second:
                dve.wait_ge(s["proj_out"], 3 * TT)
                norm_stats(dve, link, k, y_sb, k.mv)
                rsqrt_of_var(dve, link, k, s)
                for op in range(4):
                    for t in range(TT):
                        ts = TS[t]
                        y = y_sb[0:ts, t, :]
                        if op == 0:
                            ins = dve.tensor_scalar(y, y, k.mv[0:ts, t, 0:1], k.rstd[0:ts, t:t + 1], ALU.subtract, ALU.mult)
                        elif op == 3:
                            ins = dve.tensor_tensor(k.x[0:ts, t, :], k.x[0:ts, t, :], y, ALU.add)
                        else:
                            ins = dve.tensor_tensor(y, y, gb[0:ts, op - 1, :], ALU.mult if op == 1 else ALU.add)
                    link(ins)



UNROLL = 4
SW = TT * P


BASE = 256
TO_INT = 1.5 * 2 ** 23


def count_pieces():
    pieces, seen = [], set()
    for s in range(TT):
        c0 = s * NT
        while c0 < (s + 1) * NT:
            c1 = min((s + 1) * NT, (c0 // 512 + 1) * 512)
            pieces.append((s, c0, c1, c0 // 512 not in seen))
            seen.add(c0 // 512)
            c0 = c1
    return pieces


def phase_counts(k, src, dst, edge_type, node_emb, node_type):
    flat = k.psum[:].rearrange("p b n -> p (b n)")
    with ExitStack() as ctx:
        k.begin(ctx)
        edges_i = k.sb("edges_i", [EP, 3, ET], I32)
        edges_f = k.sb("edges_f", [EP, 3, ET], F32)
        over = k.sb("count_over", [P, 2], F32R)
        iota_i = k.sb("iota_i", [P, SW], I32)
        iota = k.sb("iota", [P, SW], F16)
        weight = k.sb("edge_weight", [EP, 1 + RELS, ET], F32)
        rounds = k.sb("count_rounds", [P, 1], I32)
        checks = k.sb("count_checks", [P, 4], F32)
        shift = k.sb("digit_shift", [P, 1], F32)
        quot = k.sb("digit_quot", [P, 2, NT], F32)
        upper = k.sb("digit_upper", [P, 2, NT], F32)
        quot2 = k.sb("digit_quot2", [P, 2, NT], F32)
        src_hot = k.sb("src_hot", [EP, UNROLL, SW], BF16)
        dst_hot = k.sb("dst_hot", [EP, UNROLL, NT], BF16)
        total = k.sb("count_total", [P, TT, NT], F32)
        ones_f = k.sb("ones_f", [P, P], F32)
        ones = k.sb("ones_r", [P, P], F32R)
        pos = k.sb("count_pos", [P, NT], F32)
        cnt = k.sb("count_rel", [P, NT], F32)
        emb_sb = k.sb("node_emb", [RELS, EMB], F32)
        type_i = k.sb("type_i", [RELS, NODES], I32)
        type_f = k.sb("type_f", [RELS, NODES], F32)
        own = k.sb("own_type", [RELS, 1], F32)
        onehot = k.sb("type_onehot", [RELS, NT], F32)
        s = signals(k, "c", (
            "loaded", "iota_made", "chain", "hot", "tile_mm", "copied", "ones_made", "sum_mm", "sum_read",
            "total_made", "saved", "quot", "upper", "low", "quot2",
            "over_made", "shift_made", "top_digit", "all_copied", "check_mm", "rounds_made", "emb_loaded", "own_made", "emb_made", "emb_ready", "emb_hi"))
        block = ctx.enter_context(k.nc.Block())
        pieces = count_pieces()

        @block.sync
        def _(sp):
            for i, e in enumerate((src, dst, edge_type)):
                sp.dma_start(edges_i[:, i, :], e.rearrange("(p j) -> p j", p=EP)).then_inc(s["loaded"], 16)
            sp.dma_start(emb_sb[:], node_emb).then_inc(s["emb_loaded"], 16)
            for r in range(RELS):
                sp.dma_start(type_i[r:r + 1, :], node_type.rearrange("(a n) -> a n", a=1)).then_inc(s["emb_loaded"], 16)
            sp.wait_ge(s["total_made"], 2)
            sp.dma_start(k.total_dram, total[:].rearrange("p t n -> p (t n)")).then_inc(s["saved"], 16)
            sp.wait_ge(s["saved"], 16)

        @block.gpsimd
        def _(pool):
            k.clear_last(pool)
            pool.iota(iota_i[:], [[1, SW]], base=0, channel_multiplier=0).then_inc(s["iota_made"], 1)
            pool.iota(own[:], [[0, 1]], base=0, channel_multiplier=1,
                      allow_small_or_imprecise_dtypes=True).then_inc(s["own_made"], 1)

        @block.vector
        def _(dve):
            link = Link(dve, s["chain"])
            dve.memset(ones_f[:], 1.0).then_inc(s["ones_made"], 1)
            link(dve.memset(onehot[:], 0.0))
            dve.wait_ge(s["iota_made"], 1)
            dve.tensor_copy(iota[:], iota_i[:])
            dve.wait_ge(s["loaded"], 48)
            link(dve.tensor_copy(edges_f[:], edges_i[:]))
            dve.memset(shift[:], -(BASE / 2 - 1) / BASE).then_inc(s["shift_made"], 1)
            for r in range(RELS):
                ins = dve.tensor_scalar(weight[:, 1 + r, :], edges_f[:, 2, :], float(r), None, ALU.is_equal)
                link(ins)
            link(dve.scalar_tensor_tensor(weight[:, 0, :], weight[:, 2, :], float(BASE), weight[:, 1, :], ALU.mult, ALU.add))
            link(dve.scalar_tensor_tensor(weight[:, 0, :], weight[:, 3, :], float(BASE ** 2), weight[:, 0, :],
                                          ALU.mult, ALU.add))

            by_slot = edges_f[:].rearrange("e f (g u) -> e f u g", u=UNROLL)
            weight_by_slot = weight[:].rearrange("e r (g u) -> e u (r g)", u=UNROLL)

            def one_hots(r, g, u, seq, wait):
                if wait:
                    dve.wait_ge(s["tile_mm"], seq - UNROLL + 1)
                dve.tensor_scalar(src_hot[:, u, :], iota[0:EP, :], by_slot[:, 0, u, bass.ds(g, 1)], None, ALU.is_equal)
                dve.tensor_scalar(dst_hot[:, u, :], iota[0:EP, 0:NT], by_slot[:, 1, u, bass.ds(g, 1)],
                                  weight_by_slot[:, u, bass.ds(r * (ET // UNROLL) + g, 1)], ALU.is_equal, ALU.mult).then_inc(s["hot"], 1)

            def all_one_hots(r, wait):
                for u in range(UNROLL):
                    one_hots(r, 0, u, r * ET + u, wait)
                with dve.Fori(1, ET // UNROLL) as g:
                    for u in range(UNROLL):
                        one_hots(r, g, u, g * UNROLL + (r * ET + u), True)

            all_one_hots(0, False)
            for t in range(TT):
                up = upper[:, t % 2, :]
                dve.wait_ge(s["quot"], t + 1)
                if t >= 2:
                    dve.wait_ge(s["quot2"], t - 1)
                dve.tensor_scalar(up, quot[:, t % 2, :], TO_INT, -TO_INT, ALU.add, ALU.add).then_inc(s["upper"], 1)
                dve.wait_ge(s["upper"], t + 1)
                dve.scalar_tensor_tensor(k.C[:, 0, t, :], up, -float(BASE), total[:, t, :],
                                         ALU.mult, ALU.add).then_inc(s["low"], 1)
                dve.wait_ge(s["quot2"], t + 1)
                dve.tensor_scalar(k.C[:, 2, t, :], quot2[:, t % 2, :], TO_INT, -TO_INT, ALU.add, ALU.add)\
                    .then_inc(s["top_digit"], 1)
                dve.wait_ge(s["top_digit"], t + 1)
                dve.scalar_tensor_tensor(k.C[:, 1, t, :], k.C[:, 2, t, :].bitcast(F32), -float(BASE), up,
                                         ALU.mult, ALU.add).then_inc(s["copied"], 1)
            dve.wait_ge(s["copied"], TT)
            link(dve.tensor_reduce(checks[:, 0:1], k.C[:, 2, :, :].bitcast(F32).rearrange("p t n -> p (t n)"),
                                   AX.X, ALU.max))
            dve.tensor_scalar(over[:], checks[:, 0:1].broadcast_to([P, 2]), float(BASE), None, ALU.is_ge)\
                .then_inc(s["over_made"], 1)
            dve.wait_ge(s["check_mm"], 1)
            dve.tensor_copy(checks[:, 1:2], k.banks[7][:, 0:1])
            link(dve.tensor_reduce(checks[:, 2:3], k.pair[0][:, :, 0:HN], AX.XY, ALU.add))
            link(dve.tensor_scalar(checks[:, 2:3], checks[:, 2:3], float(EDGES), None, ALU.not_equal))
            link(dve.tensor_tensor(checks[:, 2:3], checks[:, 1:2], checks[:, 2:3], ALU.add))
            link(dve.tensor_scalar(checks[:, 3:4], checks[:, 2:3], 0.5, float(RELS), ALU.is_gt, ALU.mult))
            dve.tensor_copy(rounds[:], checks[:, 3:4]).then_inc(s["rounds_made"], 1)
            dve.wait_ge(s["rounds_made"], 1)
            again = dve.value_load(rounds[0:1, 0:1], min_val=0, max_val=RELS)
            with dve.Fori(0, again) as r:
                all_one_hots(r + 1, True)
            for r in range(RELS):
                dve.wait_ge(s["sum_mm"], r + 1)
                sums = k.pair[r][:, :, 0:HN]
                link(dve.tensor_scalar(halves(pos[:]), sums, 0.0, None, ALU.is_gt))
                link(dve.tensor_scalar(halves(cnt[:]), sums, 1.0, None, ALU.max))
                link(dve.reciprocal(cnt[:], cnt[:]))
                link(dve.tensor_tensor(k.inv[:, r, :], cnt[:], pos[:], ALU.mult))
            dve.tensor_tensor(total[:], k.C[:, 0, :, :].bitcast(F32), k.C[:, 1, :, :].bitcast(F32), ALU.add).then_inc(s["total_made"], 1)
            dve.wait_ge(s["total_made"], 1)
            dve.tensor_tensor(total[:], total[:], k.C[:, 2, :, :].bitcast(F32), ALU.add).then_inc(s["total_made"], 1)
            dve.wait_ge(s["emb_loaded"], 64)
            link(dve.tensor_copy(type_f[:], type_i[:]))
            dve.wait_ge(s["own_made"], 1)
            dve.tensor_scalar(onehot[:, 0:NODES], type_f[:], own[:, 0:1], None, ALU.is_equal).then_inc(s["emb_made"], 1)
            dve.wait_ge(s["emb_hi"], 1)
            dve.tensor_tensor(halves(k.et[:, 0, 1, :]), k.pair[3][:, :, 0:HN], halves(k.et[:, 0, 0, :].bitcast(F32)),
                              ALU.subtract)

        @block.scalar
        def _(act):
            act.wait_ge(s["ones_made"], 1)
            act.activation(ones[:], ones_f[:], ACT.Copy).then_inc(s["ones_made"], 1)
            act.wait_ge(s["shift_made"], 1)
            act.wait_ge(s["tile_mm"], ET)
            def second_quotient(t):
                act.wait_ge(s["upper"], t + 1)
                if t >= 2:
                    act.wait_ge(s["top_digit"], t - 1)
                act.activation(quot2[:, t % 2, :], upper[:, t % 2, :], ACT.Identity, bias=shift[:, 0:1],
                               scale=1.0 / BASE).then_inc(s["quot2"], 1)

            for t in range(TT):
                if t >= 2:
                    act.wait_ge(s["upper"], t - 1)
                act.activation(total[:, t, :], flat[:, t * NT:(t + 1) * NT], ACT.Copy).then_inc(s["sum_read"], 1)
                act.wait_ge(s["sum_read"], t + 1)
                act.activation(quot[:, t % 2, :], total[:, t, :], ACT.Identity, bias=shift[:, 0:1],
                               scale=1.0 / BASE).then_inc(s["quot"], 1)
                if t >= 1:
                    second_quotient(t - 1)
            second_quotient(TT - 1)
            act.wait_ge(s["rounds_made"], 1)
            again = act.value_load(rounds[0:1, 0:1], min_val=0, max_val=RELS)
            with act.Fori(0, again) as r:
                act.wait_ge(s["tile_mm"], ET * r + 2 * ET)
                for t in range(TT):
                    act.activation(k.C[:, bass.ds(r, 1), t, :].rearrange("p a n -> p (a n)"),
                                   flat[:, t * NT:(t + 1) * NT], ACT.Copy).then_inc(s["copied"], 1)
            act.activation(ones_f[:, 0:1], ones_f[:, 1:2], ACT.Copy).then_inc(s["all_copied"], 1)
            act.wait_ge(s["emb_ready"], 1)
            act.activation(halves(k.et[:, 0, 0, :]), k.pair[3][:, :, 0:HN], ACT.Copy).then_inc(s["emb_hi"], 1)

        @block.tensor
        def _(pe):
            def count(u, seq, first, last):
                pe.wait_ge(s["hot"], seq + 1)
                for t, c0, c1, opens in pieces:
                    mm = pe.matmul(flat[:, c0:c1], src_hot[:, u, t * P:(t + 1) * P],
                                   dst_hot[:, u, c0 - t * NT:c1 - t * NT], start=(first and opens), stop=last,
                                   skip_group_check=True)
                return mm

            def count_all(r):
                for u in range(UNROLL):
                    count(u, r * ET + u, u == 0, False).then_inc(s["tile_mm"], 1)
                with pe.Fori(1, ET // UNROLL - 1) as g:
                    for u in range(UNROLL):
                        count(u, g * UNROLL + (r * ET + u), False, False).then_inc(s["tile_mm"], 1)
                for u in range(UNROLL):
                    count(u, r * ET + ET - UNROLL + u, False, u == UNROLL - 1).then_inc(s["tile_mm"], 1)

            count_all(0)
            pe.wait_ge(s["ones_made"], 2)
            pe.wait_ge(s["copied"], TT)
            for r in range(RELS):
                for t in range(TT):
                    for h in range(2):
                        pe.matmul(k.pair[0][:, h, 0:HN], ones[:], k.C[:, r, t, h * HN:(h + 1) * HN],
                                  start=(r == 0 and t == 0), stop=(r == RELS - 1 and t == TT - 1))
            pe.wait_ge(s["over_made"], 1)
            pe.matmul(k.banks[7][:, 0:2], ones[:], over[:], start=True, stop=True).then_inc(s["check_mm"], 1)
            pe.wait_ge(s["rounds_made"], 1)
            again = pe.value_load(rounds[0:1, 0:1], min_val=0, max_val=RELS)
            with pe.Fori(0, again) as r:
                pe.wait_ge(s["copied"], r * TT + TT)
                count_all(r + 1)
            pe.wait_ge(s["all_copied"], 1)
            for r in range(RELS):
                for t in range(TT):
                    for h in range(2):
                        mm = pe.matmul(k.pair[r][:, h, 0:HN], ones[:], k.C[:, r, t, h * HN:(h + 1) * HN],
                                       start=(t == 0), stop=(t == TT - 1))
                mm.then_inc(s["sum_mm"], 1)
            pe.wait_ge(s["emb_made"], 1)
            for h in range(2):
                mm = pe.matmul(k.pair[3][:, h, 0:HN], emb_sb[:], onehot[:, h * HN:(h + 1) * HN], start=True, stop=True)
            mm.then_inc(s["emb_ready"], 1)



def phase_rgcn(k, name, h_in, h_out, d_in, d_out, bias):
    kt, mt = d_in // P, d_out // P
    cuts = column_cuts(d_out)
    with ExitStack() as ctx:
        k.begin(ctx)
        st = k.streams[name]
        y = k.sb(f"{name}_y", [P, 2, TT, 2, 256], F32R)
        room = k.a[:].rearrange("p t d -> p (t d)")
        acc = room[:, RELS * NT:(RELS + 2) * NT].rearrange("p (m n) -> p m n", m=2)
        part = room[:, (RELS + 2) * NT:(RELS + 3) * NT]
        b = k.sb(f"{name}_b", [P, mt], F32)
        s = signals(k, name, (
            "small", "chain", "y_mm", "y_hi", "y_lo", "g_mm", "g_read", "h_f", "h_hi", "h_lo"))
        jobs = [(kind, c, r) for c in range(len(cuts))
                for kind, r in (("Y", 0), ("Y", 1), ("G", 0), ("Y", 2), ("G", 1), ("R", 3), ("G", 2))]
        y_at = {(c, r): RELS * c + r for c in range(len(cuts)) for r in range(RELS)}
        g_at, g_count = {}, 0
        for kind, c, r in jobs:
            if kind != "Y":
                g_at[c, r] = g_count
                g_count += cuts[c][1] // P
        for c in range(len(cuts)):
            for r in range(RELS):
                st.freed[4 * c + r] = (s["y_mm"], TT * (y_at[c, r] + 1))
            st.freed[4 * c + 3] = (s["g_mm"], g_at[c, 3] + cuts[c][1] // P)
        block = ctx.enter_context(k.nc.Block())

        @block.sync
        def _(sp):
            sp.dma_start(b[:], bias.rearrange("(m p) -> p m", p=P), allow_slow_non_contiguous=True).then_inc(s["small"], 16)
            stream_loads(sp, st)

        @block.gpsimd
        def _(pool):
            k.clear_last(pool)
            stream_splits(pool, st)

        @block.tensor
        def _(pe):
            for kind, c, r in jobs:
                w = cuts[c][1]
                if kind == "Y":
                    pe.wait_ge(*st.split(4 * c + r))
                    wh = st.views(4 * c + r)
                    for t in range(TT):
                        i = TT * y_at[c, r] + t
                        if i >= 3:
                            pe.wait_ge(s["y_lo"], i - 2)
                        for j in range(kt):
                            mm = split_product(pe, k.banks[i % 3][0:TS[t], 0:w],
                                               [h_in(j)[:, a, t * P:t * P + TS[t]] for a in range(2)],
                                               [v[:, j, :] for v in wh], j == 0, j == kt - 1)
                        mm.then_inc(s["y_mm"], 1)
                    continue
                for m in range(w // P):
                    i = g_at[c, r] + m
                    pair = k.pair[2 + i % 2]
                    if i >= 2:
                        pe.wait_ge(s["g_read"], i - 1)
                    if kind == "G":
                        v = y_at[c, r]
                        pe.wait_ge(s["y_lo"], TT * (v + 1))
                        for t in range(TT):
                            for a in range(2):
                                for h in range(2):
                                    mm = pe.matmul(pair[:, h, 0:HN], y[0:TS[t], v % 2, t, a, m * P:(m + 1) * P],
                                                   k.C[0:TS[t], r, t, h * HN:(h + 1) * HN],
                                                   start=(t == 0 and a == 0), stop=(t == TT - 1 and a == 1))
                    else:
                        pe.wait_ge(*st.split(4 * c + 3))
                        wh = st.views(4 * c + 3)
                        for j in range(kt):
                            mm = split_product_wide(pe, pair, [v[:, j, m * P:(m + 1) * P] for v in wh],
                                                    lambda b_, h: h_in(j)[:, b_, h * HN:(h + 1) * HN], j == 0, j == kt - 1)
                    mm.then_inc(s["g_mm"], 1)

        @block.scalar
        def _(act):
            for kind, c, r in jobs:
                w = cuts[c][1]
                if kind == "Y":
                    v = y_at[c, r]
                    if v >= 2:
                        pc, pr = divmod(v - 2, RELS)
                        act.wait_ge(s["g_mm"], g_at[pc, pr] + cuts[pc][1] // P)
                    for t in range(TT):
                        i = TT * v + t
                        act.wait_ge(s["y_mm"], i + 1)
                        act.activation(y[0:TS[t], v % 2, t, 0, 0:w], k.banks[i % 3][0:TS[t], 0:w], ACT.Copy).then_inc(s["y_hi"], 1)
                elif kind == "G" and r == 2:
                    for m in range(w // P):
                        i = 2 * c + m
                        act.wait_ge(s["h_f"], i + 1)
                        act.activation(h_out(i)[:, 0, :], acc[:, m, :], ACT.Copy).then_inc(s["h_hi"], 1)

        @block.vector
        def _(dve):
            link = Link(dve, s["chain"])
            dve.wait_ge(s["small"], 16)
            for kind, c, r in jobs:
                w = cuts[c][1]
                if kind == "Y":
                    v = y_at[c, r]
                    for t in range(TT):
                        i = TT * v + t
                        dve.wait_ge(s["y_hi"], i + 1)
                        dve.tensor_tensor(y[0:TS[t], v % 2, t, 1, 0:w], k.banks[i % 3][0:TS[t], 0:w],
                                          y[0:TS[t], v % 2, t, 0, 0:w].bitcast(F32), ALU.subtract).then_inc(s["y_lo"], 1)
                    continue
                for m in range(w // P):
                    i = g_at[c, r] + m
                    src = k.pair[2 + i % 2][:, :, 0:HN]
                    sum_ = acc[:, m, :]
                    dve.wait_ge(s["g_mm"], i + 1)
                    if kind == "G" and r == 0:
                        if c > 0:
                            dve.wait_ge(s["h_lo"], 2 * (c - 1) + m + 1)
                        dve.tensor_tensor(halves(sum_), src, halves(k.inv[:, r, :]), ALU.mult).then_inc(s["g_read"], 1)
                        dve.wait_ge(s["g_read"], i + 1)
                    elif kind == "G":
                        dve.tensor_tensor(halves(part), src, halves(k.inv[:, r, :]), ALU.mult).then_inc(s["g_read"], 1)
                        dve.wait_ge(s["g_read"], i + 1)
                        link(dve.tensor_tensor(sum_, sum_, part, ALU.add))
                    else:
                        dve.scalar_tensor_tensor(halves(sum_), src, b[:, 2 * c + m:2 * c + m + 1], halves(sum_),
                                                 ALU.add, ALU.add).then_inc(s["g_read"], 1)
                        dve.wait_ge(s["g_read"], i + 1)
                    if kind == "G" and r == 2:
                        dve.tensor_scalar(sum_, sum_, 0.0, None, ALU.max).then_inc(s["h_f"], 1)
                        if m == w // P - 1:
                            for m2 in range(w // P):
                                o = 2 * c + m2
                                dve.wait_ge(s["h_hi"], o + 1)
                                dve.tensor_tensor(h_out(o)[:, 1, :], acc[:, m2, :], h_out(o)[:, 0, :].bitcast(F32),
                                                  ALU.subtract).then_inc(s["h_lo"], 1)


def phase_add_turned(k, name, h):
    with ExitStack() as ctx:
        k.begin(ctx)
        whole = k.sb(f"{name}_whole", [P, 2, NT], F32)
        s = signals(k, name, ("whole", "turned", "added"))
        block = ctx.enter_context(k.nc.Block())

        @block.gpsimd
        def _(pool):
            k.clear_last(pool)

        @block.vector
        def _(dve):
            def add(j):
                dve.wait_ge(s["turned"], j + 1)
                for t in range(TT):
                    x = k.x[0:TS[t], t, j * P:(j + 1) * P]
                    src = k.banks[2 * (j % 2) + t // 4][0:TS[t], (t % 4) * P:(t % 4 + 1) * P]
                    ins = dve.tensor_tensor(x, src, x, ALU.add)
                ins.then_inc(s["added"], 1)

            for j in range(KD):
                if j >= 2:
                    dve.wait_ge(s["turned"], j - 1)
                dve.tensor_tensor(whole[:, j % 2, :], h(j)[:, 0, :].bitcast(F32), h(j)[:, 1, :].bitcast(F32),
                                  ALU.add).then_inc(s["whole"], 1)
                if j >= 1:
                    add(j - 1)
            add(KD - 1)

        @block.tensor
        def _(pe):
            for j in range(KD):
                pe.wait_ge(s["whole"], j + 1)
                if j >= 2:
                    pe.wait_ge(s["added"], j - 1)
                for t in range(TT):
                    mm = pe.transpose(k.banks[2 * (j % 2) + t // 4][0:TS[t], (t % 4) * P:(t % 4 + 1) * P],
                                      whole[:, j % 2, t * P:t * P + TS[t]], k.ident[:])
                mm.then_inc(s["turned"], 1)


def phase_save(k, name):
    with ExitStack() as ctx:
        k.begin(ctx)
        saved = k.sem(f"{name}_saved")
        k.x_dram = k.nc.dram_tensor("x_dram", (NODES, D), F32).ap()
        block = ctx.enter_context(k.nc.Block())

        @block.gpsimd
        def _(pool):
            k.clear_last(pool)

        @block.sync
        def _(sp):
            for t in range(TT):
                sp.dma_start(k.x_dram[t * P:t * P + TS[t], :], k.x[0:TS[t], t, :]).then_inc(saved, 16)
            sp.wait_ge(saved, 16 * TT)


def gnn_block(k, I):
    with ExitStack() as ctx:
        k.enter(ctx)
        k.et = k.sb("et_sb", [P, 1, 2, NT], F32R)
        k.C = k.sb("counts", [P, RELS, TT, NT], F32R)
        k.inv = k.a[:].rearrange("p t d -> p (t d)")[:, 0:RELS * NT].rearrange("p (r n) -> p r n", r=RELS)
        k.total_dram = k.nc.dram_tensor("count_total_dram", (P, TT * NT), F32).ap()
        phase_counts(k, I["src"], I["dst"], I["edge_type_3"], I["L0_gnn_node_emb"], I["node_type_3"])
        k.enter(ctx)
        hb = k.sb("h_b", [P, K1, 2, NT], F32R)
        first = lambda j: k.xt[:, j, :, :] if j < KD else k.et[:, 0, :, :]
        second = lambda j: hb[:, j, :, :]
        phase_rgcn(k, "g1", first, second, D1, D1, I["L0_gnn_b1"])
        phase_rgcn(k, "g2", second, first, D1, D, I["L0_gnn_b2"])
        phase_rgcn(k, "g3", first, second, D, D, I["L0_gnn_b3"])
        phase_add_turned(k, "g4", second)



EMBEDS = (384, 576, 768)
RATIOS = (2, 3, 4)
assert all(r * e >= H_FF for r in RATIOS for e in EMBEDS)
GELU_C = float(np.sqrt(2.0 / np.pi))


def phase_ffn(k, name, w_fc, b_fc, w_proj, b_proj, alpha_e, alpha_r):
    with ExitStack() as ctx:
        k.begin(ctx)
        al = k.sb(f"{name}_al", [P, 6], F32)
        sum_r = k.sb(f"{name}_sum_r", [P, 1], F32)
        coef = k.sb(f"{name}_coef", [P, 3], F32)
        fc = k.sb(f"{name}_fc", [HP, 2, D], F32)
        pr = k.sb(f"{name}_pr", [P, KD, H_FF], F32)
        w0f = k.sb(f"{name}_w0f", [P, KD, H_FF], F32)
        w0 = k.sb(f"{name}_w0", [P, 2, KD, H_FF], F32R)
        w1f = k.sb(f"{name}_w1f", [HP, 2, D], F32)
        w1 = k.sb(f"{name}_w1", [HP, 2, 2, D], F32R)
        bf = k.sb(f"{name}_bf", [HP, 2], F32)
        bp = k.sb(f"{name}_bp", [P, D], F32)
        hf = k.sb(f"{name}_hf", [HP, 2, NT], F32)
        g1 = k.sb(f"{name}_g1", [HP, 2, NT], F32)
        g2 = k.sb(f"{name}_g2", [HP, 2, NT], F32)
        h = k.sb(f"{name}_h", [HP, 2, 2, NT], F32R)
        s = signals(k, name, (
            "loaded", "chain", "scaled", "turned", "w_f", "w_hi", "w_lo", "h_mm", "g_in", "g_tanh", "h_f", "h_hi",
            "h_lo", "o_mm", "o_read"))
        block = ctx.enter_context(k.nc.Block())

        @block.gpsimd
        def _(pool):
            k.clear_last(pool)
        fc_t = k.psum[:, 0:3, :]
        pr_t = [k.psum[0:HP, 3 + 2 * g:5 + 2 * g, 0:384] for g in range(2)]

        @block.sync
        def _(sp):
            sp.dma_start(al[:, 0:3], alpha_e.partition_broadcast(P)).then_inc(s["loaded"], 16)
            sp.dma_start(al[:, 3:6], alpha_r.partition_broadcast(P)).then_inc(s["loaded"], 16)
            sp.dma_start(fc[:], w_fc.rearrange("(g p) d -> p g d", p=HP)).then_inc(s["loaded"], 16)
            sp.dma_start(pr[:], w_proj.rearrange("(k p) h -> p k h", p=P)).then_inc(s["loaded"], 16)
            sp.dma_start(bf[:], b_fc.rearrange("(g p) -> p g", p=HP), allow_slow_non_contiguous=True).then_inc(s["loaded"], 16)
            sp.dma_start(bp[:], b_proj.partition_broadcast(P)).then_inc(s["loaded"], 16)

        @block.vector
        def _(dve):
            link = Link(dve, s["chain"])
            spans = ((0, EMBEDS[0]), (EMBEDS[0], EMBEDS[1]), (EMBEDS[1], EMBEDS[2]))
            dve.wait_ge(s["loaded"], 16 * 6)
            link(dve.tensor_reduce(sum_r[:], al[:, 3:6], AX.X, ALU.add))
            link(dve.tensor_scalar(coef[:], al[:, 0:3], sum_r[:, 0:1], None, ALU.mult))
            link(dve.tensor_tensor(coef[:, 1:2], coef[:, 1:2], coef[:, 2:3], ALU.add))
            link(dve.tensor_tensor(coef[:, 0:1], coef[:, 0:1], coef[:, 1:2], ALU.add))
            for i, (c0, c1) in enumerate(spans):
                dve.tensor_scalar(bp[:, c0:c1], bp[:, c0:c1], coef[:, i:i + 1], None, ALU.mult)
                ins = dve.tensor_scalar(fc[:, :, c0:c1], fc[:, :, c0:c1], coef[0:HP, i:i + 1], None, ALU.mult)
            link(ins)
            link(dve.tensor_scalar(bf[:], bf[:], coef[0:HP, 0:1], None, ALU.mult))
            ins = dve.tensor_copy(g1[:, 0, 0:1], coef[0:HP, 0:1])
            ins.then_inc(s["scaled"], 1)
            for t in range(TT):
                ins = dve.tensor_tensor(k.x[0:TS[t], t, :], k.x[0:TS[t], t, :], bp[0:TS[t], :], ALU.add)
            link(ins)
            dve.wait_ge(s["turned"], 1)
            for j in range(3):
                dve.tensor_copy(w0f[:, 2 * j:2 * j + 2, :].rearrange("p k h -> p (k h)"), fc_t[:, j, 0:2 * H_FF])
            for g in range(2):
                w = w1f[:, g, :]
                link(dve.tensor_copy(w.rearrange("p (b n) -> p b n", b=2), pr_t[g]))
                for i, (c0, c1) in enumerate(spans):
                    ins = dve.tensor_scalar(w[:, c0:c1], w[:, c0:c1], coef[0:HP, i:i + 1], None, ALU.mult)
            ins.then_inc(s["w_f"], 1)
            dve.wait_ge(s["w_hi"], 2)
            dve.tensor_tensor(w0[:, 1, :, :], w0f[:], w0[:, 0, :, :].bitcast(F32), ALU.subtract).then_inc(s["w_lo"], 1)
            dve.tensor_tensor(w1[:, 1, :, :], w1f[:], w1[:, 0, :, :].bitcast(F32), ALU.subtract).then_inc(s["w_lo"], 1)
            for g in range(2):
                dve.wait_ge(s["h_mm"], g + 1)
                link(dve.tensor_scalar(halves(hf[:, g, :]), k.pair[g][0:HP, :, 0:HN], bf[:, g:g + 1], None, ALU.add))
                link(dve.tensor_tensor(g1[:, g, :], hf[:, g, :], hf[:, g, :], ALU.mult))
                link(dve.tensor_scalar(g1[:, g, :], g1[:, g, :], 0.044715, 1.0, ALU.mult, ALU.add))
                dve.tensor_tensor(g1[:, g, :], g1[:, g, :], hf[:, g, :], ALU.mult).then_inc(s["g_in"], 1)
            for g in range(2):
                dve.wait_ge(s["g_tanh"], g + 1)
                link(dve.tensor_scalar(g2[:, g, :], g2[:, g, :], 0.5, 0.5, ALU.mult, ALU.add))
                dve.tensor_tensor(hf[:, g, :], hf[:, g, :], g2[:, g, :], ALU.mult).then_inc(s["h_f"], 1)
            for g in range(2):
                dve.wait_ge(s["h_hi"], g + 1)
                dve.tensor_tensor(h[:, g, 1, :], hf[:, g, :], h[:, g, 0, :].bitcast(F32), ALU.subtract).then_inc(s["h_lo"], 1)
            for i in range(2 * TT):
                t, c = divmod(i, 2)
                x = k.x[0:TS[t], t, c * 384:(c + 1) * 384]
                dve.wait_ge(s["o_mm"], i + 1)
                dve.tensor_tensor(x, k.banks[4 + i % 2][0:TS[t], 0:384], x, ALU.add).then_inc(s["o_read"], 1)

        @block.scalar
        def _(act):
            act.wait_ge(s["w_f"], 1)
            act.activation(w0[:, 0, :, :], w0f[:], ACT.Copy).then_inc(s["w_hi"], 1)
            act.activation(w1[:, 0, :, :], w1f[:], ACT.Copy).then_inc(s["w_hi"], 1)
            for g in range(2):
                act.wait_ge(s["g_in"], g + 1)
                act.activation(g2[:, g, :], g1[:, g, :], ACT.Tanh, scale=GELU_C).then_inc(s["g_tanh"], 1)
            for g in range(2):
                act.wait_ge(s["h_f"], g + 1)
                act.activation(h[:, g, 0, :], hf[:, g, :], ACT.Copy).then_inc(s["h_hi"], 1)

        @block.tensor
        def _(pe):
            pe.wait_ge(s["scaled"], 1)
            for j in range(KD):
                for g in range(2):
                    c0 = (j % 2) * H_FF + g * HP
                    pe.transpose(fc_t[:, j // 2, c0:c0 + HP], fc[:, g, j * P:(j + 1) * P], k.ident[0:HP, 0:HP])
            for g in range(2):
                for j in range(KD):
                    mm = pe.transpose(pr_t[g][:, j // 3, (j % 3) * P:(j % 3 + 1) * P], pr[:, j, g * HP:(g + 1) * HP],
                                      k.ident[:])
            mm.then_inc(s["turned"], 1)
            pe.wait_ge(s["w_lo"], 2)
            for g in range(2):
                for j in range(KD):
                    mm = split_product_wide(pe, k.pair[g][0:HP], [w0[:, a, j, g * HP:(g + 1) * HP] for a in range(2)],
                                            lambda b, hh: k.xt[:, j, b, hh * HN:(hh + 1) * HN], j == 0, j == KD - 1)
                mm.then_inc(s["h_mm"], 1)
            pe.wait_ge(s["h_lo"], 2)
            for i in range(2 * TT):
                t, c = divmod(i, 2)
                if i >= 2:
                    pe.wait_ge(s["o_read"], i - 1)
                for g in range(2):
                    mm = split_product(pe, k.banks[4 + i % 2][0:TS[t], 0:384],
                                       [h[:, g, a, t * P:t * P + TS[t]] for a in range(2)],
                                       [w1[:, a, g, c * 384:(c + 1) * 384] for a in range(2)], g == 0, g == 1)
                mm.then_inc(s["o_mm"], 1)



def phase_gcn(k, name, bias):
    with ExitStack() as ctx:
        k.begin(ctx)
        st = k.streams[name]
        total = k.sb(f"{name}_total", [P, TT, NT], F32)
        adj = k.sb(f"{name}_adj", [P, TT, NT], F32R)
        ones = k.sb(f"{name}_ones", [P, 2], F32)
        y = k.sb(f"{name}_y", [P, TT, 2, D], F32R)
        yf = k.sb(f"{name}_yf", [P, 2, 256], F32)
        bp = k.sb(f"{name}_bp", [P, D], F32)
        s = signals(k, name, (
            "loaded", "chain", "ones_made", "deg_mm", "var_ready", "root_ready", "looped", "adj_made", "y_mm", "y_f",
            "y_hi", "y_lo", "o_mm", "o_read"))
        st.freed.update({c: (s["y_mm"], TT * (c + 1)) for c in range(3)})
        block = ctx.enter_context(k.nc.Block())

        @block.sync
        def _(sp):
            sp.dma_start(total[:].rearrange("p t n -> p (t n)"), k.total_dram).then_inc(s["loaded"], 16)
            sp.dma_start(bp[:], bias.partition_broadcast(P)).then_inc(s["loaded"], 16)
            stream_loads(sp, st)

        @block.gpsimd
        def _(pool):
            k.clear_last(pool)
            stream_splits(pool, st)

        @block.vector
        def _(dve):
            link = Link(dve, s["chain"])
            link(dve.memset(ones[:], 1.0))
            dve.wait_ge(s["loaded"], 32)
            for t in range(TT):
                ts = TS[t]
                ins = dve.tensor_tensor(total[0:ts, t, t * P:t * P + ts], total[0:ts, t, t * P:t * P + ts],
                                        k.ident[0:ts, 0:ts], ALU.add)
            ins.then_inc(s["looped"], 1)
            for t in range(TT):
                ins = dve.tensor_tensor(k.x[0:TS[t], t, :], k.x[0:TS[t], t, :], bp[0:TS[t], :], ALU.add)
            link(ins)
            dve.wait_ge(s["deg_mm"], 1)
            link(dve.memset(k.ve[:], 1.0))
            for t in range(TT):
                ins = dve.tensor_copy(k.ve[0:TS[t], t:t + 1], k.banks[7][0:TS[t], 2 * t:2 * t + 1])
            link(ins)
            rsqrt_of_ve(dve, link, k, s)

            def y_low(i):
                c, t = divmod(i, TT)
                dve.wait_ge(s["y_hi"], i + 1)
                dve.tensor_tensor(y[0:TS[t], t, 1, c * 256:(c + 1) * 256], yf[0:TS[t], i % 2, :],
                                  y[0:TS[t], t, 0, c * 256:(c + 1) * 256].bitcast(F32), ALU.subtract).then_inc(s["y_lo"], 1)

            for i in range(3 * TT):
                c, t = divmod(i, TT)
                dve.wait_ge(s["y_mm"], i + 1)
                if i >= 2:
                    dve.wait_ge(s["y_lo"], i - 1)
                dve.tensor_scalar(yf[0:TS[t], i % 2, :], k.banks[i % 2][0:TS[t], 0:256], k.rstd[0:TS[t], t:t + 1], None,
                                  ALU.mult).then_inc(s["y_f"], 1)
                if i >= 1:
                    y_low(i - 1)
            y_low(3 * TT - 1)
            for i in range(2 * TT):
                t, c = divmod(i, 2)
                x = k.x[0:TS[t], t, c * 384:(c + 1) * 384]
                dve.wait_ge(s["o_mm"], i + 1)
                dve.scalar_tensor_tensor(x, k.banks[2 + i % 2][0:TS[t], 0:384], k.rstd[0:TS[t], t:t + 1], x,
                                         ALU.mult, ALU.add).then_inc(s["o_read"], 1)

        @block.scalar
        def _(act):
            act.wait_ge(s["looped"], 1)
            act.activation(adj[:], total[:], ACT.Copy).then_inc(s["adj_made"], 1)
            act.wait_ge(s["var_ready"], 1)
            act.activation(k.root[:], k.ve[:], ACT.Sqrt).then_inc(s["root_ready"], 1)
            for i in range(3 * TT):
                c, t = divmod(i, TT)
                act.wait_ge(s["y_f"], i + 1)
                act.activation(y[0:TS[t], t, 0, c * 256:(c + 1) * 256], yf[0:TS[t], i % 2, :], ACT.Copy).then_inc(s["y_hi"], 1)

        @block.tensor
        def _(pe):
            pe.wait_ge(s["looped"], 1)
            for t in range(TT):
                for u in range(TT):
                    mm = pe.matmul(k.banks[7][0:TS[t], 2 * t:2 * t + 2], total[0:TS[u], u, t * P:t * P + TS[t]],
                                   ones[0:TS[u], :], start=(u == 0), stop=(u == TT - 1))
            mm.then_inc(s["deg_mm"], 1)
            for c in range(3):
                pe.wait_ge(*st.split(c))
                wh = st.views(c)
                for t in range(TT):
                    i = c * TT + t
                    if i >= 2:
                        pe.wait_ge(s["y_f"], i - 1)
                    for j in range(KD):
                        mm = split_product(pe, k.banks[i % 2][0:TS[t], 0:256],
                                           [k.xt[:, j, a, t * P:t * P + TS[t]] for a in range(2)],
                                           [v[:, j, :] for v in wh], j == 0, j == KD - 1)
                    mm.then_inc(s["y_mm"], 1)
            pe.wait_ge(s["adj_made"], 1)
            pe.wait_ge(s["y_lo"], 3 * TT)
            for i in range(2 * TT):
                t, c = divmod(i, 2)
                if i >= 2:
                    pe.wait_ge(s["o_read"], i - 1)
                for u in range(TT):
                    for a in range(2):
                        mm = pe.matmul(k.banks[2 + i % 2][0:TS[t], 0:384], adj[0:TS[u], u, t * P:t * P + TS[t]],
                                       y[0:TS[u], u, a, c * 384:(c + 1) * 384],
                                       start=(u == 0 and a == 0), stop=(u == TT - 1 and a == 1))
                mm.then_inc(s["o_mm"], 1)



CAP = 320
assert CAP % 2 == 0 and 2 * CAP >= NODES
OVER = 2 * NODES // (CAP + 1)
JOBS = EXPERTS + OVER
JC = JOBS + 1
MARK = 1024.0
assert MARK - CAP > NODES or MARK > NODES
ST = (P, P, CAP - 2 * P)


def phase_router(k, name, w_router, bias, shared_src):
    with ExitStack() as ctx:
        k.begin(ctx)
        wf = k.sb(f"{name}_wf", [P, KD, EXPERTS], F32)
        w = k.sb(f"{name}_w", [P, 2, KD, EXPERTS], F32R)
        b = k.sb(f"{name}_b", [P, EXPERTS], F32)
        logits = k.sb(f"{name}_logits", [P, TT, EXPERTS], F32)
        top = k.sb(f"{name}_top", [P, TT, 8], F32)
        at_i = k.sb(f"{name}_at_i", [P, TT, 8], U32)
        at_f = k.sb(f"{name}_at_f", [P, TT, 8], F32)
        iota_i = k.sb(f"{name}_iota_i", [P, CAP], I32)
        iota = k.sb(f"{name}_iota", [P, EXPERTS], F32)
        slot_i = k.sb(f"{name}_slot_i", [P, len(ST)], I32)
        hot = k.sb(f"{name}_hot", [P, TT, 4, EXPERTS], F32)
        gap = k.sb(f"{name}_gap", [P, TT], F32)
        ex = k.sb(f"{name}_ex", [P, TT], F32)
        den = k.sb(f"{name}_den", [P, TT], F32)
        wt = k.sb(f"{name}_wt", [P, 2, TT], F32)
        sel = k.sb(f"{name}_sel", [P, TT, EXPERTS], F32)
        selb = k.sb(f"{name}_selb", [P, TT, EXPERTS], BF16)
        ones = k.sb(f"{name}_ones", [P, P], BF16)
        weight = k.sb(f"{name}_weight", [P, TT, JC], F32)
        over = k.sb(f"{name}_over", [P, EXPERTS], F32)
        before = k.sb(f"{name}_before", [P, EXPERTS + 1], F32)
        which = k.sb(f"{name}_which", [P, OVER, EXPERTS], F32)
        prod = k.sb(f"{name}_prod", [P, 4, TT, EXPERTS], F32)
        seen = k.sb(f"{name}_seen", [P, TT], F32)
        expert_f = k.sb(f"{name}_expert_f", [P, JC], F32)
        count_f = k.sb(f"{name}_count_f", [P, 1], F32)
        s = signals(k, name, (
            "loaded", "chain", "iota_made", "later_made", "w_hi", "w_lo", "mm", "gap_made", "ex_made", "sel_made",
            "rank_mm", "weight_made", "weight_hi"))
        block = ctx.enter_context(k.nc.Block())

        @block.sync
        def _(sp):
            sp.dma_start(wf[:], weight_view(w_router)).then_inc(s["loaded"], 16)
            sp.dma_start(b[:], bias.partition_broadcast(P)).then_inc(s["loaded"], 16)
            for i in range(RAW):
                load_shared(sp, k, shared_src, i, i)

        @block.gpsimd
        def _(pool):
            k.clear_last(pool)
            pool.iota(iota_i[:], [[1, CAP]], base=0, channel_multiplier=0)
            pool.iota(slot_i[:], [[P, len(ST)]], base=int(MARK), channel_multiplier=1).then_inc(s["iota_made"], 1)
            pool.memset(k.later[:], 1.0).then_inc(s["later_made"], 1)
            pool.wait_ge(s["later_made"], 1)
            pool.affine_select(out=k.later[:], in_=k.later[:], compare_op=ALU.is_gt, fill=0.0, base=0,
                               pattern=[[-P, TT], [1, NT]], channel_multiplier=-1).then_inc(s["later_made"], 1)
            pool.wait_ge(s["later_made"], 2)
            pool.affine_select(out=k.later[:], in_=k.later[:], compare_op=ALU.not_equal, fill=MARK, base=0,
                               pattern=[[-P, TT], [1, NT]], channel_multiplier=-1).then_inc(s["later_made"], 1)

        @block.scalar
        def _(act):
            act.wait_ge(s["loaded"], 32)
            act.activation(w[:, 0, :, :], wf[:], ACT.Copy).then_inc(s["w_hi"], 1)
            act.wait_ge(s["gap_made"], 1)
            act.activation(ex[:], gap[:], ACT.Exp).then_inc(s["ex_made"], 1)
            act.wait_ge(s["weight_made"], 1)
            act.activation(k.job_w[:, :, :, 0], weight[:], ACT.Copy).then_inc(s["weight_hi"], 1)

        @block.tensor
        def _(pe):
            pe.wait_ge(s["w_lo"], 1)
            for t in range(TT):
                for j in range(KD):
                    mm = split_product(pe, k.banks[0][0:TS[t], t * EXPERTS:(t + 1) * EXPERTS],
                                       [k.xt[:, j, a, t * P:t * P + TS[t]] for a in range(2)],
                                       [w[:, a, j, :] for a in range(2)], j == 0, j == KD - 1)
            mm.then_inc(s["mm"], 1)
            pe.wait_ge(s["later_made"], 3)
            pe.wait_ge(s["sel_made"], 1)
            for t in range(TT):
                for u in range(t + 1):
                    pe.matmul(k.banks[1][0:TS[t], t * EXPERTS:(t + 1) * EXPERTS], k.later[0:TS[u], u, t * P:t * P + TS[t]],
                              selb[0:TS[u], u, :], start=(u == 0), stop=(u == t))
            for u in range(TT):
                mm = pe.matmul(k.banks[2][:, 0:EXPERTS], ones[0:TS[u], :], selb[0:TS[u], u, :],
                               start=(u == 0), stop=(u == TT - 1))
            mm.then_inc(s["rank_mm"], 1)

        @block.vector
        def _(dve):
            link = Link(dve, s["chain"])
            dve.memset(logits[:], 0.0)
            dve.memset(ones[:], 1.0)
            dve.memset(weight[:], 0.0)
            dve.memset(k.job_rank[:], 0.0)
            dve.memset(k.job_sel[:], 0.0)
            dve.memset(k.job_off[:], 0.0)
            dve.memset(before[:], 0.0)
            link(dve.memset(expert_f[:], 0.0))
            dve.wait_ge(s["iota_made"], 1)
            dve.tensor_copy(iota[:], iota_i[:, 0:EXPERTS])
            dve.tensor_scalar(k.iota_slot[:], iota_i[:], MARK, None, ALU.add)
            link(dve.tensor_copy(k.slot_id[:], slot_i[:]))
            dve.wait_ge(s["w_hi"], 1)
            dve.tensor_tensor(w[:, 1, :, :], wf[:], w[:, 0, :, :].bitcast(F32), ALU.subtract).then_inc(s["w_lo"], 1)
            dve.wait_ge(s["mm"], 1)
            for t in range(TT):
                ts = TS[t]
                ins = dve.tensor_tensor(logits[0:ts, t, :], k.banks[0][0:ts, t * EXPERTS:(t + 1) * EXPERTS], b[0:ts, :],
                                        ALU.add)
            link(ins)
            for t in range(TT):
                ins = dve.max(top[:, t, :], logits[:, t, :])
            link(ins)
            for t in range(TT):
                ins = dve.max_index(at_i[:, t, :], top[:, t, :], logits[:, t, :])
            link(ins)
            link(dve.tensor_copy(at_f[:], at_i[:]))
            dve.tensor_tensor(gap[:], top[:, :, 1], top[:, :, 0], ALU.subtract).then_inc(s["gap_made"], 1)
            for t in range(TT):
                for r in range(2):
                    ins = dve.tensor_scalar(hot[:, t, r, :], iota[:], at_f[:, t, r:r + 1], None, ALU.is_equal)
            link(ins)
            link(dve.tensor_tensor(sel[:], hot[:, :, 0, :], hot[:, :, 1, :], ALU.add))
            dve.tensor_copy(k.job_sel[:, :, 0:EXPERTS], sel[:])
            dve.tensor_copy(selb[:], sel[:]).then_inc(s["sel_made"], 1)
            dve.wait_ge(s["ex_made"], 1)
            link(dve.tensor_scalar(den[:], ex[:], 1.0, None, ALU.add))
            link(dve.reciprocal(wt[:, 0, :], den[:]))
            link(dve.tensor_tensor(wt[:, 1, :], ex[:], wt[:, 0, :], ALU.mult))
            for t in range(TT):
                for r in range(2):
                    ins = dve.tensor_scalar(hot[:, t, 2 + r, :], hot[:, t, r, :], wt[:, r, t:t + 1], None, ALU.mult)
            link(ins)
            link(dve.tensor_tensor(weight[:, :, 0:EXPERTS], hot[:, :, 2, :], hot[:, :, 3, :], ALU.add))
            dve.wait_ge(s["rank_mm"], 1)
            for t in range(TT):
                dve.tensor_copy(k.job_rank[0:TS[t], t, 0:EXPERTS], k.banks[1][0:TS[t], t * EXPERTS:(t + 1) * EXPERTS])
            dve.tensor_copy(expert_f[:, 0:EXPERTS], iota[:])
            link(dve.tensor_scalar(over[:], k.banks[2][:, 0:EXPERTS], float(CAP), None, ALU.is_gt))
            for e in range(EXPERTS):
                link(dve.tensor_tensor(before[:, e + 1:e + 2], before[:, e:e + 1], over[:, e:e + 1], ALU.add))
            for q in range(OVER):
                j = EXPERTS + q
                link(dve.tensor_scalar(which[:, q, :], before[:, 0:EXPERTS], float(q), None, ALU.is_equal))
                link(dve.tensor_tensor(which[:, q, :], which[:, q, :], over[:], ALU.mult))
                dve.tensor_tensor(prod[:, 0, 0, :], which[:, q, :], iota[:], ALU.mult)
                for i, src in enumerate((k.job_rank[:, :, 0:EXPERTS], weight[:, :, 0:EXPERTS], sel[:])):
                    ins = dve.tensor_tensor(prod[:, 1 + i, :, :], src,
                                            which[:, q:q + 1, :].broadcast_to([P, TT, EXPERTS]), ALU.mult)
                link(ins)
                dve.tensor_reduce(expert_f[:, j:j + 1], prod[:, 0, 0, :], AX.X, ALU.add)
                for i, dst in enumerate((k.job_rank[:, :, j], weight[:, :, j], seen[:])):
                    ins = dve.tensor_reduce(dst, prod[:, 1 + i, :, :], AX.X, ALU.add)
                link(ins)
                link(dve.tensor_copy(k.job_sel[:, :, j], seen[:]))
            dve.tensor_scalar(k.job_rank[:, :, EXPERTS:JOBS], k.job_rank[:, :, EXPERTS:JOBS], -float(CAP), None, ALU.add)
            dve.memset(k.job_off[:, EXPERTS:JOBS], -float(CAP))
            dve.tensor_copy(k.job_expert[:], expert_f[:])
            link(dve.tensor_scalar(count_f[:], before[:, EXPERTS:EXPERTS + 1], float(EXPERTS), None, ALU.add))
            dve.tensor_copy(k.job_count[:], count_f[:]).then_inc(s["weight_made"], 1)
            dve.wait_ge(s["weight_hi"], 1)
            dve.tensor_tensor(k.job_w[:, :, :, 1], weight[:], k.job_w[:, :, :, 0].bitcast(F32), ALU.subtract)



GC = 384
FT = D // P


RAW = 3


def shared_sources(wg, wu, wd, half):
    c = half * D
    g, u, d = (weight_view(v[0]) for v in (wg, wu, wd))
    dh = d[:, half * FT:(half + 1) * FT, :]
    return [g[:, :, c:c + GC], u[:, :, c:c + GC], g[:, :, c + GC:c + 2 * GC], u[:, :, c + GC:c + 2 * GC],
            dh[:, :, 0:GC], dh[:, :, GC:2 * GC]]


def load_shared(sp, k, src, i, slot):
    sp.dma_start(k.moe_raw[:, slot, :].rearrange("p (k c) -> p k c", c=GC), src[i]).then_inc(k.moe_loaded[slot], 16)


def phase_shared_expert(k, name, wg, wu, wd, routed):
    SPL = 4
    CH = 6
    with ExitStack() as ctx:
        k.begin(ctx)
        raw = k.moe_raw
        whi = k.sb(f"{name}_whi", [P, SPL, WE_MOE], F32R)
        wlo = k.sb(f"{name}_wlo", [P, SPL, WE_MOE], F32R)
        ht = k.sb(f"{name}_ht", [P, FT, 2, NT], F32R)
        act_g = k.sb(f"{name}_act_g", [P, 2, NT], F32)
        hf = k.sb(f"{name}_hf", [P, 2, NT], F32)
        s = signals(k, name, (
            "hi_done", "lo_done", "used", "gu_mm", "silu", "hf", "h_hi", "h_lo", "o_mm", "o_read"))
        loaded = k.moe_loaded
        block = ctx.enter_context(k.nc.Block())

        def run(eng, unit):
            for half in range(2):
                unit(half, half, half == 0)

        @block.sync
        def _(sp):
            def unit(half, n, first):
                src = shared_sources(wg, wu, wd, half)
                for i in range(RAW if first else 0, CH):
                    sp.wait_ge(s["lo_done"], n * CH + (i - RAW + 1))
                    load_shared(sp, k, src, i, i % RAW)

            run(sp, unit)
            e = routed_expert(sp, k, routed, 0)
            for i in range(LEAD):
                sp.wait_ge(s["lo_done"], 2 * CH + (i - RAW + 1))
                load_routed(sp, k, e, i)

        @block.gpsimd
        def _(pool):
            k.clear_last(pool)
            def unit(half, n, first):
                for i in range(CH):
                    slot, spl = i % RAW, (half * CH + i) % SPL
                    pool.wait_ge(loaded[slot], n * (16 * CH // RAW) + 16 * (i // RAW + 1))
                    if not (first and i < SPL):
                        pool.wait_ge(s["used"], n * CH + (i - SPL + 1))
                    pool.tensor_tensor(whi[:, spl, :], raw[:, slot, :], k.one[:].broadcast_to([P, WE_MOE]), ALU.mult)\
                        .then_inc(s["hi_done"], 1)
                    pool.wait_ge(s["hi_done"], n * CH + (i + 1))
                    pool.tensor_tensor(wlo[:, spl, :], raw[:, slot, :], whi[:, spl, :].bitcast(F32),
                                       ALU.subtract).then_inc(s["lo_done"], 1)

            run(pool, unit)

        def banks_of(half, f):
            q = (f + half) % 2
            return k.pair[2 * q], k.pair[2 * q + 1]

        def out_bank(half, i):
            return k.banks[4 * ((FT + half) % 2) + i % 4]

        @block.tensor
        def _(pe):
            def views(half, i):
                spl = (half * CH + i) % SPL
                return [w[:, spl, :].rearrange("p (k c) -> p k c", c=GC) for w in (whi, wlo)]

            def unit(half, n, first):
                for c in range(2):
                    for f in range(3 * c, 3 * c + 3):
                        m = f - 3 * c
                        pg, pu = banks_of(half, f)
                        if f >= 2:
                            pe.wait_ge(s["hf"], n * FT + (f - 1))
                        elif not first and f == 0:
                            pe.wait_ge(s["hf"], n * FT)
                        elif not first:
                            pe.wait_ge(s["o_read"], n * (2 * TT))
                        for g, pair in ((0, pg), (1, pu)):
                            if m == 0:
                                pe.wait_ge(s["lo_done"], n * CH + (2 * c + g + 1))
                            wh = views(half, 2 * c + g)
                            for j in range(KD):
                                mm = split_product_wide(pe, pair, [w[:, j, m * P:(m + 1) * P] for w in wh],
                                                        lambda b, h: k.xt[:, j, b, h * HN:(h + 1) * HN],
                                                        j == 0, j == KD - 1)
                            if m == 2:
                                mm.then_inc(s["used"], 1)
                            else:
                                mm.then_inc(s["gu_mm"], 1)
                for c in range(2):
                    pe.wait_ge(s["lo_done"], n * CH + (5 + c))
                    wh = views(half, 4 + c)
                    for t in range(TT):
                        i = c * TT + t
                        if i == 0:
                            pe.wait_ge(s["hf"], n * FT + (FT - 1))
                        if i >= 4:
                            pe.wait_ge(s["o_read"], n * (2 * TT) + (i - 3))
                        for f in range(FT):
                            if i == 0:
                                pe.wait_ge(s["h_lo"], n * FT + (f + 1))
                            mm = split_product(pe, out_bank(half, i)[0:TS[t], 0:GC],
                                               [ht[:, f, a, t * P:t * P + TS[t]] for a in range(2)],
                                               [w[:, f, :] for w in wh], f == 0, f == FT - 1)
                        if t == TT - 1:
                            mm.then_inc(s["used"], 1)
                        else:
                            mm.then_inc(s["o_mm"], 1)

            run(pe, unit)

        def gate_ready(eng, n, f):
            c, m = divmod(f, 3)
            if m == 2:
                eng.wait_ge(s["used"], n * CH + (2 * c + 1))
            else:
                eng.wait_ge(s["gu_mm"], n * 8 + (4 * c + 2 * m + 1))

        def up_ready(eng, n, f):
            c, m = divmod(f, 3)
            if m == 2:
                eng.wait_ge(s["used"], n * CH + (2 * c + 2))
            else:
                eng.wait_ge(s["gu_mm"], n * 8 + (4 * c + 2 * m + 2))

        def out_ready(eng, n, i):
            c, t = divmod(i, TT)
            if t == TT - 1:
                eng.wait_ge(s["used"], n * CH + (5 + c))
            else:
                eng.wait_ge(s["o_mm"], n * (2 * TT - 2) + (c * (TT - 1) + t + 1))

        @block.scalar
        def _(act):
            def unit(half, n, first):
                for f in range(FT):
                    gate_ready(act, n, f)
                    if not (first and f < 2):
                        act.wait_ge(s["hf"], n * FT + (f - 1))
                    act.activation(halves(act_g[:, f % 2, :]), banks_of(half, f)[0][:, :, 0:HN], ACT.Silu).then_inc(s["silu"], 1)
                    act.wait_ge(s["hf"], n * FT + (f + 1))
                    if f == 0 and not first:
                        out_ready(act, n - 1, 2 * TT - 1)
                    act.activation(ht[:, f, 0, :], hf[:, f % 2, :], ACT.Copy).then_inc(s["h_hi"], 1)

            run(act, unit)

        @block.vector
        def _(dve):
            def unit(half, n, first):
                def low(f):
                    dve.wait_ge(s["h_hi"], n * FT + (f + 1))
                    dve.tensor_tensor(ht[:, f, 1, :], hf[:, f % 2, :], ht[:, f, 0, :].bitcast(F32),
                                      ALU.subtract).then_inc(s["h_lo"], 1)

                for f in range(FT):
                    up_ready(dve, n, f)
                    dve.wait_ge(s["silu"], n * FT + (f + 1))
                    if not (first and f < 2):
                        dve.wait_ge(s["h_lo"], n * FT + (f - 1))
                    dve.tensor_tensor(halves(hf[:, f % 2, :]), banks_of(half, f)[1][:, :, 0:HN],
                                      halves(act_g[:, f % 2, :]), ALU.mult).then_inc(s["hf"], 1)
                    low(f)
                for i in range(2 * TT):
                    c, t = divmod(i, TT)
                    ts = TS[t]
                    x = k.x[0:ts, t, c * GC:(c + 1) * GC]
                    out_ready(dve, n, i)
                    if not first:
                        dve.wait_ge(s["o_read"], n * (2 * TT) + (i - 2 * TT + 1))
                    dve.tensor_tensor(x, out_bank(half, i)[0:ts, 0:GC], x, ALU.add).then_inc(s["o_read"], 1)

            run(dve, unit)



HF = F_MOE // 2 // P
RC = 256
OC = D // RC
HC = HF + OC
NC = 2 * HC
OUTS = 2 * OC * len(ST)
WE = KD * RC
RING = RAW
LEAD = RING - 1
SHARED_LOADS = 16 * 2 * 6 // RAW
assert NC % RING == 0 and HF == KD


def routed_expert(sp, k, routed, j):
    e = sp.value_load(k.job_expert[0:1, bass.ds(j, 1)], min_val=0, max_val=EXPERTS - 1)
    return [v[bass.ds(e, 1)].rearrange("a (q p) f -> p (a q) f", p=P) for v in routed]


def load_routed(sp, k, weights, i):
    g, u, d = weights
    half, r = divmod(i, HC)
    slot = i % RING
    if r < HF:
        c = (half * HF + r) * P
        dst = k.moe_raw[:, slot, 0:WE].rearrange("p (k c) -> p k c", c=2 * P)
        sp.dma_start(dst[:, :, 0:P], g[:, :, c:c + P]).then_inc(k.moe_loaded[slot], 16)
        sp.dma_start(dst[:, :, P:2 * P], u[:, :, c:c + P]).then_inc(k.moe_loaded[slot], 16)
    else:
        c = (r - HF) * RC
        dst = k.moe_raw[:, slot, 0:WE].rearrange("p (k c) -> p k c", c=RC)
        src = d[:, half * HF:(half + 1) * HF, c:c + RC]
        for a in range(2):
            sp.dma_start(dst[:, 3 * a:3 * a + 3, :], src[:, 3 * a:3 * a + 3, :]).then_inc(k.moe_loaded[slot], 16)


def phase_routed_experts(k, name, routed):
    with ExitStack() as ctx:
        k.begin(ctx)
        raw = k.moe_raw[:, :, 0:WE]
        whi = k.sb(f"{name}_whi", [P, RING, WE], F32R)
        wlo = k.sb(f"{name}_wlo", [P, RING, WE], F32R)
        xn = k.sb(f"{name}_xn", [P, TT, 2, D], F32R)
        ht = k.sb(f"{name}_ht", [P, HF, 2, CAP], F32R)
        act_g = k.sb(f"{name}_act_g", [P, 2, CAP], F32)
        hf = k.sb(f"{name}_hf", [P, 2, CAP], F32)
        y_hl = k.sb(f"{name}_y_hl", [P, OC, 2, len(ST), RC], F32R)
        sel_b = k.sb(f"{name}_sel_b", [P, TT, P], BF16)
        w_slot = k.sb(f"{name}_w_slot", [P, len(ST)], F32)
        flat = k.xt[:].rearrange("p j a n -> p (j a n)")
        at = [0, KD * 2 * CAP, KD * 2 * CAP + len(ST) * NT, KD * 2 * CAP + len(ST) * NT + TT * CAP]
        xg = flat[:, at[0]:at[1]].rearrange("p (j a n) -> p j a n", j=KD, a=2)
        to_node = flat[:, at[1]:at[2]].rearrange("p (i n) -> p i n", n=NT)
        to_slot = flat[:, at[2]:at[3]].rearrange("p (t n) -> p t n", n=CAP)
        y_all = k.a[:].rearrange("p t d -> p (t d)")
        y0 = y_all[:, 0:len(ST) * D].rearrange("p (c i n) -> p c i n", c=OC, i=len(ST))
        yf = k.sb(f"{name}_yf", [P, len(ST), RC], F32)
        s = signals(k, name, (
            "chain", "split_hi", "xn_ready", "hi_done", "lo_done", "g_mm", "u_mm", "y_mm", "silu", "hf", "h_hi", "h_lo",
            "y_read", "y_hi", "y_lo", "aux_mm", "aux_hi", "aux_read", "slot_made", "sel_made", "mapped"))
        loaded = k.moe_loaded
        block = ctx.enter_context(k.nc.Block())

        AUX = 1 + 3 * TT + KD
        AUX_AT = {"map": 0, "scatter0": 1, "scatter1": 1 + TT, "gather": 1 + 2 * TT, "scatter2": 1 + 2 * TT + KD}

        def aux_bank(i):
            return k.banks[6 + (i + 1) % 2]

        def run(eng, body):
            count = eng.value_load(k.job_count[0:1, 0:1], min_val=EXPERTS, max_val=JOBS)
            body(0, True)
            with eng.Fori(1, count) as j:
                body(j, False)

        def is_hidden(i):
            return i % HC < HF

        def wait_chunk_read(eng, j, i):
            half, r = divmod(i, HC)
            if is_hidden(i):
                eng.wait_ge(s["u_mm"], j * (2 * HF) + (half * HF + r + 1))
            else:
                eng.wait_ge(s["y_mm"], j * OUTS + (half * OC + r - HF + 1) * len(ST))

        @block.sync
        def _(sp):
            def body(j, first):
                w = routed_expert(sp, k, routed, j)
                for i in range(LEAD if first else 0, NC):
                    if not (first and i < RING):
                        sp.wait_ge(s["lo_done"], j * NC + (i - RING + 1))
                    load_routed(sp, k, w, i)

            count = sp.value_load(k.job_count[0:1, 0:1], min_val=EXPERTS, max_val=JOBS)
            body(0, True)
            with sp.Fori(1, count) as j:
                body(j, False)
            sp.wait_ge(s["lo_done"], count * NC)
            for i in range(LEAD):
                load_routed(sp, k, [weight_view(v[0]) for v in routed], i)

        @block.gpsimd
        def _(pool):
            k.clear_last(pool)

            def weights_low(j, i):
                pool.wait_ge(s["hi_done"], j * NC + (i + 1))
                pool.tensor_tensor(wlo[:, i % RING, :], raw[:, i % RING, :], whi[:, i % RING, :].bitcast(F32),
                                   ALU.subtract).then_inc(s["lo_done"], 1)

            def body(j, first):
                for i in range(LEAD, NC + LEAD):
                    weights_low(j, i)

            for i in range(LEAD):
                weights_low(0, i)
            run(pool, body)

        @block.scalar
        def _(act):
            def weights_high(j, i, first):
                slot = i % RING
                act.wait_ge(loaded[slot], j * (32 * NC // RING) + (SHARED_LOADS + 32 * (i // RING + 1)))
                if not (first and i < RING):
                    wait_chunk_read(act, j, i - RING)
                act.activation(whi[:, slot, :], raw[:, slot, :], ACT.Copy).then_inc(s["hi_done"], 1)

            def gather_high(n):
                for q in range(KD):
                    act.wait_ge(s["aux_mm"], n + (q + 1))
                    act.activation(xg[:, q, 0, :], aux_bank(AUX_AT["gather"] + q)[:, 0:CAP], ACT.Copy)\
                        .then_inc(s["aux_hi"], 1)

            def body(j, first):
                for i in range(NC):
                    half, r = divmod(i, HC)
                    weights_high(j, i + LEAD, first)
                    if is_hidden(i):
                        f = half * HF + r
                        act.wait_ge(s["g_mm"], j * (2 * HF) + (f + 1))
                        if not (first and f < 2):
                            act.wait_ge(s["hf"], j * (2 * HF) + (f - 1))
                        act.activation(act_g[:, f % 2, :], k.banks[2 * (f % 2)][:, 0:CAP], ACT.Silu)\
                            .then_inc(s["silu"], 1)
                        act.wait_ge(s["hf"], j * (2 * HF) + (f + 1))
                        if r == 0 and not (first and half == 0):
                            act.wait_ge(s["y_mm"], j * OUTS + half * OC * len(ST))
                        act.activation(ht[:, r, 0, :], hf[:, f % 2, :], ACT.Copy).then_inc(s["h_hi"], 1)
                    elif half == 1:
                        c = r - HF
                        if c == 0 and not first:
                            act.wait_ge(s["aux_mm"], j * AUX + KD)
                        act.wait_ge(s["y_read"], j * OUTS + (OC + c + 1) * len(ST))
                        act.activation(y_hl[:, c, 0, :, :], yf[:], ACT.Copy).then_inc(s["y_hi"], 1)
                gather_high(j * AUX + (KD + AUX_AT["gather"]))

            for t in range(TT):
                act.activation(xn[0:TS[t], t, 0, :], k.a[0:TS[t], t, :], ACT.Copy).then_inc(s["split_hi"], 1)
            count = act.value_load(k.job_count[0:1, 0:1], min_val=EXPERTS, max_val=JOBS)
            for i in range(LEAD):
                weights_high(0, i, True)
            gather_high(0)
            body(0, True)
            with act.Fori(1, count) as j:
                body(j, False)

        @block.vector
        def _(dve):
            link = Link(dve, s["chain"])

            def make_slots(j):
                for t in range(TT):
                    ins = dve.tensor_scalar(to_slot[0:TS[t], t, :], k.iota_slot[0:TS[t], :],
                                            k.job_rank[0:TS[t], t, bass.ds(j, 1)], None, ALU.is_equal)
                ins.then_inc(s["slot_made"], 1)

            def make_sel(j):
                dve.tensor_copy(sel_b[:], k.job_sel[:, :, bass.ds(j, 1)].broadcast_to([P, TT, P])).then_inc(s["sel_made"], 1)

            def gather_low(n):
                for q in range(KD):
                    dve.wait_ge(s["aux_hi"], (n[0] * KD) + (n[1] + q + 1))
                    dve.tensor_tensor(xg[:, q, 1, :], aux_bank(AUX_AT["gather"] + q)[:, 0:CAP],
                                      xg[:, q, 0, :].bitcast(F32), ALU.subtract).then_inc(s["aux_read"], 1)

            def scatter_add(j, c):
                base = AUX_AT[f"scatter{c}"]
                for t in range(TT):
                    x = k.x[0:TS[t], t, c * RC:(c + 1) * RC]
                    dve.wait_ge(s["aux_mm"], j * AUX + (KD + base + t + 1))
                    dve.tensor_tensor(x, aux_bank(base + t)[0:TS[t], 0:RC], x, ALU.add).then_inc(s["aux_read"], 1)

            def body(j, first):
                for i in range(NC):
                    half, r = divmod(i, HC)
                    if is_hidden(i):
                        f = half * HF + r
                        dve.wait_ge(s["u_mm"], j * (2 * HF) + (f + 1))
                        dve.wait_ge(s["silu"], j * (2 * HF) + (f + 1))
                        if not (first and f < 2):
                            dve.wait_ge(s["h_lo"], j * (2 * HF) + (f - 1))
                        dve.tensor_tensor(hf[:, f % 2, :], k.banks[2 * (f % 2) + 1][:, 0:CAP], act_g[:, f % 2, :],
                                          ALU.mult).then_inc(s["hf"], 1)
                        dve.wait_ge(s["h_hi"], j * (2 * HF) + (f + 1))
                        dve.tensor_tensor(ht[:, r, 1, :], hf[:, f % 2, :], ht[:, r, 0, :].bitcast(F32),
                                          ALU.subtract).then_inc(s["h_lo"], 1)
                        if f == 4:
                            dve.wait_ge(s["aux_mm"], j * AUX + (KD + 1))
                            for m in range(len(ST)):
                                dve.tensor_scalar(halves(to_node[0:ST[m], m, :]), k.pair[3][0:ST[m], :, 0:HN],
                                                  k.job_off[0:ST[m], bass.ds(j, 1)], k.slot_id[0:ST[m], m:m + 1],
                                                  ALU.add, ALU.is_equal).then_inc(s["mapped"], 1)
                            for m in range(len(ST)):
                                o = k.banks[6][0:ST[m], 400 + 2 * m:402 + 2 * m]
                                dve.wait_ge(s["mapped"], j * (2 * len(ST)) + (len(ST) + m))
                                ins = dve.tensor_copy(w_slot[0:ST[m], m:m + 1], o[:, 0:1])
                                ins.then_inc(s["mapped"], 1)
                            dve.wait_ge(s["mapped"], j * (2 * len(ST)) + 2 * len(ST))
                            for m in range(len(ST)):
                                o = k.banks[6][0:ST[m], 400 + 2 * m:402 + 2 * m]
                                ins = dve.tensor_tensor(w_slot[0:ST[m], m:m + 1], o[:, 1:2], w_slot[0:ST[m], m:m + 1],
                                                        ALU.add)
                            ins.then_inc(s["aux_read"], 1)
                        if f == 7:
                            make_slots(j + 1)
                            make_sel(j + 1)
                        continue
                    c = r - HF
                    for m in range(len(ST)):
                        n = (half * OC + c) * len(ST) + m
                        o = k.banks[4 + n % 2][0:ST[m], 0:RC]
                        dve.wait_ge(s["y_mm"], j * OUTS + (n + 1))
                        if half == 0:
                            if m == 0 and c == 0:
                                dve.wait_ge(s["aux_read"], j * AUX + (KD + 1))
                            dve.tensor_scalar(y0[0:ST[m], c, m, :], o, w_slot[0:ST[m], m:m + 1], None,
                                              ALU.mult).then_inc(s["y_read"], 1)
                        else:
                            if m == 0 and not (first and c == 0):
                                dve.wait_ge(s["y_lo"], j * OC + c)
                            if m == 0 and c == 0:
                                dve.wait_ge(s["y_read"], j * OUTS + OC * len(ST))
                            dve.scalar_tensor_tensor(yf[0:ST[m], m, :], o, w_slot[0:ST[m], m:m + 1],
                                                     y0[0:ST[m], c, m, :], ALU.mult, ALU.add).then_inc(s["y_read"], 1)
                    if half == 1:
                        dve.wait_ge(s["y_read"], j * OUTS + (OC + c + 1) * len(ST))
                        dve.wait_ge(s["y_hi"], j * OC + (c + 1))
                        dve.tensor_tensor(y_hl[:, c, 1, :, :], yf[:], y_hl[:, c, 0, :, :].bitcast(F32),
                                          ALU.subtract).then_inc(s["y_lo"], 1)
                        if c > 0:
                            scatter_add(j, c - 1)
                gather_low((j, KD))
                scatter_add(j, OC - 1)

            for t in range(TT):
                dve.wait_ge(s["split_hi"], t + 1)
                ins = dve.tensor_tensor(xn[0:TS[t], t, 1, :], k.a[0:TS[t], t, :], xn[0:TS[t], t, 0, :].bitcast(F32),
                                        ALU.subtract)
            ins.then_inc(s["xn_ready"], 1)
            link(dve.memset(yf[:], 0.0))
            make_slots(0)
            make_sel(0)
            gather_low((0, 0))
            run(dve, body)

        @block.tensor
        def _(pe):
            def gather(j, n):
                pe.wait_ge(s["slot_made"], j + 1)
                for q in range(KD):
                    if q >= 2 or n is not None:
                        pe.wait_ge(s["aux_read"], (0 if n is None else n) + (q - 1))
                    for t in range(TT):
                        for a in range(2):
                            mm = pe.matmul(aux_bank(AUX_AT["gather"] + q)[:, 0:CAP], xn[0:TS[t], t, a, q * P:(q + 1) * P],
                                           to_slot[0:TS[t], t, :], start=(t == 0 and a == 0), stop=(t == TT - 1 and a == 1))
                    mm.then_inc(s["aux_mm"], 1)

            def map_nodes(j):
                pe.wait_ge(s["aux_read"], j * AUX + KD)
                pe.wait_ge(s["sel_made"], j + 1)
                for t in range(TT):
                    for h in range(2):
                        pe.matmul(k.pair[3][:, h, 0:HN], sel_b[0:TS[t], t, :], k.later[0:TS[t], t, h * HN:(h + 1) * HN],
                                  start=(t == 0), stop=(t == TT - 1))
                for m in range(len(ST)):
                    for t in range(TT):
                        mm = pe.matmul(k.banks[6][0:ST[m], 400 + 2 * m:402 + 2 * m],
                                       to_slot[0:TS[t], t, m * P:m * P + ST[m]],
                                       k.job_w[0:TS[t], t, bass.ds(j, 1), :].rearrange("p a w -> p (a w)"),
                                       start=(t == 0), stop=(t == TT - 1))
                mm.then_inc(s["aux_mm"], 1)

            def scatter(j, c):
                base = AUX_AT[f"scatter{c}"]
                pe.wait_ge(s["y_lo"], j * OC + (c + 1))
                for t in range(TT):
                    pe.wait_ge(s["aux_read"], j * AUX + (KD + base + t - (0 if base + t == 1 else 1)))
                    for m in range(len(ST)):
                        for a in range(2):
                            mm = pe.matmul(aux_bank(base + t)[0:TS[t], 0:RC], to_node[0:ST[m], m, t * P:t * P + TS[t]],
                                           y_hl[0:ST[m], c, a, m, :], start=(m == 0 and a == 0),
                                           stop=(m == len(ST) - 1 and a == 1))
                    mm.then_inc(s["aux_mm"], 1)

            def body(j, first):
                for i in range(NC):
                    half, r = divmod(i, HC)
                    wh = [w[:, i % RING, :] for w in (whi, wlo)]
                    pe.wait_ge(s["lo_done"], j * NC + (i + 1))
                    if is_hidden(i):
                        f = half * HF + r
                        if not (first and f < 2):
                            pe.wait_ge(s["hf"], j * (2 * HF) + (f - 1))
                        if f == 0:
                            pe.wait_ge(s["aux_read"], j * AUX + KD)
                        for g in range(2):
                            out = k.banks[2 * (f % 2) + g][:, 0:CAP]
                            for q in range(KD):
                                mm = split_product(pe, out,
                                                   [w[:, (2 * q + g) * P:(2 * q + g + 1) * P] for w in wh],
                                                   [xg[:, q, a, :] for a in range(2)], q == 0, q == KD - 1)
                            mm.then_inc(s["u_mm"] if g else s["g_mm"], 1)
                        if f == 3:
                            map_nodes(j)
                        continue
                    c = r - HF
                    for m in range(len(ST)):
                        n = (half * OC + c) * len(ST) + m
                        o = k.banks[4 + n % 2][0:ST[m], 0:RC]
                        if not (first and n < 2):
                            pe.wait_ge(s["y_read"], j * OUTS + (n - 1))
                        for f in range(HF):
                            if c == 0 and m == 0:
                                pe.wait_ge(s["h_lo"], j * (2 * HF) + (half * HF + f + 1))
                            mm = split_product(pe, o, [ht[:, f, a, m * P:m * P + ST[m]] for a in range(2)],
                                               [w[:, f * RC:(f + 1) * RC] for w in wh], f == 0, f == HF - 1)
                        mm.then_inc(s["y_mm"], 1)
                    if half == 1 and c > 0:
                        scatter(j, c - 1)
                gather(j + 1, j * AUX + (KD + AUX_AT["gather"]))
                scatter(j, OC - 1)

            pe.wait_ge(s["xn_ready"], 1)
            gather(0, None)
            run(pe, body)


def experts_block(k, I):
    with ExitStack() as ctx:
        k.enter(ctx)
        phase_norm(k, "n3", keep=True)
        k.enter(ctx)
        k.job_rank = k.sb("job_rank", [P, TT, JC], F32)
        k.job_w = k.sb("job_w", [P, TT, JC, 2], F32R)
        k.job_sel = k.sb("job_sel", [P, TT, JC], BF16)
        k.job_off = k.sb("job_off", [P, JC], F32)
        k.job_expert = k.sb("job_expert", [P, JC], I32)
        k.job_count = k.sb("job_count", [P, 1], I32)
        k.slot_id = k.sb("slot_id", [P, len(ST)], F32)
        k.iota_slot = k.sb("iota_slot", [P, CAP], F32)
        k.later = k.sb("later", [P, TT, NT], BF16)
        k.moe_raw = k.sb("moe_raw", [P, RAW, WE_MOE], F32)
        k.moe_loaded = [k.lasting_sem(f"moe_loaded{i}") for i in range(RAW)]
        routed = (I["L1_ffn_Wg_r"], I["L1_ffn_Wu_r"], I["L1_ffn_Wd_r"])
        phase_router(k, "ro", I["L1_ffn_W_router"], I["L1_ffn_expert_bias"],
                     shared_sources(I["L1_ffn_Wg_s"], I["L1_ffn_Wu_s"], I["L1_ffn_Wd_s"], 0))
        phase_shared_expert(k, "se", I["L1_ffn_Wg_s"], I["L1_ffn_Wu_s"], I["L1_ffn_Wd_s"], routed)
        phase_routed_experts(k, "re", routed)



SEM_SETS = (range(100, 160), range(160, 220))

LASTING_SEMS = range(220, 232)


class Kit:

    def __init__(self, nc, ctx):
        self.nc, self.outer, self.inner = nc, ctx, ctx
        self.phase, self.taken, self.lasting = 0, 0, 0

    def enter(self, ctx):
        self.inner = ctx

    def begin(self, ctx):
        self.inner = ctx
        self.phase += 1
        self.taken = 0

    def sb(self, name, shape, dt):
        return self.inner.enter_context(self.nc.sbuf_tensor(name, shape, dt))

    def sem(self, name):
        num = SEM_SETS[self.phase % 2][self.taken]
        self.taken += 1
        return self.inner.enter_context(self.nc.semaphore(name, num=num))

    def lasting_sem(self, name):
        self.lasting += 1
        return self.inner.enter_context(self.nc.semaphore(name, num=LASTING_SEMS[self.lasting - 1]))

    def clear_last(self, pool):
        if self.phase > 1:
            pool.sem_clear(SEM_SETS[(self.phase + 1) % 2])


def build(nc, I, out):
    with ExitStack() as ctx:
        k = Kit(nc, ctx)
        k.x_in = I["x"]
        psum = ctx.enter_context(nc.psum_tensor("psum", [P, 8, 512], F32))
        k.psum = psum
        k.banks = [psum[:, b, :] for b in range(8)]
        k.pair = [psum[:, 2 * b:2 * b + 2, :] for b in range(4)]
        k.x = k.sb("x_sb", [P, TT, D], F32)
        k.a = k.sb("a_sb", [P, TT, D], F32)
        k.xt = k.sb("xt_sb", [P, KD, 2, NT], F32R)
        k.ident = k.sb("ident", [P, P], F32)
        k.one = k.sb("one", [P, 1], F32)
        k.bn = k.sb("bn", [P, TT, 2, 6], F32)
        k.mv = k.sb("mv", [P, TT, 2], F32)
        k.ve = k.sb("ve", [P, TT], F32)
        k.root = k.sb("root", [P, TT], F32)
        k.rstd = k.sb("rstd", [P, TT], F32)
        k.tmp5 = k.sb("tmp5", [P, TT], F32)

        first_ctx = ctx.enter_context(ExitStack())
        k.enter(first_ctx)
        ring = Ring(k)
        k.streams = {
            "m0": Stream(ring, attend_chunks(I["L0_mix_W_qkv"])),
            "p0": Stream(ring, square_chunks(I["L0_mix_W_proj"])),
            "g1": Stream(ring, rgcn_chunks(I["L0_gnn_w_rel1"], I["L0_gnn_w_root1"])),
            "g2": Stream(ring, rgcn_chunks(I["L0_gnn_w_rel2"], I["L0_gnn_w_root2"])),
            "g3": Stream(ring, rgcn_chunks(I["L0_gnn_w_rel3"], I["L0_gnn_w_root3"])),
            "m1": Stream(ring, attend_chunks(I["L1_mix_W_qkv"])),
            "p1": Stream(ring, square_chunks(I["L1_mix_W_proj"])),
            "gc": Stream(ring, square_chunks(I["L1_gnn_W"])),
        }
        in_order = list(k.streams.values())
        for st, after in zip(in_order, in_order[1:]):
            st.next = after

        phase_norm(k, "n0", load_x=True)
        phase_attend(k, "m0", False, I["L0_mix_b_qkv"], I["L0_mix_random_features"])
        phase_project(k, "p0", False, I["L0_mix_b_proj"], I["x"])
        gnn_block(k, I)
        phase_norm(k, "n1")
        phase_ffn(k, "f0", I["L0_ffn_w_fc"], I["L0_ffn_b_fc"], I["L0_ffn_w_proj"], I["L0_ffn_b_proj"],
                  I["L0_ffn_alpha_e"], I["L0_ffn_alpha_r"])
        phase_norm(k, "n2")
        phase_save(k, "save")
        phase_attend(k, "m1", True, None, I["L1_mix_random_features"])
        phase_project(k, "p1", True, I["L1_mix_b_proj"], k.x_dram, I["L1_mix_gamma"], I["L1_mix_beta"])
        phase_gcn(k, "gc", I["L1_gnn_b"])
        first_ctx.close()
        k.enter(ctx)
        experts_block(k, I)
        k.begin(ctx)
        stored = k.sem("stored")
        block = ctx.enter_context(nc.Block())

        @block.sync
        def _(sp):
            for t in range(TT):
                sp.dma_start(out[t * P:t * P + TS[t], :], k.x[0:TS[t], t, :]).then_inc(stored, 16)
            sp.wait_ge(stored, 16 * TT)


def kernel(**inputs):
    import numpy as _np
    import concourse.bacc as _bacc
    from concourse import mybir as _mybir
    from concourse.bass_utils import run_bass_kernel_spmd as _run

    nc = _bacc.Bacc("TRN2", target_bir_lowering=False, num_devices=1)
    arrays, args = {}, {}
    for name, value in inputs.items():
        a = _np.ascontiguousarray(value)
        arrays[f"in_{name}"] = a
        args[name] = nc.dram_tensor(f"in_{name}", a.shape, _mybir.dt.from_np(a.dtype), kind="ExternalInput").ap()
    out = nc.dram_tensor("out_0", (NODES, D), F32, kind="ExternalOutput").ap()
    build(nc, args, out)
    r = _run(nc, [arrays], core_ids=[0])
    return r.results[0]["out_0"]
```
